# Optimizing a Trainium2 kernel written in Bass

```python
import numpy as np
import jax
import jax.numpy as jnp

def _softmax(x, axis=-1):
    return jax.nn.softmax(x, axis=axis)

def _gelu(x):
    return jax.nn.gelu(x, approximate=True)

def _silu(x):
    return jax.nn.silu(x)

def _sigmoid(x):
    return jax.nn.sigmoid(x)

def _layernorm(x, axis=-1, eps=1e-05):
    m = jnp.mean(x, axis=axis, keepdims=True)
    v = jnp.var(x, axis=axis, keepdims=True)
    return (x - m) / jnp.sqrt(v + eps)

def _scatter_add(tgt, idx, src, axis=0):
    return tgt.at[idx].add(src)

def _segment_sum(src, seg, n):
    return jax.ops.segment_sum(src, seg, n)
kernel_name = 'mk_gnn_resnorm_d4_gnn_r8_b8fc40'

def setup_inputs(seed: int=0):
    np.random.seed(seed)
    _w = jnp.asarray

    def _rec_inputs():
        import jax
        import jax.numpy as jnp
        _gk = jax.random.key(seed)
        x = 0.0002642 + 1 * jax.random.normal(jax.random.fold_in(_gk, 1), (12500, 64), jnp.float32)
        src = jax.random.randint(jax.random.fold_in(_gk, 2), (200000,), 0, 12500, jnp.int32)
        dst = jnp.minimum((12500 * jax.random.uniform(jax.random.fold_in(_gk, 3), (200000,)) ** 2.0).astype(jnp.int32), 99999)
        _o = jnp.argsort(dst, stable=True)
        src = src[_o]
        dst = dst[_o]
        edge_attr_32 = -5.3897e-05 + 0.999841 * jax.random.normal(jax.random.fold_in(_gk, 12), (200000, 32), jnp.float32)
        edge_attr_64 = -8.16379e-05 + 0.999858 * jax.random.normal(jax.random.fold_in(_gk, 13), (200000, 64), jnp.float32)
        edge_attr_64_n2 = -8.16379e-05 + 0.999858 * jax.random.normal(jax.random.fold_in(_gk, 14), (200000, 64), jnp.float32)
        edge_attr_64_n3 = -8.16379e-05 + 0.999858 * jax.random.normal(jax.random.fold_in(_gk, 15), (200000, 64), jnp.float32)
        return (x, src, dst, edge_attr_32, edge_attr_64, edge_attr_64_n2, edge_attr_64_n3)
    x, src, dst, edge_attr_32, edge_attr_64, edge_attr_64_n2, edge_attr_64_n3 = _rec_inputs()

    def _L0_gnn_setup():
        import jax, jax.numpy as jnp
        import numpy as np
        N = 12500
        E = 200000
        IN = 64
        H = 4
        D = 16
        HD = H * D
        LN_EPS = 1e-05

        def _forward(feat, edge_src, edge_dst, Wq, bq, Wk, bk, Wv, bv, Ws, bs, Wg, bg, ln_g, ln_b, prelu_a):
            q = (feat @ Wq + bq).reshape(N, H, D)
            k = (feat @ Wk + bk).reshape(N, H, D)
            v = (feat @ Wv + bv).reshape(N, H, D)
            scores = jnp.einsum('ehd,ehd->eh', q[edge_src], k[edge_dst]) / np.sqrt(D).astype(np.float32)
            smax = jax.ops.segment_max(scores, edge_dst, num_segments=N)
            smax = jnp.where(jnp.isfinite(smax), smax, 0.0)
            ex = jnp.exp(scores - smax[edge_dst])
            denom = jax.ops.segment_sum(ex, edge_dst, num_segments=N)
            sa = ex / denom[edge_dst]
            agg = jax.ops.segment_sum(sa[:, :, None] * v[edge_src], edge_dst, num_segments=N)
            rst = agg.reshape(N, HD)
            skip = feat @ Ws + bs
            gate = jax.nn.sigmoid(jnp.concatenate([skip, rst, skip - rst], axis=-1) @ Wg + bg)
            rst = gate * skip + (1.0 - gate) * rst
            mu = jnp.mean(rst, axis=-1, keepdims=True)
            var = jnp.mean(jnp.square(rst - mu), axis=-1, keepdims=True)
            rst = (rst - mu) * jax.lax.rsqrt(var + LN_EPS) * ln_g + ln_b
            return jnp.where(rst >= 0, rst, prelu_a * rst)
        key = jax.random.key(seed)
        ks = jax.random.split(key, 16)

        def lin(k, fi, fo):
            bound = 1.0 / np.sqrt(fi)
            kw, kb = jax.random.split(k)
            W = jax.random.uniform(kw, (fi, fo), jnp.float32, -bound, bound)
            b = jax.random.uniform(kb, (fo,), jnp.float32, -bound, bound)
            return (W, b)
        Wq, bq = lin(ks[0], IN, HD)
        Wk, bk = lin(ks[1], IN, HD)
        Wv, bv = lin(ks[2], IN, HD)
        Ws, bs = lin(ks[3], IN, HD)
        Wg, bg = lin(ks[4], 3 * HD, 1)
        return {'feat': jax.random.normal(ks[5], (N, IN), jnp.float32), 'edge_src': jax.random.randint(ks[6], (E,), 0, N, jnp.int64 if jax.config.jax_enable_x64 else jnp.int32), 'edge_dst': jnp.sort(jax.random.randint(ks[7], (E,), 0, N, jnp.int64 if jax.config.jax_enable_x64 else jnp.int32)), 'Wq': Wq, 'bq': bq, 'Wk': Wk, 'bk': bk, 'Wv': Wv, 'bv': bv, 'Ws': Ws, 'bs': bs, 'Wg': Wg, 'bg': bg, 'ln_g': jnp.ones((HD,), jnp.float32), 'ln_b': jnp.zeros((HD,), jnp.float32), 'prelu_a': jnp.float32(0.25)}
    _L0_gnn_all = _L0_gnn_setup()
    _L0_gnn_in = {k: v for k, v in _L0_gnn_all.items() if k in ('Wq', 'bq', 'Wk', 'bk', 'Wv', 'bv', 'Ws', 'bs', 'Wg', 'bg', 'ln_g', 'ln_b', 'prelu_a')}
    del _L0_gnn_all

    def _L1_gnn_setup():
        import jax, jax.numpy as jnp
        import numpy as np
        N_NODES = 12500
        N_EDGES = 200000
        IN_SIZE = 64
        OUT_SIZE = 64
        N_HEADS = 2
        NEG_SLOPE = 0.2
        BN_EPS = 1e-05
        key = jax.random.key(seed)
        ks = jax.random.split(key, 8)
        atom = jax.random.normal(ks[0], (N_NODES, IN_SIZE), dtype=jnp.float32)
        bond = jax.random.normal(ks[1], (N_EDGES, IN_SIZE), dtype=jnp.float32)
        W = jax.random.normal(ks[2], (IN_SIZE, OUT_SIZE * N_HEADS), dtype=jnp.float32) * 0.1
        attn_l = jax.random.normal(ks[3], (N_HEADS, OUT_SIZE), dtype=jnp.float32) * 0.1
        attn_r = jax.random.normal(ks[4], (N_HEADS, OUT_SIZE), dtype=jnp.float32) * 0.1
        bn_gamma = jnp.ones((OUT_SIZE,), dtype=jnp.float32)
        bn_beta = jnp.zeros((OUT_SIZE,), dtype=jnp.float32)
        src = jax.random.randint(ks[5], (N_EDGES,), 0, N_NODES, dtype=jnp.int32)
        dst = jax.random.randint(ks[6], (N_EDGES,), 0, N_NODES, dtype=jnp.int32)
        return {'atom': atom, 'bond': bond, 'W': W, 'attn_l': attn_l, 'attn_r': attn_r, 'bn_gamma': bn_gamma, 'bn_beta': bn_beta, 'src': src, 'dst': dst}
    _L1_gnn_all = _L1_gnn_setup()
    _L1_gnn_in = {k: v for k, v in _L1_gnn_all.items() if k in ('W', 'attn_l', 'attn_r', 'bn_gamma', 'bn_beta')}
    del _L1_gnn_all

    def _L2_gnn_setup():
        import jax, jax.numpy as jnp
        import numpy as np
        D_MODEL = 64
        N_HEAD = 1
        N_NODES = 6250
        N_EDGES = 100000
        EPS = 1e-06
        NEG_SLOPE = 0.01
        key = jax.random.key(seed)
        ks = jax.random.split(key, 12)
        d, H = (D_MODEL, N_HEAD)
        xav = lambda k, shp: jax.random.normal(k, shp, jnp.float32) * np.sqrt(2.0 / (shp[0] + shp[1]))
        return {'h': jax.random.normal(ks[0], (N_NODES, d), jnp.float32), 'eh': jax.random.normal(ks[1], (N_EDGES, d), jnp.float32), 'qrh': jax.random.normal(ks[2], (N_EDGES, d), jnp.float32), 'qeh': jax.random.normal(ks[3], (N_EDGES, d), jnp.float32), 'src': jax.random.randint(ks[4], (N_EDGES,), 0, N_NODES, jnp.int32), 'dst': jax.random.randint(ks[5], (N_EDGES,), 0, N_NODES, jnp.int32), 'W_msg': xav(ks[6], (2 * d, H * d)), 'W_q': xav(ks[7], (2 * d, H * d)), 'W_k': xav(ks[8], (2 * d, H * d)), 'W_out': xav(ks[9], (H * d, d)), 'gamma': jnp.ones((d,), jnp.float32), 'beta': jnp.zeros((d,), jnp.float32)}
    _L2_gnn_all = _L2_gnn_setup()
    _L2_gnn_in = {k: v for k, v in _L2_gnn_all.items() if k in ('W_msg', 'W_q', 'W_k', 'W_out', 'gamma', 'beta')}
    del _L2_gnn_all

    def _L3_gnn_setup():
        import jax, jax.numpy as jnp
        import numpy as np
        N_NODES, N_EDGES = (6250, 100000)
        NODE_DIM, EDGE_DIM, HIDDEN, NUM_LAYERS = (64, 32, 64, 2)
        IN_MSG = NODE_DIM + EDGE_DIM
        IN_UPD = NODE_DIM + HIDDEN
        key = jax.random.key(seed)
        ks = jax.random.split(key, 12)

        def w(k, shape, fan_in):
            return jax.random.normal(k, shape, jnp.float32) * (1.0 / np.sqrt(fan_in))
        return {'node_features': jax.random.normal(ks[0], (N_NODES, NODE_DIM), jnp.float32), 'edge_features': jax.random.normal(ks[1], (N_EDGES, EDGE_DIM), jnp.float32), 'msg_w1': w(ks[2], (NUM_LAYERS, IN_MSG, HIDDEN), IN_MSG), 'msg_b1': w(ks[3], (NUM_LAYERS, HIDDEN), IN_MSG), 'msg_w2': w(ks[4], (NUM_LAYERS, HIDDEN, HIDDEN), HIDDEN), 'msg_b2': w(ks[5], (NUM_LAYERS, HIDDEN), HIDDEN), 'upd_w1': w(ks[6], (IN_UPD, HIDDEN), IN_UPD), 'upd_b1': w(ks[7], (HIDDEN,), IN_UPD), 'upd_w2': w(ks[8], (HIDDEN, NODE_DIM), HIDDEN), 'upd_b2': w(ks[9], (NODE_DIM,), HIDDEN), 'src': jax.random.randint(ks[10], (N_EDGES,), 0, N_NODES, dtype=jnp.int32), 'dst': jax.random.randint(ks[11], (N_EDGES,), 0, N_NODES, dtype=jnp.int32)}
    _L3_gnn_all = _L3_gnn_setup()
    _L3_gnn_in = {k: v for k, v in _L3_gnn_all.items() if k in ('msg_w1', 'msg_b1', 'msg_w2', 'msg_b2', 'upd_w1', 'upd_b1', 'upd_w2', 'upd_b2')}
    del _L3_gnn_all
    return {'x': x, 'src': src, 'dst': dst, 'edge_attr_32': edge_attr_32, 'edge_attr_64': edge_attr_64, 'edge_attr_64_n2': edge_attr_64_n2, 'edge_attr_64_n3': edge_attr_64_n3, 'L0_gnn_Wq': _L0_gnn_in['Wq'], 'L0_gnn_bq': _L0_gnn_in['bq'], 'L0_gnn_Wk': _L0_gnn_in['Wk'], 'L0_gnn_bk': _L0_gnn_in['bk'], 'L0_gnn_Wv': _L0_gnn_in['Wv'], 'L0_gnn_bv': _L0_gnn_in['bv'], 'L0_gnn_Ws': _L0_gnn_in['Ws'], 'L0_gnn_bs': _L0_gnn_in['bs'], 'L0_gnn_Wg': _L0_gnn_in['Wg'], 'L0_gnn_bg': _L0_gnn_in['bg'], 'L0_gnn_ln_g': _L0_gnn_in['ln_g'], 'L0_gnn_ln_b': _L0_gnn_in['ln_b'], 'L0_gnn_prelu_a': _L0_gnn_in['prelu_a'], 'L1_gnn_W': _L1_gnn_in['W'], 'L1_gnn_attn_l': _L1_gnn_in['attn_l'], 'L1_gnn_attn_r': _L1_gnn_in['attn_r'], 'L1_gnn_bn_gamma': _L1_gnn_in['bn_gamma'], 'L1_gnn_bn_beta': _L1_gnn_in['bn_beta'], 'L2_gnn_W_msg': _L2_gnn_in['W_msg'], 'L2_gnn_W_q': _L2_gnn_in['W_q'], 'L2_gnn_W_k': _L2_gnn_in['W_k'], 'L2_gnn_W_out': _L2_gnn_in['W_out'], 'L2_gnn_gamma': _L2_gnn_in['gamma'], 'L2_gnn_beta': _L2_gnn_in['beta'], 'L3_gnn_msg_w1': _L3_gnn_in['msg_w1'], 'L3_gnn_msg_b1': _L3_gnn_in['msg_b1'], 'L3_gnn_msg_w2': _L3_gnn_in['msg_w2'], 'L3_gnn_msg_b2': _L3_gnn_in['msg_b2'], 'L3_gnn_upd_w1': _L3_gnn_in['upd_w1'], 'L3_gnn_upd_b1': _L3_gnn_in['upd_b1'], 'L3_gnn_upd_w2': _L3_gnn_in['upd_w2'], 'L3_gnn_upd_b2': _L3_gnn_in['upd_b2']}

def reference(x, src, dst, edge_attr_32, edge_attr_64, edge_attr_64_n2, edge_attr_64_n3, L0_gnn_Wq, L0_gnn_bq, L0_gnn_Wk, L0_gnn_bk, L0_gnn_Wv, L0_gnn_bv, L0_gnn_Ws, L0_gnn_bs, L0_gnn_Wg, L0_gnn_bg, L0_gnn_ln_g, L0_gnn_ln_b, L0_gnn_prelu_a, L1_gnn_W, L1_gnn_attn_l, L1_gnn_attn_r, L1_gnn_bn_gamma, L1_gnn_bn_beta, L2_gnn_W_msg, L2_gnn_W_q, L2_gnn_W_k, L2_gnn_W_out, L2_gnn_gamma, L2_gnn_beta, L3_gnn_msg_w1, L3_gnn_msg_b1, L3_gnn_msg_w2, L3_gnn_msg_b2, L3_gnn_upd_w1, L3_gnn_upd_b1, L3_gnn_upd_w2, L3_gnn_upd_b2):
    import jax
    import jax.numpy as jnp

    def _L0_gnn_ref(feat, edge_src, edge_dst, Wq, bq, Wk, bk, Wv, bv, Ws, bs, Wg, bg, ln_g, ln_b, prelu_a):
        import jax, jax.numpy as jnp
        import numpy as np
        N = 12500
        E = 200000
        IN = 64
        H = 4
        D = 16
        HD = H * D
        LN_EPS = 1e-05

        def _forward(feat, edge_src, edge_dst, Wq, bq, Wk, bk, Wv, bv, Ws, bs, Wg, bg, ln_g, ln_b, prelu_a):
            q = (feat @ Wq + bq).reshape(N, H, D)
            k = (feat @ Wk + bk).reshape(N, H, D)
            v = (feat @ Wv + bv).reshape(N, H, D)
            scores = jnp.einsum('ehd,ehd->eh', q[edge_src], k[edge_dst]) / np.sqrt(D).astype(np.float32)
            smax = jax.ops.segment_max(scores, edge_dst, num_segments=N)
            smax = jnp.where(jnp.isfinite(smax), smax, 0.0)
            ex = jnp.exp(scores - smax[edge_dst])
            denom = jax.ops.segment_sum(ex, edge_dst, num_segments=N)
            sa = ex / denom[edge_dst]
            agg = jax.ops.segment_sum(sa[:, :, None] * v[edge_src], edge_dst, num_segments=N)
            rst = agg.reshape(N, HD)
            skip = feat @ Ws + bs
            gate = jax.nn.sigmoid(jnp.concatenate([skip, rst, skip - rst], axis=-1) @ Wg + bg)
            rst = gate * skip + (1.0 - gate) * rst
            mu = jnp.mean(rst, axis=-1, keepdims=True)
            var = jnp.mean(jnp.square(rst - mu), axis=-1, keepdims=True)
            rst = (rst - mu) * jax.lax.rsqrt(var + LN_EPS) * ln_g + ln_b
            return jnp.where(rst >= 0, rst, prelu_a * rst)
        return _forward(feat, edge_src, edge_dst, Wq, bq, Wk, bk, Wv, bv, Ws, bs, Wg, bg, ln_g, ln_b, prelu_a)

    def _L1_gnn_ref(atom, bond, W, attn_l, attn_r, bn_gamma, bn_beta, src, dst):
        import jax, jax.numpy as jnp
        import numpy as np
        N_NODES = 12500
        N_EDGES = 200000
        IN_SIZE = 64
        OUT_SIZE = 64
        N_HEADS = 2
        NEG_SLOPE = 0.2
        BN_EPS = 1e-05
        N = atom.shape[0]
        H, D = attn_l.shape
        h_edge = ((atom[src] + bond) @ W).reshape(-1, H, D)
        h_node = (atom @ W).reshape(-1, H, D)
        el = jnp.einsum('ehd,hd->eh', h_edge, attn_l)
        er = jnp.einsum('nhd,hd->nh', h_node, attn_r)
        s = el + er[dst]
        s = jnp.where(s > 0, s, NEG_SLOPE * s)
        smax = jax.ops.segment_max(s, dst, num_segments=N)
        ex = jnp.exp(s - smax[dst])
        denom = jax.ops.segment_sum(ex, dst, num_segments=N)
        alpha = ex / denom[dst]
        ft = jax.ops.segment_sum(h_edge * alpha[..., None], dst, num_segments=N)
        h = ft.mean(axis=1)
        mu = h.mean(axis=0)
        var = h.var(axis=0)
        h = (h - mu) / jnp.sqrt(var + BN_EPS) * bn_gamma + bn_beta
        h = jax.nn.relu(h)
        return h

    def _L2_gnn_ref(h, eh, qrh, qeh, src, dst, W_msg, W_q, W_k, W_out, gamma, beta):
        import jax, jax.numpy as jnp
        import numpy as np
        D_MODEL = 64
        N_HEAD = 1
        N_NODES = 6250
        N_EDGES = 100000
        EPS = 1e-06
        NEG_SLOPE = 0.01
        N, d = h.shape
        E = eh.shape[0]
        H = W_msg.shape[1] // d
        temp = jnp.asarray(d, h.dtype) ** 0.5
        src_h = h[src]
        se = jnp.concatenate([src_h, eh], axis=-1)
        msg = jax.nn.leaky_relu(se @ W_msg, NEG_SLOPE).reshape(E, H, d)
        q = (jnp.concatenate([qrh, qeh], axis=-1) @ W_q / temp).reshape(E, H, d)
        k = (se @ W_k).reshape(E, H, d)
        att = jnp.sum(q * k, axis=-1)
        m = jax.ops.segment_max(att, dst, num_segments=N)
        e = jnp.exp(att - jax.lax.stop_gradient(m)[dst])
        denom = jax.ops.segment_sum(e, dst, num_segments=N)
        alpha = e / denom[dst]
        agg = jax.ops.segment_sum(alpha[..., None] * msg, dst, num_segments=N)
        hn = jax.nn.leaky_relu(agg.reshape(N, H * d) @ W_out, NEG_SLOPE) + h
        mu = jnp.mean(hn, axis=-1, keepdims=True)
        var = jnp.mean((hn - mu) ** 2, axis=-1, keepdims=True)
        ln = (hn - mu) / jnp.sqrt(var + EPS) * gamma + beta
        deg = jax.ops.segment_sum(jnp.ones((E,), h.dtype), dst, num_segments=N)
        return jnp.where(deg[:, None] > 0, ln, h)

    def _L3_gnn_ref(node_features, edge_features, msg_w1, msg_b1, msg_w2, msg_b2, upd_w1, upd_b1, upd_w2, upd_b2, src, dst):
        import jax, jax.numpy as jnp
        import numpy as np
        N_NODES, N_EDGES = (6250, 100000)
        NODE_DIM, EDGE_DIM, HIDDEN, NUM_LAYERS = (64, 32, 64, 2)
        IN_MSG = NODE_DIM + EDGE_DIM
        IN_UPD = NODE_DIM + HIDDEN
        n_nodes = node_features.shape[0]
        combined = jnp.concatenate([node_features[src], edge_features], axis=-1)
        msg = jnp.zeros((combined.shape[0], msg_w2.shape[-1]), combined.dtype)
        for l in range(msg_w1.shape[0]):
            h = jax.nn.relu(combined @ msg_w1[l] + msg_b1[l])
            msg = msg + (h @ msg_w2[l] + msg_b2[l])
        agg = jax.ops.segment_sum(msg, dst, num_segments=n_nodes)
        deg = jax.ops.segment_sum(jnp.ones((dst.shape[0],), msg.dtype), dst, num_segments=n_nodes)
        agg = agg / (deg[:, None] + 1e-08)
        comb2 = jnp.concatenate([node_features, agg], axis=-1)
        return jax.nn.relu(comb2 @ upd_w1 + upd_b1) @ upd_w2 + upd_b2
    x = _layernorm(x + _L0_gnn_ref(x, src, dst, L0_gnn_Wq, L0_gnn_bq, L0_gnn_Wk, L0_gnn_bk, L0_gnn_Wv, L0_gnn_bv, L0_gnn_Ws, L0_gnn_bs, L0_gnn_Wg, L0_gnn_bg, L0_gnn_ln_g, L0_gnn_ln_b, L0_gnn_prelu_a), axis=-1)
    x = _layernorm(x + _L1_gnn_ref(x, edge_attr_64, L1_gnn_W, L1_gnn_attn_l, L1_gnn_attn_r, L1_gnn_bn_gamma, L1_gnn_bn_beta, src, dst), axis=-1)
    x = _layernorm(x + _L2_gnn_ref(x, edge_attr_64, edge_attr_64_n2, edge_attr_64_n3, src, dst, L2_gnn_W_msg, L2_gnn_W_q, L2_gnn_W_k, L2_gnn_W_out, L2_gnn_gamma, L2_gnn_beta), axis=-1)
    x = _layernorm(x + _L3_gnn_ref(x, edge_attr_32, L3_gnn_msg_w1, L3_gnn_msg_b1, L3_gnn_msg_w2, L3_gnn_msg_b2, L3_gnn_upd_w1, L3_gnn_upd_b1, L3_gnn_upd_w2, L3_gnn_upd_b2, src, dst), axis=-1)
    return x

_drawn_inputs = setup_inputs


def setup_inputs(seed=0):
    import zlib

    import numpy as np

    out = dict(_drawn_inputs(seed))
    spreads = {'L0_gnn_ln_g': (1.0, 0.2),
     'L0_gnn_ln_b': (0.0, 0.1),
     'L1_gnn_bn_gamma': (1.0, 0.2),
     'L1_gnn_bn_beta': (0.0, 0.1),
     'L2_gnn_gamma': (1.0, 0.2),
     'L2_gnn_beta': (0.0, 0.1)}
    factors = {'L0_gnn_bq': 8.0, 'L0_gnn_bk': 7.929}
    for name, (base, spread) in spreads.items():
        noise = np.random.default_rng([zlib.crc32(name.encode()), seed]).standard_normal(out[name].shape)
        drawn = base * np.exp(spread * noise) if base else spread * noise
        out[name] = jnp.asarray(drawn.astype(out[name].dtype))
    for name, factor in factors.items():
        out[name] = (out[name] * factor).astype(out[name].dtype)
    return out
```

```python
from contextlib import ExitStack

import numpy as np

import concourse.bass as bass
from concourse import mybir

F32 = mybir.dt.float32
I32 = mybir.dt.int32
U32 = mybir.dt.uint32
ALU = mybir.AluOpType
ACT = mybir.ActivationFunctionType
AX = mybir.AxisListType

P = 128
J = 28
G = 7
QUAD = 4
FD = 64
FAR = -1.0e30
SKIPPED = 1.0e9
BC = ["L0_gnn_Wg", "L0_gnn_ln_g", "L0_gnn_ln_b", "L1_gnn_bn_gamma", "L1_gnn_bn_beta", "L2_gnn_gamma",
      "L2_gnn_beta", "L3_gnn_msg_b2", "L3_gnn_upd_b1", "L3_gnn_upd_b2"]


def at(i, per, k):
    return i * per + k


def hold(e, sem, value, passed):
    e.wait_ge(sem, value)
    e.sem_inc(passed, 1)


def rows_of(i, b, size):
    return bass.ds(i * (2 * size) + b * size, size)


def bcast(ap, axis, n):
    a = ap.unsqueeze(axis)
    shape = list(a.shape)
    shape[axis] = n
    return a.to_broadcast(shape)


class Program:

    def __init__(self, nc, ins, out, n_nodes, ctx):
        self.nc, self.ins, self.out, self.ctx = nc, ins, out, ctx
        self.n_nodes = n_nodes
        self.edges_pp = ins["src"].shape[1]
        self.nodes_pp = ins["x"].shape[0] // P
        self.n_edges = P * self.edges_pp
        self.n_rows = P * self.nodes_pp
        self.chunks = self.edges_pp // J
        self.groups = self.nodes_pp // G
        assert self.chunks % 2 == 0 and self.groups % 2 == 0 and J % QUAD == 0
        self.find_rows, self.find_cols = ins["dst_table"].shape

        def dram(name, shape, dt=F32):
            return nc.dram_tensor(name, shape, dt).ap()

        n, e = self.n_rows, self.n_edges
        self.qv_table = dram("qv_table", [n, 2 * FD])
        self.k_table = dram("k_table", [n, FD])
        self.k_edges = dram("k_edges", [e, FD])
        self.er_table = dram("er_table", [n, 2])
        self.er_edges = dram("er_edges", [e, 2])
        self.end_table = dram("end_table", [n + 1, 1])
        self.x_tables = [dram(f"x_table{k}", [n, FD]) for k in (1, 2, 3)]
        self.find_index = dram("find_index", [P, self.nodes_pp], U32)
        self.end_index = dram("end_index", [P, self.nodes_pp], U32)
        self.start_index = dram("start_index", [P, self.nodes_pp], U32)
        self.shape = [(4, 16), (2, 64), (1, 64), (0, 128)]
        self.width = [h * (d + 2) if h else d for h, d in self.shape]
        self.sums = [dram(f"sums{k}", [e, w]) for k, w in enumerate(self.width)]

        def keep(name, shape, dt=F32):
            return ctx.enter_context(nc.sbuf_tensor(name, shape, dt))

        self.x = keep("x_now", [P, self.nodes_pp, FD])
        self.aux = keep("aux_now", [P, self.nodes_pp, FD])
        self.same = keep("same", [P, self.edges_pp])
        self.node = keep("node_number", [P, self.nodes_pp])
        self.live = keep("live", [P, self.nodes_pp])
        self.real = keep("real", [P, self.nodes_pp])
        self.degree = keep("degree", [P, self.nodes_pp])
        self.ident = keep("ident", [P, P])
        self.ones = keep("ones", [P, P])
        self.chain = keep("chain", [P, P])
        self.chain_t = keep("chain_t", [P, P])
        self.chain_pen = keep("chain_pen", [P, P])
        self.first = keep("first_dst", [P, 1])
        self.first_index = keep("first_index", [P, 1], U32)
        self.first_end_index = keep("first_end_index", [P, 1], U32)
        self.fix_from = keep("fix_from", [P, 1], U32)
        self.fix_to = keep("fix_to", [P, 1], U32)
        self.carry = keep("carry", [P, 2 * 65])
        self.peak = keep("peak", [P, J + 1, 4])
        self.param = {}
        for name in BC:
            self.param[name] = keep("bc_" + name, [P, int(np.prod(ins[name].shape))])
        self.gate_bias = keep("gate_bias", [P, 1])
        self.slope = keep("prelu_slope", [P, 1])
        self.w_nodes = keep("w_nodes", [FD + 1, 4 * FD])
        self.gate_a = keep("gate_a", [P, FD])
        self.gate_b = keep("gate_b", [P, FD])
        self.w1 = keep("w1", [FD, 2 * FD])
        self.w1_heads = keep("w1_heads", [2 * FD, FD])
        self.attn_l = keep("attn_l", [P, 2, FD])
        self.attn_r = keep("attn_r", [P, 2, FD])
        self.w2_mk = keep("w2_mk", [P, P])
        self.w2_qr = keep("w2_qr", [P, P])
        self.w2_qe = keep("w2_qe", [P, P])
        self.w2_out = keep("w2_out", [FD, FD])
        self.w3_hidden = keep("w3_hidden", [97, P])
        self.w3_msg = keep("w3_msg", [P, FD])
        self.w3_upd1 = keep("w3_upd1", [P, FD])
        self.w3_upd2 = keep("w3_upd2", [FD, FD])


def setup_phase(p):
    nc, ins = p.nc, p.ins
    with nc.reset_on_exit(), ExitStack() as ctx:
        dst_i = ctx.enter_context(nc.sbuf_tensor("dst_i", [P, p.edges_pp], I32))
        dst_f = ctx.enter_context(nc.sbuf_tensor("dst_f", [P, p.edges_pp + 1], F32))
        node_i = ctx.enter_context(nc.sbuf_tensor("node_i", [P, p.nodes_pp], I32))
        before = ctx.enter_context(nc.sbuf_tensor("before", [P, P], F32))
        att_cols = ctx.enter_context(nc.sbuf_tensor("att_cols", [FD, 4], F32))
        att_wide = ctx.enter_context(nc.sbuf_tensor("att_wide", [FD, 4, P], F32))
        w1_t = ctx.enter_context(nc.sbuf_tensor("w1_t", [FD, 2, FD], F32))
        tail_wide = ctx.enter_context(nc.sbuf_tensor("tail_wide", [P, P], F32))
        ps_a = ctx.enter_context(nc.psum_tensor("setup_ps_a", [P, 4, P], F32))
        ps_b = ctx.enter_context(nc.psum_tensor("setup_ps_b", [P, 4, P], F32))
        loaded = ctx.enter_context(nc.semaphore("setup_loaded"))
        dst_in = ctx.enter_context(nc.semaphore("dst_in"))
        cleared = ctx.enter_context(nc.semaphore("w2_cleared"))
        pool_done = ctx.enter_context(nc.semaphore("setup_pool"))
        to_pe = ctx.enter_context(nc.semaphore("setup_to_pe"))
        from_pe = ctx.enter_context(nc.semaphore("setup_from_pe"))
        block = ctx.enter_context(nc.Block())
        loads = [0]

        @block.sync
        def _(e):
            def load(to, of):
                e.dma_start(to, of).then_inc(loaded, 16)
                loads[0] += 16

            e.dma_start(dst_i[:, :], ins["dst"]).then_inc(dst_in, 16)
            load(p.x[:, :, :], ins["x"].rearrange("(p t) f -> p t f", p=P))
            for k, name in enumerate("qvks"):
                load(p.w_nodes[0:FD, k * FD:(k + 1) * FD], ins[f"L0_gnn_W{name}"])
                load(p.w_nodes[FD:FD + 1, k * FD:(k + 1) * FD], ins[f"L0_gnn_b{name}"].unsqueeze(0))
            for name in BC:
                flat = ins[name]
                if len(flat.shape) == 2:
                    flat = flat.rearrange("a b -> (a b)")
                load(p.param[name][:, :], flat.partition_broadcast(P))
            load(p.gate_bias[:, :], ins["L0_gnn_bg"].partition_broadcast(P))
            load(p.slope[:, :], ins["L0_gnn_prelu_a"].partition_broadcast(P))
            load(p.w1[:, :], ins["L1_gnn_W"])
            for h in range(2):
                load(p.w1_heads[h * FD:(h + 1) * FD, :], ins["L1_gnn_W"][:, h * FD:(h + 1) * FD])
            with nc.allow_non_contiguous_dma(reason="four short columns"):
                for k, name in enumerate("lr"):
                    load(att_cols[:, 2 * k:2 * k + 2], ins[f"L1_gnn_attn_{name}"].rearrange("h d -> d h"))
            load(p.w2_mk[:, 0:FD], ins["L2_gnn_W_msg"])
            load(p.w2_mk[:, FD:P], ins["L2_gnn_W_k"])
            load(p.w2_out[:, :], ins["L2_gnn_W_out"])
            for k in range(2):
                load(p.w3_hidden[0:96, k * FD:(k + 1) * FD], ins["L3_gnn_msg_w1"][k, :, :])
                load(p.w3_hidden[96:97, k * FD:(k + 1) * FD], ins["L3_gnn_msg_b1"][k:k + 1, :])
                load(p.w3_msg[k * FD:(k + 1) * FD, :], ins["L3_gnn_msg_w2"][k, :, :])
            load(p.w3_upd1[:, :], ins["L3_gnn_upd_w1"])
            load(p.w3_upd2[:, :], ins["L3_gnn_upd_w2"])
            e.wait_ge(cleared, 1)
            for half in range(2):
                s = slice(half * FD, (half + 1) * FD)
                load(p.w2_qr[s, s], ins["L2_gnn_W_q"][0:FD, :])
                load(p.w2_qe[s, s], ins["L2_gnn_W_q"][FD:P, :])

        @block.gpsimd
        def _(e):
            e.memset(p.ident[:, :], 0.0)
            e.memset(p.ones[:, :], 1.0)
            e.memset(before[:, :], 1.0).then_inc(pool_done, 1)
            e.wait_ge(pool_done, 1)
            e.affine_select(out=p.ident[:, :], in_=p.ident[:, :], compare_op=ALU.not_equal, fill=1.0,
                            base=0, pattern=[[-1, P]], channel_multiplier=1)
            e.affine_select(out=before[:, :], in_=before[:, :], compare_op=ALU.is_gt, fill=0.0,
                            base=0, pattern=[[-1, P]], channel_multiplier=1)
            e.iota(node_i[:, :], pattern=[[1, p.nodes_pp]], base=0, channel_multiplier=p.nodes_pp)\
                .then_inc(pool_done, 1)

        @block.vector
        def _(e):
            e.memset(p.w2_qr[:, :], 0.0)
            e.memset(p.w2_qe[:, :], 0.0).then_inc(cleared, 1)
            e.memset(dst_f[:, 0:1], -1.0)
            e.wait_ge(dst_in, 16)
            e.tensor_copy(dst_f[:, 1:], dst_i[:, :])
            e.drain()
            e.tensor_tensor(p.same[:, :], dst_f[:, 1:], dst_f[:, 0:p.edges_pp], ALU.is_equal)
            e.tensor_copy(p.first[:, :], dst_f[:, 1:2])
            e.tensor_copy(p.first_index[:, :], dst_i[:, 0:1])
            e.tensor_scalar(p.first_end_index[:, :], dst_f[:, 1:2], 1.0, None, ALU.add)
            e.wait_ge(pool_done, 2)
            e.tensor_copy(p.node[:, :], node_i[:, :])
            e.tensor_copy(tail_wide[:, :], dst_f[:, p.edges_pp:].to_broadcast([P, P]))
            e.wait_ge(loaded, loads[0])
            e.tensor_copy(att_wide[:, :, :], bcast(att_cols[:, :], 2, P)).then_inc(to_pe, 1)
            wg = p.param["L0_gnn_Wg"]
            e.tensor_tensor(p.gate_a[:, :], wg[:, 0:FD], wg[:, 2 * FD:3 * FD], ALU.add)
            e.tensor_tensor(p.gate_b[:, :], wg[:, FD:2 * FD], wg[:, 2 * FD:3 * FD], ALU.subtract)
            e.tensor_scalar(p.gate_bias[:, :], p.gate_bias[:, :], -1.0, None, ALU.mult)
            e.tensor_scalar(p.w1_heads[:, :], p.w1_heads[:, :], 0.5, None, ALU.mult)
            e.wait_ge(from_pe, 1)
            e.tensor_scalar(p.chain[:, :], ps_a[:, 0, :], p.first[:, 0:1], None, ALU.is_equal)
            e.tensor_copy(w1_t[:, :, :], ps_a[0:FD, 1:3, 0:FD])
            e.drain()
            e.tensor_tensor(p.chain[:, :], p.chain[:, :], before[:, :], ALU.mult)
            e.drain().then_inc(to_pe, 1)
            e.tensor_scalar(p.chain_pen[:, :], p.chain[:, :], -1.0, -FAR, ALU.add, ALU.mult)
            e.wait_ge(from_pe, 2)
            e.tensor_copy(p.chain_t[:, :], ps_a[:, 3, :])
            e.tensor_copy(p.attn_l[:, :, :], ps_b[:, 0:2, 0:FD])
            e.tensor_copy(p.attn_r[:, :, :], ps_b[:, 2:4, 0:FD])

        @block.tensor
        def _(e):
            e.wait_ge(pool_done, 2)
            e.wait_ge(to_pe, 1)
            e.matmul(ps_a[:, 0, :], tail_wide[:, :], p.ident[:, :], start=True, stop=True)
            for h in range(2):
                ins_ = e.transpose(ps_a[0:FD, 1 + h, 0:FD], p.w1[:, h * FD:(h + 1) * FD],
                                   p.ident[0:FD, 0:FD])
            ins_.then_inc(from_pe, 1)
            e.wait_ge(to_pe, 2)
            e.transpose(ps_a[:, 3, :], p.chain[:, :], p.ident[:, :])
            for k in range(4):
                ins_ = e.matmul(ps_b[:, k, 0:FD], att_wide[:, k, :], w1_t[:, k % 2, :],
                                start=True, stop=True)
            ins_.then_inc(from_pe, 1)


def search_phase(p):
    nc = p.nc
    R1, W, T = p.find_rows, p.find_cols, p.nodes_pp
    rounds = p.groups // 2
    with nc.reset_on_exit(), ExitStack() as ctx:
        sb = lambda n, s, d=F32: ctx.enter_context(nc.sbuf_tensor(n, s, d))
        sem = lambda n: ctx.enter_context(nc.semaphore(n))
        heads_i = sb("heads_i", [1, R1], I32)
        heads_f = sb("heads_f", [1, R1])
        heads = sb("heads", [P, R1])
        compared = sb("compared", [P, G, max(R1, W)])
        row = sb("found_row", [P, T])
        row_u = sb("found_row_u", [P, T], U32)
        start_u = sb("start_u", [P, T], U32)
        count = sb("found_count", [P, T])
        ends = sb("ends", [P, T])
        starts = sb("starts", [P, T])
        start_f = sb("start_f", [P, T])
        picked = [sb(f"picked{b}", [P, G, W], I32) for b in (0, 1)]
        pick_ix = [sb(f"pick_ix{b}", [P, G], U32) for b in (0, 1)]
        zeros = sb("zeros", [P, 2 * J * FD])
        end_zero = sb("end_zero", [1, 1])
        fix_f = sb("fix_f", [P, 1])
        fix_lim = sb("fix_lim", [P, 1])
        fix_ok = sb("fix_ok", [P, 1])
        lim_i = sb("lim_i", [P, 1], I32)
        chained = sb("chained", [P, 1])
        x_in = sb("x_in", [P, G, FD + 1])
        x_t = sb("x_t", [FD + 1, G, P])
        qv_out = sb("qv_out", [P, G, 2 * FD])
        k_out = sb("k_out", [P, G, FD])
        heads_ps = ctx.enter_context(nc.psum_tensor("heads_ps", [P, R1], F32))
        xt_ps = ctx.enter_context(nc.psum_tensor("xt_ps", [P, 2, QUAD, P], F32))
        proj_ps = ctx.enter_context(nc.psum_tensor("proj_ps", [P, 4, 2, 4 * FD], F32))
        s_head = sem("s_head")
        s_hps = sem("s_hps")
        s_row = sem("s_row")
        s_rowst = sem("s_rowst")
        s_ix = [sem(f"s_ix{b}") for b in (0, 1)]
        s_got = [sem(f"s_got{b}") for b in (0, 1)]
        s_free = [sem(f"s_free{b}") for b in (0, 1)]
        s_end = sem("s_end")
        s_endst = sem("s_endst")
        s_start = sem("s_start")
        s_zero = sem("s_zero")
        s_index = sem("s_index")
        s_indexst = sem("s_indexst")
        s_fix = sem("s_fix")
        s_lim = sem("s_lim")
        s_xin = sem("s_xin")
        s_xps = sem("s_xps")
        s_xt = sem("s_xt")
        s_proj = sem("s_proj")
        s_out = sem("s_out")
        s_outst = sem("s_outst")
        s_passed = sem("s_passed")
        block = ctx.enter_context(nc.Block())

        @block.sync
        def _(e):
            with nc.allow_non_contiguous_dma(reason="one element of every table row"):
                e.dma_start(heads_i[0:1, :], p.ins["dst_table"][:, 0:1].rearrange("r a -> a r"))\
                    .then_inc(s_head, 16)
            e.wait_ge(s_row, 1)
            e.dma_start(p.find_index, row_u[:, :]).then_inc(s_rowst, 16)
            e.wait_ge(s_rowst, 16)
            with e.Fori(0, rounds) as i:
                for b in (0, 1):
                    hold(e, s_free[b], at(i, 1, 1), s_passed)
                    e.dma_start(pick_ix[b][:, :], p.find_index[:, rows_of(i, b, G)]).then_inc(s_ix[b], 16)
            e.wait_ge(s_end, 1)
            e.dma_start(p.end_table[0:1, :], end_zero[0:1, :]).then_inc(s_endst, 16)
            e.dma_start(p.end_table[1:, :].rearrange("(p t) a -> p (t a)", p=P), ends[:, :])\
                .then_inc(s_endst, 16)
            e.wait_ge(s_endst, 32)
            e.dma_start(starts[:, :], p.end_table[0:p.n_rows, :].rearrange("(p t) a -> p (t a)", p=P))\
                .then_inc(s_start, 16)
            e.wait_ge(s_index, 1)
            e.dma_start(p.end_index, row_u[:, :]).then_inc(s_indexst, 16)
            e.dma_start(p.start_index, start_u[:, :]).then_inc(s_indexst, 16)
            e.wait_ge(s_indexst, 32)

        @block.gpsimd
        def _(e):
            e.iota(lim_i[:, :], pattern=[[0, 1]], base=p.edges_pp, channel_multiplier=p.edges_pp)\
                .then_inc(s_lim, 1)
            with e.Fori(0, rounds) as i:
                for b in (0, 1):
                    hold(e, s_ix[b], at(i, 16, 16), s_passed)
                    for t in range(G):
                        e.indirect_dma_start(picked[b][:, t, :], None, p.ins["dst_table"],
                                             bass.IndirectOffsetOnAxis(ap=pick_ix[b][:, t:t + 1], axis=0))\
                            .then_inc(s_got[b], 16)
            e.wait_ge(s_endst, 32)
            e.indirect_dma_start(fix_f[:, :], None, p.end_table,
                                 bass.IndirectOffsetOnAxis(ap=p.first_end_index[:, 0:1], axis=0))\
                .then_inc(s_fix, 16)

        @block.vector
        def _(e):
            e.memset(end_zero[:, :], 0.0)
            e.memset(zeros[:, :], 0.0).then_inc(s_zero, 1)
            for b in (0, 1):
                e.drain().then_inc(s_free[b], 1)
            e.wait_ge(s_head, 16)
            e.tensor_copy(heads_f[:, :], heads_i[:, :]).then_inc(s_hps, 1)
            e.wait_ge(s_hps, 2)
            e.tensor_copy(heads[:, :], heads_ps[:, :])
            e.drain()
            with e.Fori(0, p.groups) as i:
                now = bass.ds(i * G, G)
                e.tensor_tensor(compared[:, :, 0:R1], bcast(heads[:, :], 1, G),
                                bcast(p.node[:, now], 2, R1), ALU.is_le)
                e.drain()
                e.tensor_reduce(row[:, now], compared[:, :, 0:R1], AX.X, ALU.add)
                e.drain()
            e.tensor_scalar(row[:, :], row[:, :], -1.0, 0.0, ALU.add, ALU.max)
            e.drain()
            e.tensor_copy(row_u[:, :], row[:, :]).then_inc(s_row, 1)
            with e.Fori(0, rounds) as i:
                for b in (0, 1):
                    now = rows_of(i, b, G)
                    e.wait_ge(s_got[b], at(i, 16 * G, 16 * G))
                    e.tensor_tensor(compared[:, :, 0:W], picked[b][:, :, :],
                                    bcast(p.node[:, now], 2, W), ALU.is_le)
                    e.drain().then_inc(s_free[b], 1)
                    e.tensor_reduce(count[:, now], compared[:, :, 0:W], AX.X, ALU.add)
                    e.drain()
            e.scalar_tensor_tensor(ends[:, :], row[:, :], float(W), count[:, :], ALU.mult, ALU.add)\
                .then_inc(s_end, 1)
            e.tensor_scalar(p.real[:, :], p.node[:, :], float(p.n_nodes), None, ALU.is_lt)
            e.wait_ge(s_start, 16)
            e.tensor_tensor(p.degree[:, :], ends[:, :], starts[:, :], ALU.subtract)
            e.drain()
            e.tensor_tensor(p.degree[:, :], p.degree[:, :], p.real[:, :], ALU.mult)
            e.tensor_scalar(count[:, :], ends[:, :], -1.0, 0.0, ALU.add, ALU.max)
            e.drain()
            e.tensor_scalar(p.live[:, :], p.degree[:, :], 0.0, None, ALU.is_gt)
            e.wait_ge(s_rowst, 16)
            e.tensor_copy(row_u[:, :], count[:, :])
            e.drain()
            e.tensor_scalar(start_f[:, :], p.live[:, :], -1.0, -SKIPPED, ALU.add, ALU.mult)
            e.tensor_tensor(starts[:, :], starts[:, :], p.live[:, :], ALU.mult)
            e.drain()
            e.tensor_tensor(start_f[:, :], start_f[:, :], starts[:, :], ALU.add)
            e.drain()
            e.tensor_copy(start_u[:, :], start_f[:, :]).then_inc(s_index, 1)
            e.wait_ge(s_lim, 1)
            e.tensor_copy(fix_lim[:, :], lim_i[:, :])
            e.tensor_reduce(chained[:, :], p.chain[:, :], AX.X, ALU.max)
            e.wait_ge(s_fix, 16)
            e.drain()
            e.tensor_tensor(fix_ok[:, :], fix_f[:, :], fix_lim[:, :], ALU.is_le)
            e.drain()
            e.tensor_scalar(fix_lim[:, :], fix_f[:, :], -1.0, 0.0, ALU.add, ALU.max)
            e.drain()
            e.tensor_tensor(fix_ok[:, :], fix_ok[:, :], chained[:, :], ALU.mult)
            e.tensor_copy(p.fix_from[:, :], fix_lim[:, :])
            e.drain()
            e.tensor_tensor(fix_lim[:, :], fix_lim[:, :], fix_ok[:, :], ALU.mult)
            e.tensor_scalar(fix_ok[:, :], fix_ok[:, :], -1.0, -SKIPPED, ALU.add, ALU.mult)
            e.drain()
            e.tensor_tensor(fix_f[:, :], fix_lim[:, :], fix_ok[:, :], ALU.add)
            e.drain()
            e.tensor_copy(p.fix_to[:, :], fix_f[:, :])

        @block.tensor
        def _(e):
            e.wait_ge(s_hps, 1)
            e.matmul(heads_ps[:, :], p.ones[0:1, :], heads_f[0:1, :], start=True, stop=True)\
                .then_inc(s_hps, 1)
            with e.Fori(0, p.groups) as i:
                e.wait_ge(s_xin, at(i, 1, 1))
                for t in range(G):
                    last = e.transpose(xt_ps[0:FD + 1, t // QUAD, t % QUAD, :], x_in[:, t, :],
                                       p.ident[:, :])
                last.then_inc(s_xps, 1)
                e.wait_ge(s_xt, at(i, 1, 1))
                for t in range(G):
                    last = e.matmul(proj_ps[:, t // 2, t % 2, :], x_t[:, t, :], p.w_nodes[:, :],
                                    start=True, stop=True)
                last.then_inc(s_proj, 1)

        @block.scalar
        def _(e):
            e.wait_ge(s_zero, 1)
            per = 2 * J * FD
            flat = p.k_edges.rearrange("(p j) f -> p (j f)", p=P)
            with e.Fori(0, p.chunks // 2) as i:
                e.dma_start(flat[:, bass.ds(i * per, per)], zeros[:, :]).then_inc(s_zero, 16)
            small = p.er_edges.rearrange("(p j) f -> p (j f)", p=P)
            e.dma_start(small, zeros[:, 0:2 * p.edges_pp]).then_inc(s_zero, 16)
            e.activation(x_in[:, :, FD:FD + 1], p.ones[:, 0:G].unsqueeze(2), ACT.Copy)
            with e.Fori(0, p.groups) as i:
                now = bass.ds(i * G, G)
                e.activation(x_in[:, :, 0:FD], p.x[:, now, :], ACT.Copy).then_inc(s_xin, 1)
                e.wait_ge(s_xps, at(i, 1, 1))
                e.activation(x_t[:, 0:QUAD, :], xt_ps[0:FD + 1, 0, :, :], ACT.Copy)
                e.activation(x_t[:, QUAD:G, :], xt_ps[0:FD + 1, 1, 0:G - QUAD, :], ACT.Copy)\
                    .then_inc(s_xt, 1)
                e.wait_ge(s_proj, at(i, 1, 1))
                for k in range(4):
                    n = min(2, G - 2 * k)
                    ts = slice(2 * k, 2 * k + n)
                    e.activation(qv_out[:, ts, :], proj_ps[:, k, 0:n, 0:2 * FD], ACT.Copy)
                    e.activation(k_out[:, ts, :], proj_ps[:, k, 0:n, 2 * FD:3 * FD], ACT.Copy)
                    skip = p.aux[:, bass.ds(i * G + 2 * k, n), :]
                    e.activation(skip, proj_ps[:, k, 0:n, 3 * FD:], ACT.Copy)
                e.drain().then_inc(s_out, 1)
                e.wait_ge(s_out, at(i, 1, 1))
                for table, tile in ((p.qv_table, qv_out), (p.k_table, k_out)):
                    e.dma_start(table.rearrange("(p t) f -> p t f", p=P)[:, now, :], tile[:, :, :])\
                        .then_inc(s_outst, 16)
                e.wait_ge(s_outst, at(i, 32, 32))
            e.wait_ge(s_zero, 1 + 16 * (p.chunks // 2) + 16)


def spread_phase(p, table, edges, width, tag):
    nc = p.nc
    with nc.reset_on_exit(), ExitStack() as ctx:
        sb = lambda n, s, d=F32: ctx.enter_context(nc.sbuf_tensor(f"{tag}_{n}", s, d))
        sem = lambda n: ctx.enter_context(nc.semaphore(f"{tag}_{n}"))
        index = [sb(f"ix{b}", [P, G], U32) for b in (0, 1)]
        rows = [sb(f"rows{b}", [P, G, width]) for b in (0, 1)]
        firsts = sb("firsts", [P, width])
        s_in = [sem(f"in{b}") for b in (0, 1)]
        s_sent = [sem(f"sent{b}") for b in (0, 1)]
        s_first = sem("first")
        s_passed = sem("passed")
        s_done = sem("done")
        block = ctx.enter_context(nc.Block())
        nodes = table.rearrange("(p t) f -> p t f", p=P)

        @block.sync
        def _(e):
            def load(b, now):
                e.dma_start(index[b][:, :], p.start_index[:, now]).then_inc(s_in[b], 16)
                e.dma_start(rows[b][:, :, :], nodes[:, now, :]).then_inc(s_in[b], 16)

            for b in (0, 1):
                load(b, slice(b * G, (b + 1) * G))
            with e.Fori(0, p.groups // 2 - 1) as i:
                for b in (0, 1):
                    hold(e, s_sent[b], at(i, 16 * G, 16 * G), s_passed)
                    load(b, bass.ds(i * (2 * G) + (2 + b) * G, G))

        @block.gpsimd
        def _(e):
            e.indirect_dma_start(firsts[:, :], None, table,
                                 bass.IndirectOffsetOnAxis(ap=p.first_index[:, 0:1], axis=0))\
                .then_inc(s_first, 16)
            with e.Fori(0, p.groups // 2) as i:
                for b in (0, 1):
                    hold(e, s_in[b], at(i, 32, 32), s_passed)
                    for t in range(G):
                        e.indirect_dma_start(edges, bass.IndirectOffsetOnAxis(ap=index[b][:, t:t + 1], axis=0),
                                             rows[b][:, t, :], None, bounds_check=p.n_edges - 1,
                                             oob_is_err=False).then_inc(s_sent[b], 16)
            for b in (0, 1):
                e.wait_ge(s_sent[b], 16 * G * (p.groups // 2))
            e.wait_ge(s_first, 16)
            e.dma_start(edges.rearrange("(p j) f -> p j f", p=P)[:, 0, :], firsts[:, :]).then_inc(s_done, 16)
            e.wait_ge(s_done, 16)


class EdgePhase:

    def __init__(self, p, layer, ctx, gather_from, gather_into):
        nc = p.nc
        self.p, self.k = p, layer
        self.heads, self.depth = p.shape[layer]
        self.width = p.width[layer]
        self.rounds = p.chunks // 2
        self.gather_from, self.gather_into = gather_from, gather_into
        tag = f"edge{layer}"
        self.sb = lambda n, s, d=F32: ctx.enter_context(nc.sbuf_tensor(f"{tag}_{n}", s, d))
        self.sem = lambda n: ctx.enter_context(nc.semaphore(f"{tag}_{n}"))
        self.index = [self.sb(f"ix{b}", [P, J], U32) for b in (0, 1)]
        self.val = [self.sb(f"val{b}", [P, J, self.width]) for b in (0, 1)]
        self.index_in = [self.sem(f"index_in{b}") for b in (0, 1)]
        self.attr_in = [self.sem(f"attr_in{b}") for b in (0, 1)]
        self.gathered = [self.sem(f"gathered{b}") for b in (0, 1)]
        self.rows_free = [self.sem(f"rows_free{b}") for b in (0, 1)]
        self.attr_free = [self.sem(f"attr_free{b}") for b in (0, 1)]
        self.ready = [self.sem(f"ready{b}") for b in (0, 1)]
        self.stored = [self.sem(f"stored{b}") for b in (0, 1)]
        self.val_free = [self.sem(f"val_free{b}") for b in (0, 1)]
        self.passed = self.sem("passed")
        self.src_now = self.p.ins["src"]
        h = self.heads
        if h:
            self.pen = self.sb("pen", [P, J])
            self.weight_arg = self.sb("weight_arg", [P, J, h])
            self.decay_arg = self.sb("decay_arg", [P, J, h])
            self.decay = self.sb("decay", [P, J, h])
            self.to_exp, self.from_exp = self.sem("to_exp"), self.sem("from_exp")
        self.same_now = self.sb("same_now", [P, J])

    def sync(self, e, attrs):
        p = self.p
        out = p.sums[self.k].rearrange("(p j) f -> p j f", p=P)

        def load(b, now):
            e.dma_start(self.index[b][:, :], self.src_now[:, now]).then_inc(self.index_in[b], 16)
            for tiles, of in attrs:
                e.dma_start(tiles[b], of[:, now, :]).then_inc(self.attr_in[b], 16)

        def store(b, now):
            e.dma_start(out[:, now, :], self.val[b][:, :, :]).then_inc(self.stored[b], 16)

        for b in (0, 1):
            e.sem_inc(self.val_free[b], 1)
            load(b, slice(b * J, (b + 1) * J))
        with e.Fori(0, self.rounds - 1) as i:
            for b in (0, 1):
                hold(e, self.rows_free[b], at(i, 1, 2), self.passed)
                if attrs:
                    hold(e, self.attr_free[b], at(i, 1, 1), self.passed)
                load(b, bass.ds(i * (2 * J) + (2 + b) * J, J))
                hold(e, self.ready[b], at(i, 1, 1), self.passed)
                store(b, rows_of(i, b, J))
                e.wait_ge(self.stored[b], at(i, 16, 16))
                e.sem_inc(self.val_free[b], 1)
        for b in (0, 1):
            e.wait_ge(self.ready[b], self.rounds)
            store(b, slice((2 * self.rounds - 2 + b) * J, (2 * self.rounds - 1 + b) * J))
        for b in (0, 1):
            e.wait_ge(self.stored[b], 16 * self.rounds)

    def gpsimd(self, e):
        for b in (0, 1):
            e.sem_inc(self.rows_free[b], 1)
        with e.Fori(0, self.rounds) as i:
            for b in (0, 1):
                e.wait_ge(self.index_in[b], at(i, 16, 16))
                hold(e, self.rows_free[b], at(i, 1, 1), self.passed)
                for j in range(J):
                    e.indirect_dma_start(self.gather_into(b, j), None, self.gather_from,
                                         bass.IndirectOffsetOnAxis(ap=self.index[b][:, j:j + 1], axis=0))\
                        .then_inc(self.gathered[b], 16)

    def wait_gathered(self, e, i, b):
        e.wait_ge(self.gathered[b], at(i, 16 * J, 16 * J))

    def wait_attrs(self, e, i, b, n):
        e.wait_ge(self.attr_in[b], at(i, 16 * n, 16 * n))

    def wait_val_free(self, e, i, b):
        e.wait_ge(self.val_free[b], at(i, 1, 1))

    def clear_carries(self, e):
        e.memset(self.p.carry[:, :], 0.0)
        e.memset(self.p.peak[:, 0, :], FAR)
        e.drain()

    def segment_flags(self, e, i, b):
        now = rows_of(i, b, J)
        if self.heads:
            e.tensor_scalar(self.pen[:, :], self.p.same[:, now], -1.0, -FAR, ALU.add, ALU.mult)
        e.tensor_copy(self.same_now[:, :], self.p.same[:, now])
        e.drain()

    def running_softmax(self, e, i, b, score):
        h, peak = self.heads, self.p.peak
        for n in range(h):
            e.tensor_tensor_scan(out=peak[:, 1:, n], data0=self.pen[:, :], data1=score[:, :, n],
                                 initial=peak[:, 0, n:n + 1], op0=ALU.add, op1=ALU.max)
        e.drain()
        e.tensor_tensor(self.weight_arg[:, :, :], score[:, :, :], peak[:, 1:, 0:h], ALU.subtract)
        e.tensor_tensor(self.decay_arg[:, :, :], peak[:, 0:J, 0:h], bcast(self.pen[:, :], 2, h), ALU.add)
        e.drain()
        e.tensor_tensor(self.decay_arg[:, :, :], self.decay_arg[:, :, :], peak[:, 1:, 0:h], ALU.subtract)\
            .then_inc(self.to_exp, 1)
        at_row = h * (self.depth + 1)
        e.tensor_copy(self.val[b][:, :, at_row:at_row + h], peak[:, 1:, 0:h])

    def weights(self, b):
        h, d = self.heads, self.depth
        return self.val[b][:, :, 0:h * (d + 1)].rearrange("p j (h d) -> p j h d", h=h)[:, :, :, d]

    def values(self, b):
        h, d = self.heads, self.depth
        return self.val[b][:, :, 0:h * (d + 1)].rearrange("p j (h d) -> p j h d", h=h)[:, :, :, 0:d]

    def exponentials(self, e, i, b):
        e.wait_ge(self.to_exp, at(i, 2, 1 + b))
        e.activation(self.weights(b), self.weight_arg[:, :, :], ACT.Exp)
        e.activation(self.decay[:, :, :], self.decay_arg[:, :, :], ACT.Exp).then_inc(self.from_exp, 1)

    def wait_weights(self, e, i, b):
        e.wait_ge(self.from_exp, at(i, 2, 1 + b))

    def scan_sums(self, e, b):
        h, d = self.heads, self.depth
        val, carry = self.val[b], self.p.carry
        n = h * (d + 1) if h else d
        for f in range(n):
            keep = self.decay[:, :, f // (d + 1)] if h else self.same_now[:, :]
            e.tensor_tensor_scan(out=val[:, :, f], data0=keep, data1=val[:, :, f],
                                 initial=carry[:, f:f + 1], op0=ALU.mult, op1=ALU.add)
        e.drain()
        e.tensor_copy(carry[:, 0:n], val[:, J - 1, 0:n])
        if h:
            e.tensor_copy(self.p.peak[:, 0, 0:h], self.p.peak[:, J, 0:h])
        e.drain().then_inc(self.ready[b], 1)


def edge_phase_0(p):
    nc = p.nc
    with nc.reset_on_exit(), ExitStack() as ctx:
        tiles = [ctx.enter_context(nc.sbuf_tensor(f"qv{b}", [P, J, 2 * FD], F32)) for b in (0, 1)]
        ph = EdgePhase(p, 0, ctx, p.qv_table, lambda b, j: tiles[b][:, j, :])
        k = [ph.sb(f"k{b}", [P, J, FD]) for b in (0, 1)]
        k_carry = ph.sb("k_carry", [P, FD])
        score = ph.sb("score", [P, J, 4])
        block = ctx.enter_context(nc.Block())
        k_edges = p.k_edges.rearrange("(p j) f -> p j f", p=P)

        @block.sync
        def _(e):
            ph.sync(e, [([k[0][:, :, :], k[1][:, :, :]], k_edges)])

        @block.gpsimd
        def _(e):
            ph.gpsimd(e)

        @block.vector
        def _(e):
            e.memset(k_carry[:, :], 0.0)
            ph.clear_carries(e)
            with e.Fori(0, ph.rounds) as i:
                for b in (0, 1):
                    ph.segment_flags(e, i, b)
                    ph.wait_attrs(e, i, b, 1)
                    for f in range(FD):
                        e.tensor_tensor_scan(out=k[b][:, :, f], data0=ph.same_now[:, :], data1=k[b][:, :, f],
                                             initial=k_carry[:, f:f + 1], op0=ALU.mult, op1=ALU.add)
                    e.drain()
                    e.tensor_copy(k_carry[:, :], k[b][:, J - 1, :])
                    e.drain()
                    ph.wait_gathered(e, i, b)
                    e.tensor_tensor(k[b][:, :, :], k[b][:, :, :], tiles[b][:, :, 0:FD], ALU.mult)
                    e.drain()
                    e.tensor_reduce(score[:, :, :], k[b][:, :, :].rearrange("p j (h d) -> p j h d", h=4),
                                    AX.X, ALU.add)
                    e.drain().then_inc(ph.attr_free[b], 1)
                    e.tensor_scalar(score[:, :, :], score[:, :, :], 0.25, None, ALU.mult)
                    e.drain()
                    ph.wait_val_free(e, i, b)
                    ph.running_softmax(e, i, b, score)
                    ph.wait_weights(e, i, b)
                    e.tensor_tensor(ph.values(b), tiles[b][:, :, FD:].rearrange("p j (h d) -> p j h d", h=4),
                                    bcast(ph.weights(b), 3, 16), ALU.mult)
                    e.drain().then_inc(ph.rows_free[b], 1)
                    ph.scan_sums(e, b)

        @block.scalar
        def _(e):
            with e.Fori(0, ph.rounds) as i:
                for b in (0, 1):
                    ph.exponentials(e, i, b)


def edge_phase_1(p):
    nc = p.nc
    with nc.reset_on_exit(), ExitStack() as ctx:
        g = [ctx.enter_context(nc.sbuf_tensor(f"g{b}", [P, J, FD], F32)) for b in (0, 1)]
        ph = EdgePhase(p, 1, ctx, p.x_tables[0], lambda b, j: g[b][:, j, :])
        bond = [ph.sb(f"bond{b}", [P, J, FD]) for b in (0, 1)]
        product = ph.sb("product", [P, J, 2, FD])
        score = ph.sb("score", [P, J, 2])
        er = ph.sb("er", [P, p.edges_pp, 2])
        er_in = ph.sem("er_in")
        block = ctx.enter_context(nc.Block())

        @block.sync
        def _(e):
            e.dma_start(er[:, :, :], p.er_edges.rearrange("(p j) f -> p j f", p=P)).then_inc(er_in, 16)
            ph.sync(e, [([bond[0][:, :, :], bond[1][:, :, :]], p.ins["edge_attr_64"])])

        @block.gpsimd
        def _(e):
            ph.gpsimd(e)

        @block.vector
        def _(e):
            ph.clear_carries(e)
            e.wait_ge(er_in, 16)
            for n in range(2):
                e.tensor_tensor_scan(out=er[:, :, n], data0=p.same[:, :], data1=er[:, :, n], initial=0.0,
                                     op0=ALU.mult, op1=ALU.add)
            e.drain()
            with e.Fori(0, ph.rounds) as i:
                for b in (0, 1):
                    ph.segment_flags(e, i, b)
                    ph.wait_attrs(e, i, b, 1)
                    ph.wait_gathered(e, i, b)
                    e.tensor_tensor(g[b][:, :, :], g[b][:, :, :], bond[b][:, :, :], ALU.add)
                    e.drain().then_inc(ph.attr_free[b], 1)
                    e.tensor_tensor(product[:, :, :, :], bcast(g[b][:, :, :], 2, 2),
                                    bcast(p.attn_l[:, :, :], 1, J), ALU.mult)
                    e.drain()
                    e.tensor_reduce(score[:, :, :], product[:, :, :, :], AX.X, ALU.add)
                    e.drain()
                    e.tensor_tensor(score[:, :, :], score[:, :, :], er[:, rows_of(i, b, J), :], ALU.add)
                    e.drain()
                    e.scalar_tensor_tensor(score[:, :, :], score[:, :, :], 0.2, score[:, :, :],
                                           ALU.mult, ALU.max)
                    e.drain()
                    ph.wait_val_free(e, i, b)
                    ph.running_softmax(e, i, b, score)
                    ph.wait_weights(e, i, b)
                    e.tensor_tensor(ph.values(b), bcast(g[b][:, :, :], 2, 2),
                                    bcast(ph.weights(b), 3, FD), ALU.mult)
                    e.drain().then_inc(ph.rows_free[b], 1)
                    ph.scan_sums(e, b)

        @block.scalar
        def _(e):
            with e.Fori(0, ph.rounds) as i:
                for b in (0, 1):
                    ph.exponentials(e, i, b)


def edge_phase_2(p):
    nc = p.nc
    quads = J // QUAD
    per = 2 * quads
    with nc.reset_on_exit(), ExitStack() as ctx:
        se = [ctx.enter_context(nc.sbuf_tensor(f"se{b}", [P, J, P], F32)) for b in (0, 1)]
        ph = EdgePhase(p, 2, ctx, p.x_tables[1], lambda b, j: se[b][:, j, 0:FD])
        eh = [ph.sb(f"eh{b}", [P, J, FD]) for b in (0, 1)]
        qr = [ph.sb(f"qr{b}", [P, J, FD]) for b in (0, 1)]
        qe = [ph.sb(f"qe{b}", [P, J, FD]) for b in (0, 1)]
        se_t = [ph.sb(f"se_t{u}", [P, QUAD, P]) for u in (0, 1)]
        q_t = [ph.sb(f"q_t{u}", [P, QUAD, P]) for u in (0, 1)]
        q_now = [ph.sb(f"q_now{u}", [P, QUAD, FD]) for u in (0, 1)]
        product = ph.sb("product", [P, J, FD])
        score = ph.sb("score", [P, J, 1])
        ps = lambda n: ctx.enter_context(nc.psum_tensor(n, [P, QUAD, P], F32))
        se_ps = [ps(f"se_ps{u}") for u in (0, 1)]
        q_ps = [ps(f"q_ps{u}") for u in (0, 1)]
        mk_ps = [ps(f"mk_ps{u}") for u in (0, 1)]
        qo_ps = [ps(f"qo_ps{u}") for u in (0, 1)]
        joined = ph.sem("joined")
        turned = ph.sem("turned")
        moved = ph.sem("moved")
        multiplied = ph.sem("multiplied")
        taken = ph.sem("taken")
        scored = ph.sem("scored")
        msg_in = ph.sem("msg_in")
        block = ctx.enter_context(nc.Block())

        @block.sync
        def _(e):
            attr = lambda tiles, name: ([t[:, :, :] for t in tiles], p.ins[name])
            ph.sync(e, [attr(eh, "edge_attr_64"), attr(qr, "edge_attr_64_n2"), attr(qe, "edge_attr_64_n3")])

        @block.gpsimd
        def _(e):
            ph.gpsimd(e)

        @block.tensor
        def _(e):
            e.sem_inc(multiplied, 2)

            def turn(i, b, c):
                n = b * quads + c
                u = n % 2
                e.wait_ge(moved, at(i, per, n + 1))
                for j in range(QUAD):
                    e.transpose(se_ps[u][:, j, :], se[b][:, QUAD * c + j, :], p.ident[:, :])
                for s, tile in enumerate((qr, qe)):
                    for half in range(2):
                        j = QUAD * c + 2 * half
                        last = e.transpose(q_ps[u][:, 2 * s + half, :],
                                           tile[b][:, j:j + 2, :].rearrange("p a f -> p (a f)"), p.ident[:, :])
                last.then_inc(turned, 1)
                if c == quads - 1:
                    e.drain().then_inc(ph.rows_free[b], 1)
                    e.drain().then_inc(ph.attr_free[b], 1)

            def multiply(i, b, c):
                n = b * quads + c
                u = n % 2
                e.wait_ge(moved, at(i, per, n + 3))
                e.wait_ge(taken, at(i, per, n + 1))
                e.wait_ge(scored, at(i, per, n + 1))
                for j in range(QUAD):
                    e.matmul(mk_ps[u][:, j, :], se_t[u][:, j, :], p.w2_mk[:, :], start=True, stop=True)
                for half in range(2):
                    e.matmul(qo_ps[u][:, half, :], q_t[u][:, half, :], p.w2_qr[:, :], start=True, stop=False)
                    last = e.matmul(qo_ps[u][:, half, :], q_t[u][:, 2 + half, :], p.w2_qe[:, :],
                                    start=False, stop=True)
                last.then_inc(multiplied, 1)

            with e.Fori(0, ph.rounds) as i:
                for b in (0, 1):
                    ph.wait_gathered(e, i, b)
                    ph.wait_attrs(e, i, b, 3)
                    e.wait_ge(joined, at(i, 2, b + 1))
                    turn(i, b, 0)
                    for c in range(quads):
                        if c + 1 < quads:
                            turn(i, b, c + 1)
                        multiply(i, b, c)

        @block.scalar
        def _(e):
            e.sem_inc(moved, 2)
            e.sem_inc(taken, 2)

            def move(i, b, c):
                n = b * quads + c
                u = n % 2
                e.wait_ge(turned, at(i, per, n + 1))
                e.wait_ge(multiplied, at(i, per, n + 1))
                e.activation(se_t[u][:, :, :], se_ps[u][:, :, :], ACT.Copy)
                e.activation(q_t[u][:, :, :], q_ps[u][:, :, :], ACT.Copy).then_inc(moved, 1)

            def take(i, b, c):
                n = b * quads + c
                u = n % 2
                e.wait_ge(multiplied, at(i, per, n + 3))
                e.wait_ge(scored, at(i, per, n + 1))
                e.activation(q_now[u][:, :, :], qo_ps[u][:, 0:2, :].rearrange("p a (c f) -> p (a c) f", c=2),
                             ACT.Copy)
                e.activation(ph.val[b][:, QUAD * c:QUAD * (c + 1), 0:FD], mk_ps[u][:, :, 0:FD], ACT.Copy)\
                    .then_inc(taken, 1)

            with e.Fori(0, ph.rounds) as i:
                for b in (0, 1):
                    e.wait_ge(ph.rows_free[b], at(i, 1, 1))
                    ph.wait_attrs(e, i, b, 3)
                    e.activation(se[b][:, :, FD:], eh[b][:, :, :], ACT.Copy).then_inc(joined, 1)
                    ph.wait_val_free(e, i, b)
                    move(i, b, 0)
                    for c in range(quads):
                        if c + 1 < quads:
                            move(i, b, c + 1)
                        take(i, b, c)
                    e.drain().then_inc(msg_in, 1)
                    ph.exponentials(e, i, b)

        @block.vector
        def _(e):
            e.sem_inc(scored, 2)
            ph.clear_carries(e)
            with e.Fori(0, ph.rounds) as i:
                for b in (0, 1):
                    ph.segment_flags(e, i, b)
                    for c in range(quads):
                        n = b * quads + c
                        u = n % 2
                        e.wait_ge(taken, at(i, per, n + 3))
                        e.tensor_tensor(product[:, QUAD * c:QUAD * (c + 1), :], mk_ps[u][:, :, FD:],
                                        q_now[u][:, :, :], ALU.mult).then_inc(scored, 1)
                    e.drain()
                    e.tensor_reduce(score[:, :, :], product[:, :, :], AX.X, ALU.add)
                    e.drain()
                    e.tensor_scalar(score[:, :, :], score[:, :, :], 0.125, None, ALU.mult)
                    e.drain()
                    e.wait_ge(msg_in, at(i, 2, b + 1))
                    ph.running_softmax(e, i, b, score)
                    msg = ph.val[b][:, :, 0:FD]
                    e.scalar_tensor_tensor(msg, msg, 0.01, msg, ALU.mult, ALU.max)
                    e.drain()
                    ph.wait_weights(e, i, b)
                    e.tensor_tensor(msg, msg, ph.weights(b).to_broadcast([P, J, FD]), ALU.mult)
                    e.drain()
                    ph.scan_sums(e, b)


def edge_phase_3(p):
    nc = p.nc
    quads = J // QUAD
    per = 2 * quads
    K = 97
    with nc.reset_on_exit(), ExitStack() as ctx:
        comb = [ctx.enter_context(nc.sbuf_tensor(f"comb{b}", [P, J, K], F32)) for b in (0, 1)]
        ph = EdgePhase(p, 3, ctx, p.x_tables[2], lambda b, j: comb[b][:, j, 0:FD])
        ea = [ph.sb(f"ea{b}", [P, J, 32]) for b in (0, 1)]
        comb_t = [ph.sb(f"comb_t{u}", [K, QUAD, P]) for u in (0, 1)]
        ps = lambda n: ctx.enter_context(nc.psum_tensor(n, [P, QUAD, P], F32))
        t_ps = [ps(f"t_ps{u}") for u in (0, 1)]
        h_ps = [ps(f"h_ps{u}") for u in (0, 1)]
        joined = ph.sem("joined")
        turned = ph.sem("turned")
        moved = ph.sem("moved")
        multiplied = ph.sem("multiplied")
        taken = ph.sem("taken")
        block = ctx.enter_context(nc.Block())

        @block.sync
        def _(e):
            ph.sync(e, [([t[:, :, :] for t in ea], p.ins["edge_attr_32"])])

        @block.gpsimd
        def _(e):
            ph.gpsimd(e)

        @block.tensor
        def _(e):
            e.sem_inc(multiplied, 2)

            def turn(i, b, c):
                n = b * quads + c
                e.wait_ge(moved, at(i, per, n + 1))
                for j in range(QUAD):
                    last = e.transpose(t_ps[n % 2][0:K, j, :], comb[b][:, QUAD * c + j, :], p.ident[:, :])
                last.then_inc(turned, 1)
                if c == quads - 1:
                    e.drain().then_inc(ph.rows_free[b], 1)

            def multiply(i, b, c):
                n = b * quads + c
                e.wait_ge(moved, at(i, per, n + 3))
                e.wait_ge(taken, at(i, per, n + 1))
                for j in range(QUAD):
                    last = e.matmul(h_ps[n % 2][:, j, :], comb_t[n % 2][:, j, :], p.w3_hidden[:, :],
                                    start=True, stop=True)
                last.then_inc(multiplied, 1)

            with e.Fori(0, ph.rounds) as i:
                for b in (0, 1):
                    ph.wait_gathered(e, i, b)
                    e.wait_ge(joined, at(i, 2, b + 1))
                    turn(i, b, 0)
                    for c in range(quads):
                        if c + 1 < quads:
                            turn(i, b, c + 1)
                        multiply(i, b, c)

        @block.scalar
        def _(e):
            e.sem_inc(moved, 2)
            e.sem_inc(taken, 2)
            for b in (0, 1):
                e.activation(comb[b][:, :, K - 1:], p.ones[:, 0:J].unsqueeze(2), ACT.Copy)

            def move(i, b, c):
                n = b * quads + c
                e.wait_ge(turned, at(i, per, n + 1))
                e.wait_ge(multiplied, at(i, per, n + 1))
                e.activation(comb_t[n % 2][:, :, :], t_ps[n % 2][0:K, :, :], ACT.Copy).then_inc(moved, 1)

            def take(i, b, c):
                n = b * quads + c
                e.wait_ge(multiplied, at(i, per, n + 3))
                e.activation(ph.val[b][:, QUAD * c:QUAD * (c + 1), :], h_ps[n % 2][:, :, :], ACT.Relu)\
                    .then_inc(taken, 1)

            with e.Fori(0, ph.rounds) as i:
                for b in (0, 1):
                    e.wait_ge(ph.rows_free[b], at(i, 1, 1))
                    ph.wait_attrs(e, i, b, 1)
                    e.activation(comb[b][:, :, FD:K - 1], ea[b][:, :, :], ACT.Copy).then_inc(joined, 1)
                    e.drain().then_inc(ph.attr_free[b], 1)
                    ph.wait_val_free(e, i, b)
                    move(i, b, 0)
                    for c in range(quads):
                        if c + 1 < quads:
                            move(i, b, c + 1)
                        take(i, b, c)

        @block.vector
        def _(e):
            ph.clear_carries(e)
            with e.Fori(0, ph.rounds) as i:
                for b in (0, 1):
                    ph.segment_flags(e, i, b)
                    e.wait_ge(taken, at(i, per, (b + 1) * quads + 2))
                    ph.scan_sums(e, b)


def fix_phase(p, layer):
    nc = p.nc
    h, d = p.shape[layer]
    w = p.width[layer]
    with nc.reset_on_exit(), ExitStack() as ctx:
        sb = lambda n, s, dt=F32: ctx.enter_context(nc.sbuf_tensor(f"fix{layer}_{n}", s, dt))
        sem = lambda n: ctx.enter_context(nc.semaphore(f"fix{layer}_{n}"))
        row = sb("row", [P, w])
        n = max(h, 1)
        wide = sb("wide", [P, n, P])
        turned = sb("turned", [P, n, P])
        top = sb("top", [P, n])
        scale = sb("scale", [P, n])
        ps = ctx.enter_context(nc.psum_tensor(f"fix{layer}_ps", [P, n, P], F32))
        ps_t = ctx.enter_context(nc.psum_tensor(f"fix{layer}_ps_t", [P, n, P], F32))
        ps_s = ctx.enter_context(nc.psum_tensor(f"fix{layer}_ps_s", [P, 130], F32))
        got, ready, done, v2a, a2v = sem("got"), sem("ready"), sem("done"), sem("v2a"), sem("a2v")
        v2p, p2v = sem("v2p"), sem("p2v")
        block = ctx.enter_context(nc.Block())

        @block.gpsimd
        def _(e):
            e.indirect_dma_start(row[:, :], None, p.sums[layer],
                                 bass.IndirectOffsetOnAxis(ap=p.fix_from[:, 0:1], axis=0)).then_inc(got, 16)
            e.wait_ge(ready, 1)
            e.indirect_dma_start(p.sums[layer], bass.IndirectOffsetOnAxis(ap=p.fix_to[:, 0:1], axis=0),
                                 row[:, :], None, bounds_check=p.n_edges - 1, oob_is_err=False)\
                .then_inc(done, 16)
            e.wait_ge(done, 16)

        @block.vector
        def _(e):
            if h:
                e.tensor_copy(wide[:, :, :], bcast(p.peak[:, 0, 0:h], 2, P)).then_inc(v2p, 1)
                e.wait_ge(got, 16)
                e.wait_ge(p2v, 1)
                e.tensor_tensor(wide[:, :, :], ps[:, :, :], bcast(p.chain_pen[:, :], 1, h), ALU.add)
                e.drain()
                e.tensor_reduce(top[:, :], wide[:, :, :], AX.X, ALU.max)
                e.drain()
                e.tensor_tensor(top[:, :], top[:, :], row[:, h * (d + 1):], ALU.max)
                e.drain()
                e.tensor_tensor(wide[:, :, :], wide[:, :, :], bcast(top[:, :], 2, P), ALU.subtract)
                e.tensor_tensor(scale[:, :], row[:, h * (d + 1):], top[:, :], ALU.subtract).then_inc(v2a, 1)
                e.wait_ge(p2v, 2)
                e.tensor_copy(turned[:, :, :], ps_t[:, :, :]).then_inc(v2p, 1)
                e.wait_ge(p2v, 3)
                own = row[:, 0:h * (d + 1)].rearrange("p (h d) -> p h d", h=h)
                e.tensor_tensor(own, own, bcast(scale[:, :], 2, d + 1), ALU.mult)
                e.drain()
                e.tensor_tensor(row[:, 0:h * (d + 1)], row[:, 0:h * (d + 1)], ps_s[:, 0:h * (d + 1)], ALU.add)\
                    .then_inc(ready, 1)
            else:
                e.wait_ge(got, 16)
                e.wait_ge(p2v, 1)
                e.tensor_tensor(row[:, :], row[:, :], ps_s[:, 0:d], ALU.add).then_inc(ready, 1)

        @block.scalar
        def _(e):
            if h:
                e.wait_ge(v2a, 1)
                e.activation(wide[:, :, :], wide[:, :, :], ACT.Exp)
                e.activation(scale[:, :], scale[:, :], ACT.Exp).then_inc(a2v, 1)

        @block.tensor
        def _(e):
            if h:
                e.wait_ge(v2p, 1)
                for k in range(h):
                    last = e.matmul(ps[:, k, :], wide[:, k, :], p.ident[:, :], start=True, stop=True)
                last.then_inc(p2v, 1)
                e.wait_ge(a2v, 1)
                for k in range(h):
                    last = e.transpose(ps_t[:, k, :], wide[:, k, :], p.ident[:, :])
                last.then_inc(p2v, 1)
                e.wait_ge(v2p, 2)
                for k in range(h):
                    s = slice(k * (d + 1), (k + 1) * (d + 1))
                    last = e.matmul(ps_s[:, s], turned[:, k, :], p.carry[:, s], start=True, stop=True)
                last.then_inc(p2v, 1)
            else:
                e.matmul(ps_s[:, 0:d], p.chain_t[:, :], p.carry[:, 0:d], start=True, stop=True)\
                    .then_inc(p2v, 1)


class NodePhase:

    def __init__(self, p, layer, ctx):
        nc = p.nc
        self.p, self.layer = p, layer
        tag = f"node{layer}"
        self.sb = lambda n, s, d=F32: ctx.enter_context(nc.sbuf_tensor(f"{tag}_{n}", s, d))
        self.sem = lambda n: ctx.enter_context(nc.semaphore(f"{tag}_{n}"))
        self.rounds = p.groups // 2
        self.index = [self.sb(f"ix{b}", [P, G], U32) for b in (0, 1)]
        self.rows = [self.sb(f"rows{b}", [P, G, p.width[layer]]) for b in (0, 1)]
        self.index_in = [self.sem(f"index_in{b}") for b in (0, 1)]
        self.gathered = [self.sem(f"gathered{b}") for b in (0, 1)]
        self.rows_free = [self.sem(f"rows_free{b}") for b in (0, 1)]
        self.state = [self.sb(f"state{b}", [P, G, FD]) for b in (0, 1)]
        self.state_ready = [self.sem(f"state_ready{b}") for b in (0, 1)]
        self.state_out = [self.sem(f"state_out{b}") for b in (0, 1)]
        self.state_free = [self.sem(f"state_free{b}") for b in (0, 1)]
        self.passed = self.sem("passed")
        self.square = self.sb("square", [P, G, FD])
        self.mean = self.sb("mean", [P, G])
        self.var = self.sb("var", [P, G])
        self.to_root, self.from_root = self.sem("to_root"), self.sem("from_root")

    def sync(self, e, table, extra=()):
        p = self.p
        for b in (0, 1):
            e.sem_inc(self.state_free[b], 1)
            e.dma_start(self.index[b][:, :], p.end_index[:, b * G:(b + 1) * G]).then_inc(self.index_in[b], 16)
        out = None if table is None else table.rearrange("(p t) f -> p t f", p=P)

        def store(b, now):
            e.dma_start(out[:, now, :], self.state[b][:, :, :]).then_inc(self.state_out[b], 16)
            for tiles, to in extra:
                e.dma_start(to[:, now, :], tiles[b]).then_inc(self.state_out[b], 16)

        with e.Fori(0, self.rounds - 1) as i:
            for b in (0, 1):
                hold(e, self.rows_free[b], at(i, 1, 2), self.passed)
                e.dma_start(self.index[b][:, :], p.end_index[:, bass.ds(i * (2 * G) + (2 + b) * G, G)])\
                    .then_inc(self.index_in[b], 16)
                if out is not None:
                    hold(e, self.state_ready[b], at(i, 1, 1), self.passed)
                    store(b, rows_of(i, b, G))
                    stores = 16 * (1 + len(extra))
                    e.wait_ge(self.state_out[b], at(i, stores, stores))
                    e.sem_inc(self.state_free[b], 1)
        if out is not None:
            for b in (0, 1):
                e.wait_ge(self.state_ready[b], self.rounds)
                store(b, slice((2 * self.rounds - 2 + b) * G, (2 * self.rounds - 1 + b) * G))
            for b in (0, 1):
                e.wait_ge(self.state_out[b], 16 * (1 + len(extra)) * self.rounds)

    def gpsimd(self, e):
        for b in (0, 1):
            e.sem_inc(self.rows_free[b], 1)
        with e.Fori(0, self.rounds) as i:
            for b in (0, 1):
                e.wait_ge(self.index_in[b], at(i, 16, 16))
                hold(e, self.rows_free[b], at(i, 1, 1), self.passed)
                for t in range(G):
                    e.indirect_dma_start(self.rows[b][:, t, :], None, self.p.sums[self.layer],
                                         bass.IndirectOffsetOnAxis(ap=self.index[b][:, t:t + 1], axis=0))\
                        .then_inc(self.gathered[b], 16)

    def wait_gathered(self, e, i, b):
        e.wait_ge(self.gathered[b], at(i, 16 * G, 16 * G))

    def shares(self, e, i, b, share, heads, depth):
        den = self.rows[b][:, :, 0:heads * (depth + 1)].rearrange("p t (h d) -> p t h d", h=heads)[:, :, :, depth]
        e.reciprocal(share[:, :, :], den)
        e.drain()
        e.tensor_tensor(share[:, :, :], share[:, :, :],
                        bcast(self.p.live[:, rows_of(i, b, G)], 2, heads), ALU.mult)
        e.drain()

    def normalise(self, e, a, i, per, n, eps):
        normalise(e, a, self.square[:, :, :], self.mean[:, :], self.var[:, :], eps,
                  self.to_root, self.from_root, at(i, per, n))

    def roots(self, e, i, per, n):
        e.wait_ge(self.to_root, at(i, per, n))
        e.activation(self.var[:, :], self.var[:, :], ACT.Sqrt).then_inc(self.from_root, 1)


def normalise(e, a, square, mean, var, eps, to_root, from_root, count):
    e.tensor_reduce(mean, a, AX.X, ALU.add)
    e.drain()
    e.tensor_scalar(mean, mean, 1.0 / FD, None, ALU.mult)
    e.drain()
    e.tensor_tensor(a, a, bcast(mean, 2, FD), ALU.subtract)
    e.drain()
    e.tensor_tensor(square, a, a, ALU.mult)
    e.drain()
    e.tensor_reduce(var, square, AX.X, ALU.add)
    e.drain()
    e.tensor_scalar(var, var, 1.0 / FD, eps, ALU.mult, ALU.add).then_inc(to_root, 1)
    e.wait_ge(from_root, count)
    e.reciprocal(var, var)
    e.drain()
    e.tensor_tensor(a, a, bcast(var, 2, FD), ALU.mult)
    e.drain()


def node_phase_0(p):
    nc = p.nc
    with nc.reset_on_exit(), ExitStack() as ctx:
        ph = NodePhase(p, 0, ctx)
        share = ph.sb("share", [P, G, 4])
        agg = ph.sb("agg", [P, G, FD])
        diff = ph.sb("diff", [P, G, FD])
        gate = ph.sb("gate", [P, G])
        er = [ph.sb(f"er{b}", [P, G, 2]) for b in (0, 1)]
        to_exp, from_exp = ph.sem("to_exp"), ph.sem("from_exp")
        block = ctx.enter_context(nc.Block())

        @block.sync
        def _(e):
            ph.sync(e, p.x_tables[0],
                    [([er[0][:, :, :], er[1][:, :, :]], p.er_table.rearrange("(p t) f -> p t f", p=P))])

        @block.gpsimd
        def _(e):
            ph.gpsimd(e)

        @block.scalar
        def _(e):
            with e.Fori(0, ph.rounds) as i:
                for b in (0, 1):
                    e.wait_ge(to_exp, at(i, 2, 1 + b))
                    e.activation(gate[:, :], gate[:, :], ACT.Exp, bias=p.gate_bias[:, 0:1], scale=-1.0)\
                        .then_inc(from_exp, 1)
                    ph.roots(e, i, 4, 2 * b + 1)
                    ph.roots(e, i, 4, 2 * b + 2)

        @block.vector
        def _(e):
            with e.Fori(0, ph.rounds) as i:
                for b in (0, 1):
                    now = rows_of(i, b, G)
                    skip, state = p.aux[:, now, :], ph.state[b][:, :, :]
                    ph.wait_gathered(e, i, b)
                    ph.shares(e, i, b, share, 4, 16)
                    rows = ph.rows[b][:, :, 0:68].rearrange("p t (h d) -> p t h d", h=4)[:, :, :, 0:16]
                    e.tensor_tensor(agg[:, :, :].rearrange("p t (h d) -> p t h d", h=4), rows,
                                    bcast(share[:, :, :], 3, 16), ALU.mult)
                    e.drain().then_inc(ph.rows_free[b], 1)
                    e.tensor_tensor(ph.square[:, :, :], skip, bcast(p.gate_a[:, :], 1, G), ALU.mult)
                    e.tensor_tensor(diff[:, :, :], agg[:, :, :], bcast(p.gate_b[:, :], 1, G), ALU.mult)
                    e.drain()
                    e.tensor_tensor(ph.square[:, :, :], ph.square[:, :, :], diff[:, :, :], ALU.add)
                    e.drain()
                    e.tensor_reduce(gate[:, :], ph.square[:, :, :], AX.X, ALU.add)
                    e.drain().then_inc(to_exp, 1)
                    e.tensor_tensor(diff[:, :, :], skip, agg[:, :, :], ALU.subtract)
                    e.wait_ge(from_exp, at(i, 2, 1 + b))
                    e.tensor_scalar(gate[:, :], gate[:, :], 1.0, None, ALU.add)
                    e.drain()
                    e.reciprocal(gate[:, :], gate[:, :])
                    e.drain()
                    e.tensor_tensor(diff[:, :, :], diff[:, :, :], bcast(gate[:, :], 2, FD), ALU.mult)
                    e.drain()
                    e.tensor_tensor(agg[:, :, :], agg[:, :, :], diff[:, :, :], ALU.add)
                    e.drain()
                    ph.normalise(e, agg[:, :, :], i, 4, 2 * b + 1, 1e-5)
                    e.tensor_tensor(agg[:, :, :], agg[:, :, :], bcast(p.param["L0_gnn_ln_g"][:, :], 1, G), ALU.mult)
                    e.drain()
                    e.tensor_tensor(agg[:, :, :], agg[:, :, :], bcast(p.param["L0_gnn_ln_b"][:, :], 1, G), ALU.add)
                    e.drain()
                    e.tensor_scalar(diff[:, :, :], agg[:, :, :], 0.0, p.slope[:, 0:1], ALU.min, ALU.mult)
                    e.drain()
                    e.scalar_tensor_tensor(agg[:, :, :], agg[:, :, :], 0.0, diff[:, :, :], ALU.max, ALU.add)
                    e.drain()
                    e.wait_ge(ph.state_free[b], at(i, 1, 1))
                    e.tensor_tensor(state, p.x[:, now, :], agg[:, :, :], ALU.add)
                    e.drain()
                    ph.normalise(e, state, i, 4, 2 * b + 2, 1e-5)
                    e.tensor_copy(p.x[:, now, :], state)
                    for n in range(2):
                        e.tensor_tensor(diff[:, :, :], state, bcast(p.attn_r[:, n, :], 1, G), ALU.mult)
                        e.drain()
                        e.tensor_reduce(er[b][:, :, n], diff[:, :, :], AX.X, ALU.add)
                        e.drain()
                    e.drain().then_inc(ph.state_ready[b], 1)


def node_phase_1(p):
    nc = p.nc
    T = p.nodes_pp
    with nc.reset_on_exit(), ExitStack() as ctx:
        ph = NodePhase(p, 1, ctx)
        share = ph.sb("share", [P, G, 2])
        agg = ph.sb("agg", [P, G, 2, FD])
        agg_t = ph.sb("agg_t", [P, G, P])
        all_sq = ph.sb("all_sq", [P, T, FD])
        all_mean = ph.sb("all_mean", [P, T])
        all_var = ph.sb("all_var", [P, T])
        part = ph.sb("part", [P, FD])
        bn_mean = ph.sb("bn_mean", [P, FD])
        bn_rstd = ph.sb("bn_rstd", [P, FD])
        t_ps = ctx.enter_context(nc.psum_tensor("n1_t_ps", [P, 2, QUAD, P], F32))
        h_ps = ctx.enter_context(nc.psum_tensor("n1_h_ps", [P, G, FD], F32))
        sum_ps = ctx.enter_context(nc.psum_tensor("n1_sum_ps", [P, 512], F32))
        agg_in, turned, moved, multiplied = ph.sem("agg_in"), ph.sem("turned"), ph.sem("moved"), ph.sem("mult")
        v2p, p2v, out = ph.sem("v2p"), ph.sem("p2v"), ph.sem("out")
        block = ctx.enter_context(nc.Block())

        @block.sync
        def _(e):
            ph.sync(e, None)
            e.wait_ge(v2p, 3)
            e.dma_start(p.x_tables[1].rearrange("(p t) f -> p t f", p=P), p.x[:, :, :]).then_inc(out, 16)
            e.wait_ge(out, 16)

        @block.gpsimd
        def _(e):
            ph.gpsimd(e)

        @block.tensor
        def _(e):
            with e.Fori(0, p.groups) as i:
                e.wait_ge(agg_in, at(i, 1, 1))
                for t in range(G):
                    last = e.transpose(t_ps[:, t // QUAD, t % QUAD, :],
                                       agg[:, t, :, :].rearrange("p h f -> p (h f)"), p.ident[:, :])
                last.then_inc(turned, 1)
                e.wait_ge(moved, at(i, 1, 1))
                for t in range(G):
                    last = e.matmul(h_ps[:, t, :], agg_t[:, t, :], p.w1_heads[:, :], start=True, stop=True)
                last.then_inc(multiplied, 1)
            for k in range(2):
                e.wait_ge(v2p, k + 1)
                e.matmul(sum_ps[:, k * FD:(k + 1) * FD], p.ones[:, :], part[:, :], start=True, stop=True)\
                    .then_inc(p2v, 1)

        @block.scalar
        def _(e):
            with e.Fori(0, p.groups) as i:
                e.wait_ge(turned, at(i, 1, 1))
                e.activation(agg_t[:, 0:QUAD, :], t_ps[:, 0, :, :], ACT.Copy)
                e.activation(agg_t[:, QUAD:G, :], t_ps[:, 1, 0:G - QUAD, :], ACT.Copy).then_inc(moved, 1)
            e.wait_ge(ph.to_root, 1)
            e.activation(bn_rstd[:, :], bn_rstd[:, :], ACT.Sqrt).then_inc(ph.from_root, 1)
            e.wait_ge(ph.to_root, 2)
            e.activation(all_var[:, :], all_var[:, :], ACT.Sqrt).then_inc(ph.from_root, 1)

        @block.vector
        def _(e):
            with e.Fori(0, ph.rounds) as i:
                for b in (0, 1):
                    now = rows_of(i, b, G)
                    ph.wait_gathered(e, i, b)
                    ph.shares(e, i, b, share, 2, FD)
                    rows = ph.rows[b][:, :, 0:130].rearrange("p t (h d) -> p t h d", h=2)[:, :, :, 0:FD]
                    e.tensor_tensor(agg[:, :, :, :], rows, bcast(share[:, :, :], 3, FD), ALU.mult)
                    e.drain().then_inc(ph.rows_free[b], 1)
                    e.drain().then_inc(agg_in, 1)
                    e.wait_ge(multiplied, at(i, 2, 1 + b))
                    e.tensor_copy(p.aux[:, now, :], h_ps[:, :, :])
                    e.drain()
            h, gamma, beta = p.aux[:, :, :], p.param["L1_gnn_bn_gamma"], p.param["L1_gnn_bn_beta"]
            by_feature = lambda a: a.rearrange("p t f -> p f t")
            e.tensor_reduce(part[:, :], by_feature(h), AX.X, ALU.add)
            e.drain().then_inc(v2p, 1)
            e.wait_ge(p2v, 1)
            e.tensor_scalar(bn_mean[:, :], sum_ps[:, 0:FD], 1.0 / p.n_nodes, None, ALU.mult)
            e.drain()
            e.tensor_tensor(h, h, bcast(bn_mean[:, :], 1, T), ALU.subtract)
            e.drain()
            e.tensor_tensor(h, h, bcast(p.real[:, :], 2, FD), ALU.mult)
            e.drain()
            e.tensor_tensor(all_sq[:, :, :], h, h, ALU.mult)
            e.drain()
            e.tensor_reduce(part[:, :], by_feature(all_sq[:, :, :]), AX.X, ALU.add)
            e.drain().then_inc(v2p, 1)
            e.wait_ge(p2v, 2)
            e.tensor_scalar(bn_rstd[:, :], sum_ps[:, FD:2 * FD], 1.0 / p.n_nodes, 1e-5, ALU.mult, ALU.add)\
                .then_inc(ph.to_root, 1)
            e.wait_ge(ph.from_root, 1)
            e.reciprocal(bn_rstd[:, :], bn_rstd[:, :])
            e.drain()
            e.tensor_tensor(bn_rstd[:, :], bn_rstd[:, :], gamma[:, :], ALU.mult)
            e.drain()
            e.tensor_tensor(h, h, bcast(bn_rstd[:, :], 1, T), ALU.mult)
            e.drain()
            e.tensor_tensor(h, h, bcast(beta[:, :], 1, T), ALU.add)
            e.drain()
            x = p.x[:, :, :]
            e.tensor_scalar(h, h, 0.0, None, ALU.max)
            e.drain()
            e.tensor_tensor(x, x, h, ALU.add)
            e.drain()
            normalise(e, x, all_sq[:, :, :], all_mean[:, :], all_var[:, :], 1e-5, ph.to_root, ph.from_root, 2)
            e.drain().then_inc(v2p, 1)


def node_phase_2(p):
    nc = p.nc
    with nc.reset_on_exit(), ExitStack() as ctx:
        ph = NodePhase(p, 2, ctx)
        share = ph.sb("share", [P, G, 1])
        agg = ph.sb("agg", [P, G, FD])
        agg_t = ph.sb("agg_t", [FD, G, P])
        other = ph.sb("other", [P, G, FD])
        idle = ph.sb("idle", [P, G])
        t_ps = ctx.enter_context(nc.psum_tensor("n2_t_ps", [P, 2, QUAD, P], F32))
        h_ps = ctx.enter_context(nc.psum_tensor("n2_h_ps", [P, G, FD], F32))
        agg_in, turned, moved, multiplied = ph.sem("agg_in"), ph.sem("turned"), ph.sem("moved"), ph.sem("mult")
        block = ctx.enter_context(nc.Block())

        @block.sync
        def _(e):
            ph.sync(e, p.x_tables[2])

        @block.gpsimd
        def _(e):
            ph.gpsimd(e)

        @block.tensor
        def _(e):
            with e.Fori(0, p.groups) as i:
                hold(e, agg_in, at(i, 1, 1), ph.passed)
                for t in range(G):
                    last = e.transpose(t_ps[0:FD, t // QUAD, t % QUAD, :], agg[:, t, :], p.ident[:, :])
                last.then_inc(turned, 1)
                e.wait_ge(moved, at(i, 1, 1))
                for t in range(G):
                    last = e.matmul(h_ps[:, t, :], agg_t[:, t, :], p.w2_out[:, :], start=True, stop=True)
                last.then_inc(multiplied, 1)

        @block.scalar
        def _(e):
            with e.Fori(0, ph.rounds) as i:
                for b in (0, 1):
                    e.wait_ge(turned, at(i, 2, 1 + b))
                    e.activation(agg_t[:, 0:QUAD, :], t_ps[0:FD, 0, :, :], ACT.Copy)
                    e.activation(agg_t[:, QUAD:G, :], t_ps[0:FD, 1, 0:G - QUAD, :], ACT.Copy).then_inc(moved, 1)
                    ph.roots(e, i, 4, 2 * b + 1)
                    ph.roots(e, i, 4, 2 * b + 2)

        @block.vector
        def _(e):
            with e.Fori(0, ph.rounds) as i:
                for b in (0, 1):
                    now = rows_of(i, b, G)
                    state, x = ph.state[b][:, :, :], p.x[:, now, :]
                    ph.wait_gathered(e, i, b)
                    ph.shares(e, i, b, share, 1, FD)
                    e.tensor_tensor(agg[:, :, :], ph.rows[b][:, :, 0:FD], share[:, :, :].to_broadcast([P, G, FD]),
                                    ALU.mult)
                    e.drain().then_inc(ph.rows_free[b], 1)
                    e.drain().then_inc(agg_in, 1)
                    e.wait_ge(multiplied, at(i, 2, 1 + b))
                    e.tensor_copy(other[:, :, :], h_ps[:, :, :])
                    e.drain()
                    e.scalar_tensor_tensor(other[:, :, :], other[:, :, :], 0.01, other[:, :, :], ALU.mult, ALU.max)
                    e.drain()
                    e.tensor_tensor(other[:, :, :], other[:, :, :], x, ALU.add)
                    e.drain()
                    ph.normalise(e, other[:, :, :], i, 4, 2 * b + 1, 1e-6)
                    e.tensor_tensor(other[:, :, :], other[:, :, :], bcast(p.param["L2_gnn_gamma"][:, :], 1, G), ALU.mult)
                    e.drain()
                    e.tensor_tensor(other[:, :, :], other[:, :, :], bcast(p.param["L2_gnn_beta"][:, :], 1, G), ALU.add)
                    e.tensor_scalar(idle[:, :], p.live[:, now], -1.0, -1.0, ALU.add, ALU.mult)
                    e.drain()
                    e.tensor_tensor(other[:, :, :], other[:, :, :], bcast(p.live[:, now], 2, FD), ALU.mult)
                    e.wait_ge(ph.state_free[b], at(i, 1, 1))
                    e.tensor_tensor(state, x, bcast(idle[:, :], 2, FD), ALU.mult)
                    e.drain()
                    e.tensor_tensor(other[:, :, :], other[:, :, :], state, ALU.add)
                    e.drain()
                    e.tensor_tensor(state, other[:, :, :], x, ALU.add)
                    e.drain()
                    ph.normalise(e, state, i, 4, 2 * b + 2, 1e-5)
                    e.tensor_copy(x, state)
                    e.drain().then_inc(ph.state_ready[b], 1)


def node_phase_3(p):
    nc = p.nc
    with nc.reset_on_exit(), ExitStack() as ctx:
        ph = NodePhase(p, 3, ctx)
        inv = ph.sb("inv", [P, G])
        agg = ph.sb("agg", [P, G, P])
        wide_t = ph.sb("wide_t", [P, G, P])
        hidden = ph.sb("hidden", [P, G, FD])
        bias = ph.sb("bias", [P, FD])
        t_ps = ctx.enter_context(nc.psum_tensor("n3_t_ps", [P, 2, QUAD, P], F32))
        h_ps = ctx.enter_context(nc.psum_tensor("n3_h_ps", [P, G, FD], F32))
        v2p, turned, moved, multiplied = ph.sem("v2p"), ph.sem("turned"), ph.sem("moved"), ph.sem("mult")
        block = ctx.enter_context(nc.Block())
        out = p.out

        @block.sync
        def _(e):
            ph.sync(e, out)

        @block.gpsimd
        def _(e):
            ph.gpsimd(e)

        @block.tensor
        def _(e):
            with e.Fori(0, p.groups) as i:
                for k, (tile, w) in enumerate(((agg, p.w3_msg), (agg, p.w3_upd1), (hidden, p.w3_upd2))):
                    wide = w.shape[0]
                    hold(e, v2p, at(i, 3, k + 1), ph.passed)
                    for t in range(G):
                        last = e.transpose(t_ps[0:wide, t // QUAD, t % QUAD, :], tile[:, t, :], p.ident[:, :])
                    last.then_inc(turned, 1)
                    e.wait_ge(moved, at(i, 3, k + 1))
                    for t in range(G):
                        last = e.matmul(h_ps[:, t, :], wide_t[0:wide, t, :], w[:, :], start=True, stop=True)
                    last.then_inc(multiplied, 1)

        @block.scalar
        def _(e):
            with e.Fori(0, p.groups) as i:
                for k in range(3):
                    wide = P if k < 2 else FD
                    e.wait_ge(turned, at(i, 3, k + 1))
                    e.activation(wide_t[0:wide, 0:QUAD, :], t_ps[0:wide, 0, :, :], ACT.Copy)
                    e.activation(wide_t[0:wide, QUAD:G, :], t_ps[0:wide, 1, 0:G - QUAD, :], ACT.Copy)\
                        .then_inc(moved, 1)
                ph.roots(e, i, 1, 1)

        @block.vector
        def _(e):
            b2 = p.param["L3_gnn_msg_b2"]
            e.tensor_tensor(bias[:, :], b2[:, 0:FD], b2[:, FD:], ALU.add)
            with e.Fori(0, ph.rounds) as i:
                for b in (0, 1):
                    now = rows_of(i, b, G)
                    state, x = ph.state[b][:, :, :], p.x[:, now, :]
                    e.tensor_scalar(inv[:, :], p.degree[:, now], 1e-8, None, ALU.add)
                    e.drain()
                    e.reciprocal(inv[:, :], inv[:, :])
                    e.drain()
                    e.tensor_tensor(inv[:, :], inv[:, :], p.live[:, now], ALU.mult)
                    e.drain()
                    ph.wait_gathered(e, i, b)
                    e.tensor_tensor(agg[:, :, :], ph.rows[b][:, :, :], bcast(inv[:, :], 2, P), ALU.mult)
                    e.drain().then_inc(v2p, 1)
                    e.drain().then_inc(ph.rows_free[b], 1)
                    e.tensor_tensor(inv[:, :], inv[:, :], p.degree[:, now], ALU.mult)
                    e.drain()
                    e.tensor_tensor(hidden[:, :, :], bcast(inv[:, :], 2, FD), bcast(bias[:, :], 1, G), ALU.mult)
                    e.drain()
                    e.wait_ge(multiplied, at(i, 6, 3 * b + 1))
                    e.tensor_tensor(agg[:, :, FD:], h_ps[:, :, :], hidden[:, :, :], ALU.add)
                    e.tensor_copy(agg[:, :, 0:FD], x)
                    e.drain().then_inc(v2p, 1)
                    e.wait_ge(multiplied, at(i, 6, 3 * b + 2))
                    e.tensor_tensor(hidden[:, :, :], h_ps[:, :, :], bcast(p.param["L3_gnn_upd_b1"][:, :], 1, G), ALU.add)
                    e.drain()
                    e.tensor_scalar(hidden[:, :, :], hidden[:, :, :], 0.0, None, ALU.max)
                    e.drain().then_inc(v2p, 1)
                    e.wait_ge(ph.state_free[b], at(i, 1, 1))
                    e.tensor_tensor(state, x, bcast(p.param["L3_gnn_upd_b2"][:, :], 1, G), ALU.add)
                    e.drain()
                    e.wait_ge(multiplied, at(i, 6, 3 * b + 3))
                    e.tensor_tensor(state, h_ps[:, :, :], state, ALU.add)
                    e.drain()
                    normalise(e, state, ph.square[:, :, :], ph.mean[:, :], ph.var[:, :], 1e-5,
                              ph.to_root, ph.from_root, at(i, 2, b + 1))
                    e.drain().then_inc(ph.state_ready[b], 1)


def gnn_program(nc, ins, out, n_nodes):
    with ExitStack() as top:
        p = Program(nc, ins, out, n_nodes, top)
        setup_phase(p)
        search_phase(p)
        spread_phase(p, p.k_table, p.k_edges, FD, "spread_k")
        edge_phase_0(p)
        fix_phase(p, 0)
        node_phase_0(p)
        spread_phase(p, p.er_table, p.er_edges, 2, "spread_er")
        edge_phase_1(p)
        fix_phase(p, 1)
        node_phase_1(p)
        edge_phase_2(p)
        fix_phase(p, 2)
        node_phase_2(p)
        edge_phase_3(p)
        fix_phase(p, 3)
        node_phase_3(p)


def laid_out(inputs, edges_pp, nodes_pp, find):
    n_nodes, n_edges = inputs["x"].shape[0], inputs["src"].shape[0]
    arrays = {}
    for name, a in inputs.items():
        a = np.ascontiguousarray(a)
        if name == "x":
            full = np.zeros((P * nodes_pp, a.shape[1]), a.dtype)
            full[:n_nodes] = a
        elif name in ("src", "dst") or name.startswith("edge_attr"):
            full = np.full((P * edges_pp, *a.shape[1:]), n_nodes if name == "dst" else 0, a.dtype)
            full[:n_edges] = a
            if name == "dst":
                arrays["dst_table"] = full.reshape(find)
            full = full.reshape(P, edges_pp, *a.shape[1:])
        else:
            full = a.reshape(1) if a.ndim == 0 else a
        arrays[name] = full
    arrays["src"] = arrays["src"].view(np.uint32)
    return arrays


def kernel(**inputs):
    import concourse.bacc as bacc
    from concourse.bass_utils import run_bass_kernel_spmd

    n_nodes, n_edges = inputs["x"].shape[0], inputs["src"].shape[0]
    edges_pp = -(-n_edges // (P * 2 * J)) * 2 * J
    nodes_pp = -(-(n_nodes + 1) // (P * 2 * G)) * 2 * G
    rows = next(r for r in range(int((P * edges_pp) ** 0.5), 0, -1) if P * edges_pp % r == 0)
    arrays = laid_out(inputs, edges_pp, nodes_pp, (rows, P * edges_pp // rows))
    nc = bacc.Bacc("TRN2", target_bir_lowering=False, num_devices=1)
    aps = {name: nc.dram_tensor("in_" + name, a.shape, mybir.dt.from_np(a.dtype), kind="ExternalInput").ap()
           for name, a in arrays.items()}
    out = nc.dram_tensor("out_x", (P * nodes_pp, FD), F32, kind="ExternalOutput").ap()
    gnn_program(nc, aps, out, n_nodes)
    r = run_bass_kernel_spmd(nc, [{"in_" + name: a for name, a in arrays.items()}], core_ids=[0])
    return r.results[0]["out_x"][:n_nodes]
```

```python
from contextlib import ExitStack

import numpy as np

import concourse.bass as bass
from concourse import mybir

F32 = mybir.dt.float32
I32 = mybir.dt.int32
U32 = mybir.dt.uint32
ALU = mybir.AluOpType
ACT = mybir.ActivationFunctionType
AX = mybir.AxisListType

P = 128
J = 28
G = 7
QUAD = 4
FD = 64
FAR = -1.0e30
SKIPPED = 1.0e9
BC = ["L0_gnn_Wg", "L0_gnn_ln_g", "L0_gnn_ln_b", "L1_gnn_bn_gamma", "L1_gnn_bn_beta", "L2_gnn_gamma",
      "L2_gnn_beta", "L3_gnn_msg_b2", "L3_gnn_upd_b1", "L3_gnn_upd_b2"]


def at(i, per, k):
    return i * per + k


def hold(e, sem, value, passed):
    e.wait_ge(sem, value)
    e.sem_inc(passed, 1)


def rows_of(i, b, size):
    return bass.ds(i * (2 * size) + b * size, size)


def bcast(ap, axis, n):
    a = ap.unsqueeze(axis)
    shape = list(a.shape)
    shape[axis] = n
    return a.to_broadcast(shape)


class Program:

    def __init__(self, nc, ins, out, n_nodes, ctx):
        self.nc, self.ins, self.out, self.ctx = nc, ins, out, ctx
        self.n_nodes = n_nodes
        self.edges_pp = ins["src"].shape[1]
        self.nodes_pp = ins["x"].shape[0] // P
        self.n_edges = P * self.edges_pp
        self.n_rows = P * self.nodes_pp
        self.chunks = self.edges_pp // J
        self.groups = self.nodes_pp // G
        assert self.chunks % 2 == 0 and self.groups % 2 == 0 and J % QUAD == 0
        self.find_rows, self.find_cols = ins["dst_table"].shape

        def dram(name, shape, dt=F32):
            return nc.dram_tensor(name, shape, dt).ap()

        n, e = self.n_rows, self.n_edges
        self.qv_table = dram("qv_table", [n, 2 * FD])
        self.k_table = dram("k_table", [n, FD])
        self.k_edges = dram("k_edges", [e, FD])
        self.er_table = dram("er_table", [n, 2])
        self.er_edges = dram("er_edges", [e, 2])
        self.end_table = dram("end_table", [n + 1, 1])
        self.x_tables = [dram(f"x_table{k}", [n, FD]) for k in (1, 2, 3)]
        self.find_index = dram("find_index", [P, self.nodes_pp], U32)
        self.end_index = dram("end_index", [P, self.nodes_pp], U32)
        self.start_index = dram("start_index", [P, self.nodes_pp], U32)
        self.shape = [(4, 16), (2, 64), (1, 64), (0, 128)]
        self.width = [h * (d + 2) if h else d for h, d in self.shape]
        self.sums = [dram(f"sums{k}", [e, w]) for k, w in enumerate(self.width)]

        def keep(name, shape, dt=F32):
            return ctx.enter_context(nc.sbuf_tensor(name, shape, dt))

        self.x = keep("x_now", [P, self.nodes_pp, FD])
        self.aux = keep("aux_now", [P, self.nodes_pp, FD])
        self.same = keep("same", [P, self.edges_pp])
        self.node = keep("node_number", [P, self.nodes_pp])
        self.live = keep("live", [P, self.nodes_pp])
        self.real = keep("real", [P, self.nodes_pp])
        self.degree = keep("degree", [P, self.nodes_pp])
        self.x_share = keep("x_share", [P, self.nodes_pp])
        self.mean_share = keep("mean_share", [P, self.nodes_pp])
        self.bias_share = keep("bias_share", [P, self.nodes_pp])
        self.skip_gate = keep("skip_gate", [P, self.nodes_pp])
        self.msg_bias = keep("msg_bias", [P, FD])
        self.eps = keep("eps", [P, 2])
        self.ident = keep("ident", [P, P])
        self.ones = keep("ones", [P, P])
        self.chain = keep("chain", [P, P])
        self.chain_t = keep("chain_t", [P, P])
        self.chain_pen = keep("chain_pen", [P, P])
        self.first = keep("first_dst", [P, 1])
        self.first_index = keep("first_index", [P, 1], U32)
        self.first_end_index = keep("first_end_index", [P, 1], U32)
        self.fix_from = keep("fix_from", [P, 1], U32)
        self.fix_to = keep("fix_to", [P, 1], U32)
        self.carry = keep("carry", [P, 2 * 65])
        self.peak = keep("peak", [P, J + 1, 4])
        self.param = {}
        for name in BC:
            self.param[name] = keep("bc_" + name, [P, int(np.prod(ins[name].shape))])
        self.gate_bias = keep("gate_bias", [P, 1])
        self.slope = keep("prelu_slope", [P, 1])
        self.w_nodes = keep("w_nodes", [FD + 1, 4 * FD])
        self.gate_a = keep("gate_a", [P, FD])
        self.gate_b = keep("gate_b", [P, FD])
        self.w1 = keep("w1", [FD, 2 * FD])
        self.w1_heads = keep("w1_heads", [2 * FD, FD])
        self.attn_l = keep("attn_l", [P, 2, FD])
        self.attn_r = keep("attn_r", [FD, 2])
        self.w2_mk = keep("w2_mk", [P, P])
        self.w2_qr = keep("w2_qr", [P, P])
        self.w2_qe = keep("w2_qe", [P, P])
        self.w2_out = keep("w2_out", [FD, FD])
        self.w3_hidden = keep("w3_hidden", [97, P])
        self.w3_msg = keep("w3_msg", [P, FD])
        self.w3_upd1 = keep("w3_upd1", [P, FD])
        self.w3_upd2 = keep("w3_upd2", [FD, FD])


def setup_phase(p):
    nc, ins = p.nc, p.ins
    with nc.reset_on_exit(), ExitStack() as ctx:
        dst_i = ctx.enter_context(nc.sbuf_tensor("dst_i", [P, p.edges_pp], I32))
        dst_f = ctx.enter_context(nc.sbuf_tensor("dst_f", [P, p.edges_pp + 1], F32))
        node_i = ctx.enter_context(nc.sbuf_tensor("node_i", [P, p.nodes_pp], I32))
        before = ctx.enter_context(nc.sbuf_tensor("before", [P, P], F32))
        att_cols = ctx.enter_context(nc.sbuf_tensor("att_cols", [FD, 4], F32))
        att_wide = ctx.enter_context(nc.sbuf_tensor("att_wide", [FD, 4, P], F32))
        w1_t = ctx.enter_context(nc.sbuf_tensor("w1_t", [FD, 2, FD], F32))
        tail_wide = ctx.enter_context(nc.sbuf_tensor("tail_wide", [P, P], F32))
        ps_a = ctx.enter_context(nc.psum_tensor("setup_ps_a", [P, 4, P], F32))
        ps_b = ctx.enter_context(nc.psum_tensor("setup_ps_b", [P, 4, P], F32))
        loaded = ctx.enter_context(nc.semaphore("setup_loaded"))
        dst_in = ctx.enter_context(nc.semaphore("dst_in"))
        cleared = ctx.enter_context(nc.semaphore("w2_cleared"))
        pool_done = ctx.enter_context(nc.semaphore("setup_pool"))
        to_pe = ctx.enter_context(nc.semaphore("setup_to_pe"))
        from_pe = ctx.enter_context(nc.semaphore("setup_from_pe"))
        block = ctx.enter_context(nc.Block())
        loads = [0]

        @block.sync
        def _(e):
            def load(to, of):
                e.dma_start(to, of).then_inc(loaded, 16)
                loads[0] += 16

            e.dma_start(dst_i[:, :], ins["dst"]).then_inc(dst_in, 16)
            load(p.x[:, :, :], ins["x"].rearrange("(p t) f -> p t f", p=P))
            for k, name in enumerate("qvks"):
                load(p.w_nodes[0:FD, k * FD:(k + 1) * FD], ins[f"L0_gnn_W{name}"])
                load(p.w_nodes[FD:FD + 1, k * FD:(k + 1) * FD], ins[f"L0_gnn_b{name}"].unsqueeze(0))
            for name in BC:
                flat = ins[name]
                if len(flat.shape) == 2:
                    flat = flat.rearrange("a b -> (a b)")
                load(p.param[name][:, :], flat.partition_broadcast(P))
            load(p.gate_bias[:, :], ins["L0_gnn_bg"].partition_broadcast(P))
            load(p.slope[:, :], ins["L0_gnn_prelu_a"].partition_broadcast(P))
            load(p.w1[:, :], ins["L1_gnn_W"])
            for h in range(2):
                load(p.w1_heads[h * FD:(h + 1) * FD, :], ins["L1_gnn_W"][:, h * FD:(h + 1) * FD])
            with nc.allow_non_contiguous_dma(reason="four short columns"):
                for k, name in enumerate("lr"):
                    load(att_cols[:, 2 * k:2 * k + 2], ins[f"L1_gnn_attn_{name}"].rearrange("h d -> d h"))
            load(p.w2_mk[:, 0:FD], ins["L2_gnn_W_msg"])
            load(p.w2_mk[:, FD:P], ins["L2_gnn_W_k"])
            load(p.w2_out[:, :], ins["L2_gnn_W_out"])
            for k in range(2):
                load(p.w3_hidden[0:96, k * FD:(k + 1) * FD], ins["L3_gnn_msg_w1"][k, :, :])
                load(p.w3_hidden[96:97, k * FD:(k + 1) * FD], ins["L3_gnn_msg_b1"][k:k + 1, :])
                load(p.w3_msg[k * FD:(k + 1) * FD, :], ins["L3_gnn_msg_w2"][k, :, :])
            load(p.w3_upd1[:, :], ins["L3_gnn_upd_w1"])
            load(p.w3_upd2[:, :], ins["L3_gnn_upd_w2"])
            e.wait_ge(cleared, 1)
            for half in range(2):
                s = slice(half * FD, (half + 1) * FD)
                load(p.w2_qr[s, s], ins["L2_gnn_W_q"][0:FD, :])
                load(p.w2_qe[s, s], ins["L2_gnn_W_q"][FD:P, :])

        @block.gpsimd
        def _(e):
            e.memset(p.ident[:, :], 0.0)
            e.memset(p.ones[:, :], 1.0)
            e.memset(before[:, :], 1.0).then_inc(pool_done, 1)
            e.wait_ge(pool_done, 1)
            e.affine_select(out=p.ident[:, :], in_=p.ident[:, :], compare_op=ALU.not_equal, fill=1.0,
                            base=0, pattern=[[-1, P]], channel_multiplier=1)
            e.affine_select(out=before[:, :], in_=before[:, :], compare_op=ALU.is_gt, fill=0.0,
                            base=0, pattern=[[-1, P]], channel_multiplier=1)
            e.iota(node_i[:, :], pattern=[[1, p.nodes_pp]], base=0, channel_multiplier=p.nodes_pp)\
                .then_inc(pool_done, 1)

        @block.vector
        def _(e):
            e.memset(p.w2_qr[:, :], 0.0)
            e.memset(p.w2_qe[:, :], 0.0).then_inc(cleared, 1)
            e.memset(dst_f[:, 0:1], -1.0)
            e.wait_ge(dst_in, 16)
            e.tensor_copy(dst_f[:, 1:], dst_i[:, :])
            e.drain()
            e.tensor_tensor(p.same[:, :], dst_f[:, 1:], dst_f[:, 0:p.edges_pp], ALU.is_equal)
            e.tensor_copy(p.first[:, :], dst_f[:, 1:2])
            e.tensor_copy(p.first_index[:, :], dst_i[:, 0:1])
            e.tensor_scalar(p.first_end_index[:, :], dst_f[:, 1:2], 1.0, None, ALU.add)
            e.wait_ge(pool_done, 2)
            e.tensor_copy(p.node[:, :], node_i[:, :])
            e.tensor_copy(tail_wide[:, :], dst_f[:, p.edges_pp:].to_broadcast([P, P]))
            e.wait_ge(loaded, loads[0])
            e.tensor_copy(att_wide[:, :, :], bcast(att_cols[:, :], 2, P)).then_inc(to_pe, 1)
            wg = p.param["L0_gnn_Wg"]
            e.tensor_tensor(p.gate_a[:, :], wg[:, 0:FD], wg[:, 2 * FD:3 * FD], ALU.add)
            e.tensor_tensor(p.gate_b[:, :], wg[:, FD:2 * FD], wg[:, 2 * FD:3 * FD], ALU.subtract)
            e.tensor_scalar(p.gate_bias[:, :], p.gate_bias[:, :], -1.0, None, ALU.mult)
            e.tensor_scalar(p.w1_heads[:, :], p.w1_heads[:, :], 0.5, None, ALU.mult)
            e.wait_ge(from_pe, 1)
            e.tensor_scalar(p.chain[:, :], ps_a[:, 0, :], p.first[:, 0:1], None, ALU.is_equal)
            e.tensor_copy(w1_t[:, :, :], ps_a[0:FD, 1:3, 0:FD])
            e.drain()
            e.tensor_tensor(p.chain[:, :], p.chain[:, :], before[:, :], ALU.mult)
            e.drain().then_inc(to_pe, 1)
            e.tensor_scalar(p.chain_pen[:, :], p.chain[:, :], -1.0, -FAR, ALU.add, ALU.mult)
            e.wait_ge(from_pe, 2)
            e.tensor_copy(p.chain_t[:, :], ps_a[:, 3, :])
            e.tensor_copy(p.attn_l[:, :, :], ps_b[:, 0:2, 0:FD])
            e.tensor_copy(p.attn_r[:, :], ps_b[0:FD, 2, 0:2])
            e.memset(p.eps[:, 0:1], 1e-5)
            e.memset(p.eps[:, 1:2], 1e-6)
            b2 = p.param["L3_gnn_msg_b2"]
            e.tensor_tensor(p.msg_bias[:, :], b2[:, 0:FD], b2[:, FD:], ALU.add)

        @block.tensor
        def _(e):
            e.wait_ge(pool_done, 2)
            e.wait_ge(to_pe, 1)
            e.matmul(ps_a[:, 0, :], tail_wide[:, :], p.ident[:, :], start=True, stop=True)
            for h in range(2):
                ins_ = e.transpose(ps_a[0:FD, 1 + h, 0:FD], p.w1[:, h * FD:(h + 1) * FD],
                                   p.ident[0:FD, 0:FD])
            ins_.then_inc(from_pe, 1)
            e.wait_ge(to_pe, 2)
            e.transpose(ps_a[:, 3, :], p.chain[:, :], p.ident[:, :])
            for k in range(2):
                e.matmul(ps_b[:, k, 0:FD], att_wide[:, k, :], w1_t[:, k, :], start=True, stop=True)
            for k in range(2):
                ins_ = e.matmul(ps_b[0:FD, 2, k:k + 1], w1_t[:, k, :], att_cols[:, 2 + k:3 + k],
                                start=True, stop=True)
            ins_.then_inc(from_pe, 1)


def search_phase(p):
    nc = p.nc
    R1, W, T = p.find_rows, p.find_cols, p.nodes_pp
    rounds = p.groups // 2
    with nc.reset_on_exit(), ExitStack() as ctx:
        sb = lambda n, s, d=F32: ctx.enter_context(nc.sbuf_tensor(n, s, d))
        sem = lambda n: ctx.enter_context(nc.semaphore(n))
        heads_i = sb("heads_i", [1, R1], I32)
        heads_f = sb("heads_f", [1, R1])
        heads = sb("heads", [P, R1])
        compared = sb("compared", [P, G, max(R1, W)])
        row = sb("found_row", [P, T])
        row_u = sb("found_row_u", [P, T], U32)
        start_u = sb("start_u", [P, T], U32)
        count = sb("found_count", [P, T])
        ends = sb("ends", [P, T])
        starts = sb("starts", [P, T])
        start_f = sb("start_f", [P, T])
        picked = [sb(f"picked{b}", [P, G, W], I32) for b in (0, 1)]
        pick_ix = [sb(f"pick_ix{b}", [P, G], U32) for b in (0, 1)]
        zeros = sb("zeros", [P, 2 * J * FD])
        end_zero = sb("end_zero", [1, 1])
        fix_f = sb("fix_f", [P, 1])
        fix_lim = sb("fix_lim", [P, 1])
        fix_ok = sb("fix_ok", [P, 1])
        lim_i = sb("lim_i", [P, 1], I32)
        chained = sb("chained", [P, 1])
        x_in = sb("x_in", [P, G, FD + 1])
        x_t = sb("x_t", [FD + 1, G, P])
        qv_out = sb("qv_out", [P, G, 2 * FD])
        k_out = sb("k_out", [P, G, FD])
        heads_ps = ctx.enter_context(nc.psum_tensor("heads_ps", [P, R1], F32))
        xt_ps = ctx.enter_context(nc.psum_tensor("xt_ps", [P, 2, QUAD, P], F32))
        proj_ps = ctx.enter_context(nc.psum_tensor("proj_ps", [P, 4, 2, 4 * FD], F32))
        s_head = sem("s_head")
        s_hps = sem("s_hps")
        s_row = sem("s_row")
        s_rowst = sem("s_rowst")
        s_ix = [sem(f"s_ix{b}") for b in (0, 1)]
        s_got = [sem(f"s_got{b}") for b in (0, 1)]
        s_free = [sem(f"s_free{b}") for b in (0, 1)]
        s_end = sem("s_end")
        s_endst = sem("s_endst")
        s_start = sem("s_start")
        s_zero = sem("s_zero")
        s_cleared = sem("s_cleared")
        s_index = sem("s_index")
        s_indexst = sem("s_indexst")
        s_fix = sem("s_fix")
        s_lim = sem("s_lim")
        s_xin = sem("s_xin")
        s_xps = sem("s_xps")
        s_xt = sem("s_xt")
        s_proj = sem("s_proj")
        s_out = sem("s_out")
        s_outst = sem("s_outst")
        s_passed = sem("s_passed")
        block = ctx.enter_context(nc.Block())

        @block.sync
        def _(e):
            with nc.allow_non_contiguous_dma(reason="one element of every table row"):
                e.dma_start(heads_i[0:1, :], p.ins["dst_table"][:, 0:1].rearrange("r a -> a r"))\
                    .then_inc(s_head, 16)
            e.wait_ge(s_zero, 1)
            per = 2 * J * FD
            flat = p.k_edges.rearrange("(p j) f -> p (j f)", p=P)
            with e.Fori(0, p.chunks // 2) as i:
                e.dma_start(flat[:, bass.ds(i * per, per)], zeros[:, :]).then_inc(s_cleared, 16)
            e.dma_start(p.er_edges.rearrange("(p j) f -> p (j f)", p=P), zeros[:, 0:2 * p.edges_pp])\
                .then_inc(s_cleared, 16)
            e.wait_ge(s_row, 1)
            e.dma_start(p.find_index, row_u[:, :]).then_inc(s_rowst, 16)
            e.wait_ge(s_rowst, 16)
            with e.Fori(0, rounds) as i:
                for b in (0, 1):
                    hold(e, s_free[b], at(i, 1, 1), s_passed)
                    e.dma_start(pick_ix[b][:, :], p.find_index[:, rows_of(i, b, G)]).then_inc(s_ix[b], 16)
            e.wait_ge(s_end, 1)
            e.dma_start(p.end_table[0:1, :], end_zero[0:1, :]).then_inc(s_endst, 16)
            e.dma_start(p.end_table[1:, :].rearrange("(p t) a -> p (t a)", p=P), ends[:, :])\
                .then_inc(s_endst, 16)
            e.wait_ge(s_endst, 32)
            e.dma_start(starts[:, :], p.end_table[0:p.n_rows, :].rearrange("(p t) a -> p (t a)", p=P))\
                .then_inc(s_start, 16)
            e.wait_ge(s_index, 1)
            e.dma_start(p.end_index, row_u[:, :]).then_inc(s_indexst, 16)
            e.dma_start(p.start_index, start_u[:, :]).then_inc(s_indexst, 16)
            e.wait_ge(s_indexst, 32)
            e.wait_ge(s_cleared, 16 * (p.chunks // 2) + 16)

        @block.gpsimd
        def _(e):
            e.iota(lim_i[:, :], pattern=[[0, 1]], base=p.edges_pp, channel_multiplier=p.edges_pp)\
                .then_inc(s_lim, 1)
            with e.Fori(0, rounds) as i:
                for b in (0, 1):
                    hold(e, s_ix[b], at(i, 16, 16), s_passed)
                    for t in range(G):
                        e.indirect_dma_start(picked[b][:, t, :], None, p.ins["dst_table"],
                                             bass.IndirectOffsetOnAxis(ap=pick_ix[b][:, t:t + 1], axis=0))\
                            .then_inc(s_got[b], 16)
            e.wait_ge(s_endst, 32)
            e.indirect_dma_start(fix_f[:, :], None, p.end_table,
                                 bass.IndirectOffsetOnAxis(ap=p.first_end_index[:, 0:1], axis=0))\
                .then_inc(s_fix, 16)

        @block.vector
        def _(e):
            e.memset(end_zero[:, :], 0.0)
            e.memset(zeros[:, :], 0.0).then_inc(s_zero, 1)
            for b in (0, 1):
                e.drain().then_inc(s_free[b], 1)
            e.wait_ge(s_head, 16)
            e.tensor_copy(heads_f[:, :], heads_i[:, :]).then_inc(s_hps, 1)
            e.wait_ge(s_hps, 2)
            e.tensor_copy(heads[:, :], heads_ps[:, :])
            e.drain()
            with e.Fori(0, p.groups) as i:
                now = bass.ds(i * G, G)
                e.tensor_tensor(compared[:, :, 0:R1], bcast(heads[:, :], 1, G),
                                bcast(p.node[:, now], 2, R1), ALU.is_le)
                e.drain()
                e.tensor_reduce(row[:, now], compared[:, :, 0:R1], AX.X, ALU.add)
                e.drain()
            e.tensor_scalar(row[:, :], row[:, :], -1.0, 0.0, ALU.add, ALU.max)
            e.drain()
            e.tensor_copy(row_u[:, :], row[:, :]).then_inc(s_row, 1)
            with e.Fori(0, rounds) as i:
                for b in (0, 1):
                    now = rows_of(i, b, G)
                    e.wait_ge(s_got[b], at(i, 16 * G, 16 * G))
                    e.tensor_tensor(compared[:, :, 0:W], picked[b][:, :, :],
                                    bcast(p.node[:, now], 2, W), ALU.is_le)
                    e.drain().then_inc(s_free[b], 1)
                    e.tensor_reduce(count[:, now], compared[:, :, 0:W], AX.X, ALU.add)
                    e.drain()
            e.scalar_tensor_tensor(ends[:, :], row[:, :], float(W), count[:, :], ALU.mult, ALU.add)\
                .then_inc(s_end, 1)
            e.tensor_scalar(p.real[:, :], p.node[:, :], float(p.n_nodes), None, ALU.is_lt)
            e.wait_ge(s_start, 16)
            e.tensor_tensor(p.degree[:, :], ends[:, :], starts[:, :], ALU.subtract)
            e.drain()
            e.tensor_tensor(p.degree[:, :], p.degree[:, :], p.real[:, :], ALU.mult)
            e.tensor_scalar(count[:, :], ends[:, :], -1.0, 0.0, ALU.add, ALU.max)
            e.drain()
            e.tensor_scalar(p.live[:, :], p.degree[:, :], 0.0, None, ALU.is_gt)
            e.wait_ge(s_rowst, 16)
            e.tensor_copy(row_u[:, :], count[:, :])
            e.drain()
            e.tensor_scalar(start_f[:, :], p.live[:, :], -1.0, -SKIPPED, ALU.add, ALU.mult)
            e.tensor_tensor(starts[:, :], starts[:, :], p.live[:, :], ALU.mult)
            e.drain()
            e.tensor_tensor(start_f[:, :], start_f[:, :], starts[:, :], ALU.add)
            e.drain()
            e.tensor_copy(start_u[:, :], start_f[:, :]).then_inc(s_index, 1)
            e.tensor_scalar(p.x_share[:, :], p.live[:, :], -1.0, 2.0, ALU.mult, ALU.add)
            e.tensor_scalar(p.mean_share[:, :], p.degree[:, :], 1e-8, None, ALU.add)
            e.drain()
            e.reciprocal(p.mean_share[:, :], p.mean_share[:, :])
            e.drain()
            e.tensor_tensor(p.bias_share[:, :], p.mean_share[:, :], p.degree[:, :], ALU.mult)
            e.drain()
            e.tensor_tensor(p.mean_share[:, :], p.mean_share[:, :], p.live[:, :], ALU.mult)
            e.wait_ge(s_lim, 1)
            e.tensor_copy(fix_lim[:, :], lim_i[:, :])
            e.tensor_reduce(chained[:, :], p.chain[:, :], AX.X, ALU.max)
            e.wait_ge(s_fix, 16)
            e.drain()
            e.tensor_tensor(fix_ok[:, :], fix_f[:, :], fix_lim[:, :], ALU.is_le)
            e.drain()
            e.tensor_scalar(fix_lim[:, :], fix_f[:, :], -1.0, 0.0, ALU.add, ALU.max)
            e.drain()
            e.tensor_tensor(fix_ok[:, :], fix_ok[:, :], chained[:, :], ALU.mult)
            e.tensor_copy(p.fix_from[:, :], fix_lim[:, :])
            e.drain()
            e.tensor_tensor(fix_lim[:, :], fix_lim[:, :], fix_ok[:, :], ALU.mult)
            e.tensor_scalar(fix_ok[:, :], fix_ok[:, :], -1.0, -SKIPPED, ALU.add, ALU.mult)
            e.drain()
            e.tensor_tensor(fix_f[:, :], fix_lim[:, :], fix_ok[:, :], ALU.add)
            e.drain()
            e.tensor_copy(p.fix_to[:, :], fix_f[:, :])

        @block.tensor
        def _(e):
            e.wait_ge(s_hps, 1)
            e.matmul(heads_ps[:, :], p.ones[0:1, :], heads_f[0:1, :], start=True, stop=True)\
                .then_inc(s_hps, 1)
            with e.Fori(0, p.groups) as i:
                e.wait_ge(s_xin, at(i, 1, 1))
                for t in range(G):
                    last = e.transpose(xt_ps[0:FD + 1, t // QUAD, t % QUAD, :], x_in[:, t, :],
                                       p.ident[:, :])
                last.then_inc(s_xps, 1)
                e.wait_ge(s_xt, at(i, 1, 1))
                for t in range(G):
                    last = e.matmul(proj_ps[:, t // 2, t % 2, :], x_t[:, t, :], p.w_nodes[:, :],
                                    start=True, stop=True)
                last.then_inc(s_proj, 1)

        @block.scalar
        def _(e):
            e.activation(x_in[:, :, FD:FD + 1], p.ones[:, 0:G].unsqueeze(2), ACT.Copy)
            with e.Fori(0, p.groups) as i:
                now = bass.ds(i * G, G)
                e.activation(x_in[:, :, 0:FD], p.x[:, now, :], ACT.Copy).then_inc(s_xin, 1)
                e.wait_ge(s_xps, at(i, 1, 1))
                e.activation(x_t[:, 0:QUAD, :], xt_ps[0:FD + 1, 0, :, :], ACT.Copy)
                e.activation(x_t[:, QUAD:G, :], xt_ps[0:FD + 1, 1, 0:G - QUAD, :], ACT.Copy)\
                    .then_inc(s_xt, 1)
                e.wait_ge(s_proj, at(i, 1, 1))
                for k in range(4):
                    n = min(2, G - 2 * k)
                    ts = slice(2 * k, 2 * k + n)
                    e.activation(qv_out[:, ts, :], proj_ps[:, k, 0:n, 0:2 * FD], ACT.Copy)
                    e.activation(k_out[:, ts, :], proj_ps[:, k, 0:n, 2 * FD:3 * FD], ACT.Copy)
                    skip = p.aux[:, bass.ds(i * G + 2 * k, n), :]
                    e.activation(skip, proj_ps[:, k, 0:n, 3 * FD:], ACT.Copy)
                e.drain().then_inc(s_out, 1)
                e.wait_ge(s_out, at(i, 1, 1))
                for table, tile in ((p.qv_table, qv_out), (p.k_table, k_out)):
                    e.dma_start(table.rearrange("(p t) f -> p t f", p=P)[:, now, :], tile[:, :, :])\
                        .then_inc(s_outst, 16)
                e.wait_ge(s_outst, at(i, 32, 32))


def spread_phase(p, table, edges, width, tag):
    nc = p.nc
    with nc.reset_on_exit(), ExitStack() as ctx:
        sb = lambda n, s, d=F32: ctx.enter_context(nc.sbuf_tensor(f"{tag}_{n}", s, d))
        sem = lambda n: ctx.enter_context(nc.semaphore(f"{tag}_{n}"))
        index = [sb(f"ix{b}", [P, G], U32) for b in (0, 1)]
        rows = [sb(f"rows{b}", [P, G, width]) for b in (0, 1)]
        firsts = sb("firsts", [P, width])
        s_in = [sem(f"in{b}") for b in (0, 1)]
        s_sent = [sem(f"sent{b}") for b in (0, 1)]
        s_first = sem("first")
        s_passed = sem("passed")
        s_done = sem("done")
        block = ctx.enter_context(nc.Block())
        nodes = table.rearrange("(p t) f -> p t f", p=P)

        @block.sync
        def _(e):
            def load(b, now):
                e.dma_start(index[b][:, :], p.start_index[:, now]).then_inc(s_in[b], 16)
                e.dma_start(rows[b][:, :, :], nodes[:, now, :]).then_inc(s_in[b], 16)

            for b in (0, 1):
                load(b, slice(b * G, (b + 1) * G))
            with e.Fori(0, p.groups // 2 - 1) as i:
                for b in (0, 1):
                    hold(e, s_sent[b], at(i, 16 * G, 16 * G), s_passed)
                    load(b, bass.ds(i * (2 * G) + (2 + b) * G, G))

        @block.gpsimd
        def _(e):
            e.indirect_dma_start(firsts[:, :], None, table,
                                 bass.IndirectOffsetOnAxis(ap=p.first_index[:, 0:1], axis=0))\
                .then_inc(s_first, 16)
            with e.Fori(0, p.groups // 2) as i:
                for b in (0, 1):
                    hold(e, s_in[b], at(i, 32, 32), s_passed)
                    for t in range(G):
                        e.indirect_dma_start(edges, bass.IndirectOffsetOnAxis(ap=index[b][:, t:t + 1], axis=0),
                                             rows[b][:, t, :], None, bounds_check=p.n_edges - 1,
                                             oob_is_err=False).then_inc(s_sent[b], 16)
            for b in (0, 1):
                e.wait_ge(s_sent[b], 16 * G * (p.groups // 2))
            e.wait_ge(s_first, 16)
            e.dma_start(edges.rearrange("(p j) f -> p j f", p=P)[:, 0, :], firsts[:, :]).then_inc(s_done, 16)
            e.wait_ge(s_done, 16)


class EdgePhase:

    def __init__(self, p, layer, ctx, gather_from, gather_into):
        nc = p.nc
        self.p, self.k = p, layer
        self.heads, self.depth = p.shape[layer]
        self.width = p.width[layer]
        self.rounds = p.chunks // 2
        self.gather_from, self.gather_into = gather_from, gather_into
        tag = f"edge{layer}"
        self.sb = lambda n, s, d=F32: ctx.enter_context(nc.sbuf_tensor(f"{tag}_{n}", s, d))
        self.sem = lambda n: ctx.enter_context(nc.semaphore(f"{tag}_{n}"))
        self.index = [self.sb(f"ix{b}", [P, J], U32) for b in (0, 1)]
        self.sums = [self.sb(f"sums{b}", [P, J + 1, self.width]) for b in (0, 1)]
        self.val = [t[:, 1:, :] for t in self.sums]
        self.index_in = [self.sem(f"index_in{b}") for b in (0, 1)]
        self.attr_in = [self.sem(f"attr_in{b}") for b in (0, 1)]
        self.gathered = [self.sem(f"gathered{b}") for b in (0, 1)]
        self.rows_free = [self.sem(f"rows_free{b}") for b in (0, 1)]
        self.attr_free = [self.sem(f"attr_free{b}") for b in (0, 1)]
        self.ready = [self.sem(f"ready{b}") for b in (0, 1)]
        self.stored = [self.sem(f"stored{b}") for b in (0, 1)]
        self.val_free = [self.sem(f"val_free{b}") for b in (0, 1)]
        self.passed = self.sem("passed")
        self.src_now = self.p.ins["src"]
        h = self.heads
        if h:
            self.pen = self.sb("pen", [P, J])
            self.weight_arg = self.sb("weight_arg", [P, J, h])
            self.decay_arg = self.sb("decay_arg", [P, J, h])
            self.decay = self.sb("decay", [P, J + 1, h])
            self.to_exp, self.from_exp = self.sem("to_exp"), self.sem("from_exp")
        self.same_now = self.sb("same_now", [P, J + 1])

    def sync(self, e, attrs):
        p = self.p
        out = p.sums[self.k].rearrange("(p j) f -> p j f", p=P)

        def load(b, now):
            e.dma_start(self.index[b][:, :], self.src_now[:, now]).then_inc(self.index_in[b], 16)
            for tiles, of in attrs:
                e.dma_start(tiles[b], of[:, now, :]).then_inc(self.attr_in[b], 16)

        def store(b, now):
            e.dma_start(out[:, now, :], self.val[b]).then_inc(self.stored[b], 16)

        for b in (0, 1):
            e.sem_inc(self.val_free[b], 1)
            load(b, slice(b * J, (b + 1) * J))
        with e.Fori(0, self.rounds - 1) as i:
            for b in (0, 1):
                hold(e, self.rows_free[b], at(i, 1, 2), self.passed)
                if attrs:
                    hold(e, self.attr_free[b], at(i, 1, 1), self.passed)
                load(b, bass.ds(i * (2 * J) + (2 + b) * J, J))
                hold(e, self.ready[b], at(i, 1, 1), self.passed)
                store(b, rows_of(i, b, J))
                e.wait_ge(self.stored[b], at(i, 16, 16))
                e.sem_inc(self.val_free[b], 1)
        for b in (0, 1):
            e.wait_ge(self.ready[b], self.rounds)
            store(b, slice((2 * self.rounds - 2 + b) * J, (2 * self.rounds - 1 + b) * J))
        for b in (0, 1):
            e.wait_ge(self.stored[b], 16 * self.rounds)

    def gpsimd(self, e):
        for b in (0, 1):
            e.sem_inc(self.rows_free[b], 1)
        with e.Fori(0, self.rounds) as i:
            for b in (0, 1):
                e.wait_ge(self.index_in[b], at(i, 16, 16))
                hold(e, self.rows_free[b], at(i, 1, 1), self.passed)
                for j in range(J):
                    e.indirect_dma_start(self.gather_into(b, j), None, self.gather_from,
                                         bass.IndirectOffsetOnAxis(ap=self.index[b][:, j:j + 1], axis=0))\
                        .then_inc(self.gathered[b], 16)

    def wait_gathered(self, e, i, b):
        e.wait_ge(self.gathered[b], at(i, 16 * J, 16 * J))

    def wait_attrs(self, e, i, b, n):
        e.wait_ge(self.attr_in[b], at(i, 16 * n, 16 * n))

    def wait_val_free(self, e, i, b):
        e.wait_ge(self.val_free[b], at(i, 1, 1))

    def clear_carries(self, e):
        e.memset(self.sums[0][:, 0, :], 0.0)
        e.memset(self.p.peak[:, 0, :], FAR)
        e.memset(self.same_now[:, 0:1], 1.0)
        if self.heads:
            e.memset(self.decay[:, 0, :], 1.0)
        e.drain()

    def segment_flags(self, e, i, b):
        now = rows_of(i, b, J)
        if self.heads:
            e.tensor_scalar(self.pen[:, :], self.p.same[:, now], -1.0, -FAR, ALU.add, ALU.mult)
        e.tensor_copy(self.same_now[:, 1:], self.p.same[:, now])
        e.drain()

    def running_softmax(self, e, i, b, score):
        h, peak = self.heads, self.p.peak
        for n in range(h):
            e.tensor_tensor_scan(out=peak[:, 1:, n], data0=self.pen[:, :], data1=score[:, :, n],
                                 initial=peak[:, 0, n:n + 1], op0=ALU.add, op1=ALU.max)
        e.drain()
        e.tensor_tensor(self.weight_arg[:, :, :], score[:, :, :], peak[:, 1:, 0:h], ALU.subtract)
        e.tensor_tensor(self.decay_arg[:, :, :], peak[:, 0:J, 0:h], bcast(self.pen[:, :], 2, h), ALU.add)
        e.drain()
        e.tensor_tensor(self.decay_arg[:, :, :], self.decay_arg[:, :, :], peak[:, 1:, 0:h], ALU.subtract)\
            .then_inc(self.to_exp, 1)
        at_row = h * (self.depth + 1)
        e.tensor_copy(self.val[b][:, :, at_row:at_row + h], peak[:, 1:, 0:h])

    def weights(self, b):
        h, d = self.heads, self.depth
        return self.val[b][:, :, 0:h * (d + 1)].rearrange("p j (h d) -> p j h d", h=h)[:, :, :, d]

    def values(self, b):
        h, d = self.heads, self.depth
        return self.val[b][:, :, 0:h * (d + 1)].rearrange("p j (h d) -> p j h d", h=h)[:, :, :, 0:d]

    def exponentials(self, e, i, b):
        e.wait_ge(self.to_exp, at(i, 2, 1 + b))
        e.activation(self.weights(b), self.weight_arg[:, :, :], ACT.Exp)
        e.activation(self.decay[:, 1:, :], self.decay_arg[:, :, :], ACT.Exp).then_inc(self.from_exp, 1)

    def wait_weights(self, e, i, b):
        e.wait_ge(self.from_exp, at(i, 2, 1 + b))

    def scan_sums(self, e, b):
        self.scan(e, b, range(self.heads * (self.depth + 1) if self.heads else self.depth))
        self.pass_on(e, b)

    def scan(self, e, b, features):
        h, d = self.heads, self.depth
        sums = self.sums[b]
        for f in features:
            keep = self.decay[:, :, f // (d + 1)] if h else self.same_now[:, :]
            e.tensor_tensor_scan(out=sums[:, :, f], data0=keep, data1=sums[:, :, f], initial=0.0,
                                 op0=ALU.mult, op1=ALU.add)

    def pass_on(self, e, b):
        h = self.heads
        n = h * (self.depth + 1) if h else self.depth
        e.drain()
        e.tensor_copy(self.sums[1 - b][:, 0, 0:n], self.sums[b][:, J, 0:n])
        if h:
            e.tensor_copy(self.p.peak[:, 0, 0:h], self.p.peak[:, J, 0:h])
        e.drain().then_inc(self.ready[b], 1)

    def keep_tails(self, e):
        e.tensor_copy(self.p.carry[:, 0:min(self.width, 130)], self.sums[0][:, 0, 0:min(self.width, 130)])


def edge_phase_0(p):
    nc = p.nc
    with nc.reset_on_exit(), ExitStack() as ctx:
        tiles = [ctx.enter_context(nc.sbuf_tensor(f"qv{b}", [P, J, 2 * FD], F32)) for b in (0, 1)]
        ph = EdgePhase(p, 0, ctx, p.qv_table, lambda b, j: tiles[b][:, j, :])
        k_all = [ph.sb(f"k{b}", [P, J + 1, FD]) for b in (0, 1)]
        k = [t[:, 1:, :] for t in k_all]
        score = ph.sb("score", [P, J, 4])
        gated = ph.sb("gated", [P, p.nodes_pp, FD])
        block = ctx.enter_context(nc.Block())
        k_edges = p.k_edges.rearrange("(p j) f -> p j f", p=P)

        @block.sync
        def _(e):
            ph.sync(e, [(k, k_edges)])

        @block.gpsimd
        def _(e):
            ph.gpsimd(e)

        @block.vector
        def _(e):
            e.memset(k_all[0][:, 0, :], 0.0)
            e.tensor_tensor(gated[:, :, :], p.aux[:, :, :], bcast(p.gate_a[:, :], 1, p.nodes_pp), ALU.mult)
            e.drain()
            e.tensor_reduce(p.skip_gate[:, :], gated[:, :, :], AX.X, ALU.add)
            ph.clear_carries(e)
            with e.Fori(0, ph.rounds) as i:
                for b in (0, 1):
                    ph.segment_flags(e, i, b)
                    ph.wait_attrs(e, i, b, 1)
                    for f in range(FD):
                        e.tensor_tensor_scan(out=k_all[b][:, :, f], data0=ph.same_now[:, :],
                                             data1=k_all[b][:, :, f], initial=0.0, op0=ALU.mult, op1=ALU.add)
                    e.drain()
                    e.tensor_copy(k_all[1 - b][:, 0, :], k_all[b][:, J, :])
                    e.drain()
                    ph.wait_gathered(e, i, b)
                    e.tensor_tensor(k[b], k[b], tiles[b][:, :, 0:FD], ALU.mult)
                    e.drain()
                    e.tensor_reduce(score[:, :, :], k[b].rearrange("p j (h d) -> p j h d", h=4),
                                    AX.X, ALU.add)
                    e.drain().then_inc(ph.attr_free[b], 1)
                    e.tensor_scalar(score[:, :, :], score[:, :, :], 0.25, None, ALU.mult)
                    e.drain()
                    ph.wait_val_free(e, i, b)
                    ph.running_softmax(e, i, b, score)
                    ph.wait_weights(e, i, b)
                    e.tensor_tensor(ph.values(b), tiles[b][:, :, FD:].rearrange("p j (h d) -> p j h d", h=4),
                                    bcast(ph.weights(b), 3, 16), ALU.mult)
                    e.drain().then_inc(ph.rows_free[b], 1)
                    ph.scan_sums(e, b)
            ph.keep_tails(e)

        @block.scalar
        def _(e):
            with e.Fori(0, ph.rounds) as i:
                for b in (0, 1):
                    ph.exponentials(e, i, b)


def edge_phase_1(p):
    nc = p.nc
    with nc.reset_on_exit(), ExitStack() as ctx:
        g = [ctx.enter_context(nc.sbuf_tensor(f"g{b}", [P, J, FD], F32)) for b in (0, 1)]
        ph = EdgePhase(p, 1, ctx, p.x_tables[0], lambda b, j: g[b][:, j, :])
        bond = [ph.sb(f"bond{b}", [P, J, FD]) for b in (0, 1)]
        product = ph.sb("product", [P, J, 2, FD])
        score = ph.sb("score", [P, J, 2])
        er = ph.sb("er", [P, p.edges_pp, 2])
        er_in = ph.sem("er_in")
        weighed = ph.sem("weighed")
        block = ctx.enter_context(nc.Block())

        @block.sync
        def _(e):
            e.dma_start(er[:, :, :], p.er_edges.rearrange("(p j) f -> p j f", p=P)).then_inc(er_in, 16)
            ph.sync(e, [([bond[0][:, :, :], bond[1][:, :, :]], p.ins["edge_attr_64"])])

        @block.gpsimd
        def _(e):
            ph.gpsimd(e)

        @block.vector
        def _(e):
            ph.clear_carries(e)
            e.wait_ge(er_in, 16)
            for n in range(2):
                e.tensor_tensor_scan(out=er[:, :, n], data0=p.same[:, :], data1=er[:, :, n], initial=0.0,
                                     op0=ALU.mult, op1=ALU.add)
            e.drain()
            with e.Fori(0, ph.rounds) as i:
                for b in (0, 1):
                    ph.segment_flags(e, i, b)
                    ph.wait_attrs(e, i, b, 1)
                    ph.wait_gathered(e, i, b)
                    e.tensor_tensor(g[b][:, :, :], g[b][:, :, :], bond[b][:, :, :], ALU.add)
                    e.drain().then_inc(ph.attr_free[b], 1)
                    e.tensor_tensor(product[:, :, :, :], bcast(g[b][:, :, :], 2, 2),
                                    bcast(p.attn_l[:, :, :], 1, J), ALU.mult)
                    e.drain()
                    e.tensor_reduce(score[:, :, :], product[:, :, :, :], AX.X, ALU.add)
                    e.drain()
                    e.tensor_tensor(score[:, :, :], score[:, :, :], er[:, rows_of(i, b, J), :], ALU.add)
                    e.drain()
                    e.scalar_tensor_tensor(score[:, :, :], score[:, :, :], 0.2, score[:, :, :],
                                           ALU.mult, ALU.max)
                    e.drain()
                    ph.wait_val_free(e, i, b)
                    ph.running_softmax(e, i, b, score)
                    ph.wait_weights(e, i, b)
                    e.tensor_tensor(ph.values(b)[:, :, 0, :], g[b][:, :, :],
                                    bcast(ph.weights(b)[:, :, 0], 2, FD), ALU.mult)
                    e.drain()
                    ph.scan(e, b, range(0, FD + 1))
                    e.wait_ge(weighed, at(i, 2, 1 + b))
                    e.sem_inc(ph.rows_free[b], 1)
                    ph.scan(e, b, range(FD + 1, 2 * FD + 2))
                    ph.pass_on(e, b)
            ph.keep_tails(e)

        @block.scalar
        def _(e):
            with e.Fori(0, ph.rounds) as i:
                for b in (0, 1):
                    ph.exponentials(e, i, b)
                    e.drain()
                    for j in range(J):
                        e.activation(ph.values(b)[:, j, 1, :], g[b][:, j, :], ACT.Copy,
                                     scale=ph.weights(b)[:, j, 1:2])
                    e.drain().then_inc(weighed, 1)


def edge_phase_2(p):
    nc = p.nc
    quads = J // QUAD
    per = 2 * quads
    with nc.reset_on_exit(), ExitStack() as ctx:
        se = [ctx.enter_context(nc.sbuf_tensor(f"se{b}", [P, J, P], F32)) for b in (0, 1)]
        ph = EdgePhase(p, 2, ctx, p.x_tables[1], lambda b, j: se[b][:, j, 0:FD])
        eh = [ph.sb(f"eh{b}", [P, J, FD]) for b in (0, 1)]
        qr = [ph.sb(f"qr{b}", [P, J, FD]) for b in (0, 1)]
        qe = [ph.sb(f"qe{b}", [P, J, FD]) for b in (0, 1)]
        se_t = [ph.sb(f"se_t{u}", [P, QUAD, P]) for u in (0, 1)]
        q_t = [ph.sb(f"q_t{u}", [P, QUAD, P]) for u in (0, 1)]
        q_now = [ph.sb(f"q_now{u}", [P, QUAD, FD]) for u in (0, 1)]
        product = ph.sb("product", [P, J, FD])
        score = ph.sb("score", [P, J, 1])
        ps = lambda n: ctx.enter_context(nc.psum_tensor(n, [P, QUAD, P], F32))
        se_ps = [ps(f"se_ps{u}") for u in (0, 1)]
        q_ps = [ps(f"q_ps{u}") for u in (0, 1)]
        mk_ps = [ps(f"mk_ps{u}") for u in (0, 1)]
        qo_ps = [ps(f"qo_ps{u}") for u in (0, 1)]
        joined = ph.sem("joined")
        turned = ph.sem("turned")
        moved = ph.sem("moved")
        multiplied = ph.sem("multiplied")
        taken = ph.sem("taken")
        scored = ph.sem("scored")
        msg_in = ph.sem("msg_in")
        block = ctx.enter_context(nc.Block())

        @block.sync
        def _(e):
            attr = lambda tiles, name: ([t[:, :, :] for t in tiles], p.ins[name])
            ph.sync(e, [attr(eh, "edge_attr_64"), attr(qr, "edge_attr_64_n2"), attr(qe, "edge_attr_64_n3")])

        @block.gpsimd
        def _(e):
            ph.gpsimd(e)

        @block.tensor
        def _(e):
            e.sem_inc(multiplied, 2)

            def turn(i, b, c):
                n = b * quads + c
                u = n % 2
                e.wait_ge(moved, at(i, per, n + 1))
                for j in range(QUAD):
                    e.transpose(se_ps[u][:, j, :], se[b][:, QUAD * c + j, :], p.ident[:, :])
                for s, tile in enumerate((qr, qe)):
                    for half in range(2):
                        j = QUAD * c + 2 * half
                        last = e.transpose(q_ps[u][:, 2 * s + half, :],
                                           tile[b][:, j:j + 2, :].rearrange("p a f -> p (a f)"), p.ident[:, :])
                last.then_inc(turned, 1)
                if c == quads - 1:
                    e.drain().then_inc(ph.rows_free[b], 1)
                    e.drain().then_inc(ph.attr_free[b], 1)

            def multiply(i, b, c):
                n = b * quads + c
                u = n % 2
                e.wait_ge(moved, at(i, per, n + 3))
                e.wait_ge(taken, at(i, per, n + 1))
                e.wait_ge(scored, at(i, per, n + 1))
                for j in range(QUAD):
                    e.matmul(mk_ps[u][:, j, :], se_t[u][:, j, :], p.w2_mk[:, :], start=True, stop=True)
                for half in range(2):
                    e.matmul(qo_ps[u][:, half, :], q_t[u][:, half, :], p.w2_qr[:, :], start=True, stop=False)
                    last = e.matmul(qo_ps[u][:, half, :], q_t[u][:, 2 + half, :], p.w2_qe[:, :],
                                    start=False, stop=True)
                last.then_inc(multiplied, 1)

            with e.Fori(0, ph.rounds) as i:
                for b in (0, 1):
                    ph.wait_gathered(e, i, b)
                    ph.wait_attrs(e, i, b, 3)
                    e.wait_ge(joined, at(i, 2, b + 1))
                    turn(i, b, 0)
                    for c in range(quads):
                        if c + 1 < quads:
                            turn(i, b, c + 1)
                        multiply(i, b, c)

        @block.scalar
        def _(e):
            e.sem_inc(moved, 2)
            e.sem_inc(taken, 2)

            def move(i, b, c):
                n = b * quads + c
                u = n % 2
                e.wait_ge(turned, at(i, per, n + 1))
                e.wait_ge(multiplied, at(i, per, n + 1))
                e.activation(se_t[u][:, :, :], se_ps[u][:, :, :], ACT.Copy)
                e.activation(q_t[u][:, :, :], q_ps[u][:, :, :], ACT.Copy).then_inc(moved, 1)

            def take(i, b, c):
                n = b * quads + c
                u = n % 2
                e.wait_ge(multiplied, at(i, per, n + 3))
                e.wait_ge(scored, at(i, per, n + 1))
                e.activation(q_now[u][:, :, :], qo_ps[u][:, 0:2, :].rearrange("p a (c f) -> p (a c) f", c=2),
                             ACT.Copy)
                e.activation(ph.val[b][:, QUAD * c:QUAD * (c + 1), 0:FD], mk_ps[u][:, :, 0:FD], ACT.Copy)\
                    .then_inc(taken, 1)

            with e.Fori(0, ph.rounds) as i:
                for b in (0, 1):
                    e.wait_ge(ph.rows_free[b], at(i, 1, 1))
                    ph.wait_attrs(e, i, b, 3)
                    e.activation(se[b][:, :, FD:], eh[b][:, :, :], ACT.Copy).then_inc(joined, 1)
                    ph.wait_val_free(e, i, b)
                    move(i, b, 0)
                    for c in range(quads):
                        if c + 1 < quads:
                            move(i, b, c + 1)
                        take(i, b, c)
                    e.drain().then_inc(msg_in, 1)
                    ph.exponentials(e, i, b)

        @block.vector
        def _(e):
            e.sem_inc(scored, 2)
            ph.clear_carries(e)
            with e.Fori(0, ph.rounds) as i:
                for b in (0, 1):
                    ph.segment_flags(e, i, b)
                    for c in range(quads):
                        n = b * quads + c
                        u = n % 2
                        e.wait_ge(taken, at(i, per, n + 3))
                        e.tensor_tensor(product[:, QUAD * c:QUAD * (c + 1), :], mk_ps[u][:, :, FD:],
                                        q_now[u][:, :, :], ALU.mult).then_inc(scored, 1)
                    e.drain()
                    e.tensor_reduce(score[:, :, :], product[:, :, :], AX.X, ALU.add)
                    e.drain()
                    e.tensor_scalar(score[:, :, :], score[:, :, :], 0.125, None, ALU.mult)
                    e.drain()
                    e.wait_ge(msg_in, at(i, 2, b + 1))
                    ph.running_softmax(e, i, b, score)
                    msg = ph.val[b][:, :, 0:FD]
                    e.scalar_tensor_tensor(msg, msg, 0.01, msg, ALU.mult, ALU.max)
                    e.drain()
                    ph.wait_weights(e, i, b)
                    e.tensor_tensor(msg, msg, ph.weights(b).to_broadcast([P, J, FD]), ALU.mult)
                    e.drain()
                    ph.scan_sums(e, b)
            ph.keep_tails(e)


def edge_phase_3(p):
    nc = p.nc
    quads = J // QUAD
    per = 2 * quads
    K = 97
    with nc.reset_on_exit(), ExitStack() as ctx:
        comb = [ctx.enter_context(nc.sbuf_tensor(f"comb{b}", [P, J, K], F32)) for b in (0, 1)]
        ph = EdgePhase(p, 3, ctx, p.x_tables[2], lambda b, j: comb[b][:, j, 0:FD])
        ea = [ph.sb(f"ea{b}", [P, J, 32]) for b in (0, 1)]
        comb_t = [ph.sb(f"comb_t{u}", [K, QUAD, P]) for u in (0, 1)]
        ps = lambda n: ctx.enter_context(nc.psum_tensor(n, [P, QUAD, P], F32))
        t_ps = [ps(f"t_ps{u}") for u in (0, 1)]
        h_ps = [ps(f"h_ps{u}") for u in (0, 1)]
        joined = ph.sem("joined")
        turned = ph.sem("turned")
        moved = ph.sem("moved")
        multiplied = ph.sem("multiplied")
        taken = ph.sem("taken")
        block = ctx.enter_context(nc.Block())

        @block.sync
        def _(e):
            ph.sync(e, [([t[:, :, :] for t in ea], p.ins["edge_attr_32"])])

        @block.gpsimd
        def _(e):
            ph.gpsimd(e)

        @block.tensor
        def _(e):
            e.sem_inc(multiplied, 2)

            def turn(i, b, c):
                n = b * quads + c
                e.wait_ge(moved, at(i, per, n + 1))
                for j in range(QUAD):
                    last = e.transpose(t_ps[n % 2][0:K, j, :], comb[b][:, QUAD * c + j, :], p.ident[:, :])
                last.then_inc(turned, 1)
                if c == quads - 1:
                    e.drain().then_inc(ph.rows_free[b], 1)

            def multiply(i, b, c):
                n = b * quads + c
                e.wait_ge(moved, at(i, per, n + 3))
                e.wait_ge(taken, at(i, per, n + 1))
                for j in range(QUAD):
                    last = e.matmul(h_ps[n % 2][:, j, :], comb_t[n % 2][:, j, :], p.w3_hidden[:, :],
                                    start=True, stop=True)
                last.then_inc(multiplied, 1)

            with e.Fori(0, ph.rounds) as i:
                for b in (0, 1):
                    ph.wait_gathered(e, i, b)
                    e.wait_ge(joined, at(i, 2, b + 1))
                    turn(i, b, 0)
                    for c in range(quads):
                        if c + 1 < quads:
                            turn(i, b, c + 1)
                        multiply(i, b, c)

        @block.scalar
        def _(e):
            e.sem_inc(moved, 2)
            e.sem_inc(taken, 2)
            for b in (0, 1):
                e.activation(comb[b][:, :, K - 1:], p.ones[:, 0:J].unsqueeze(2), ACT.Copy)

            def move(i, b, c):
                n = b * quads + c
                e.wait_ge(turned, at(i, per, n + 1))
                e.wait_ge(multiplied, at(i, per, n + 1))
                e.activation(comb_t[n % 2][:, :, :], t_ps[n % 2][0:K, :, :], ACT.Copy).then_inc(moved, 1)

            def take(i, b, c):
                n = b * quads + c
                e.wait_ge(multiplied, at(i, per, n + 3))
                e.activation(ph.val[b][:, QUAD * c:QUAD * (c + 1), :], h_ps[n % 2][:, :, :], ACT.Relu)\
                    .then_inc(taken, 1)

            with e.Fori(0, ph.rounds) as i:
                for b in (0, 1):
                    e.wait_ge(ph.rows_free[b], at(i, 1, 1))
                    ph.wait_attrs(e, i, b, 1)
                    e.activation(comb[b][:, :, FD:K - 1], ea[b][:, :, :], ACT.Copy).then_inc(joined, 1)
                    e.drain().then_inc(ph.attr_free[b], 1)
                    ph.wait_val_free(e, i, b)
                    move(i, b, 0)
                    for c in range(quads):
                        if c + 1 < quads:
                            move(i, b, c + 1)
                        take(i, b, c)

        @block.vector
        def _(e):
            ph.clear_carries(e)
            with e.Fori(0, ph.rounds) as i:
                for b in (0, 1):
                    ph.segment_flags(e, i, b)
                    e.wait_ge(taken, at(i, per, (b + 1) * quads + 2))
                    ph.scan_sums(e, b)
            ph.keep_tails(e)


def fix_phase(p, layer):
    nc = p.nc
    h, d = p.shape[layer]
    w = p.width[layer]
    with nc.reset_on_exit(), ExitStack() as ctx:
        sb = lambda n, s, dt=F32: ctx.enter_context(nc.sbuf_tensor(f"fix{layer}_{n}", s, dt))
        sem = lambda n: ctx.enter_context(nc.semaphore(f"fix{layer}_{n}"))
        row = sb("row", [P, w])
        n = max(h, 1)
        wide = sb("wide", [P, n, P])
        turned = sb("turned", [P, n, P])
        top = sb("top", [P, n])
        scale = sb("scale", [P, n])
        ps = ctx.enter_context(nc.psum_tensor(f"fix{layer}_ps", [P, n, P], F32))
        ps_t = ctx.enter_context(nc.psum_tensor(f"fix{layer}_ps_t", [P, n, P], F32))
        ps_s = ctx.enter_context(nc.psum_tensor(f"fix{layer}_ps_s", [P, 130], F32))
        got, ready, done, v2a, a2v = sem("got"), sem("ready"), sem("done"), sem("v2a"), sem("a2v")
        v2p, p2v = sem("v2p"), sem("p2v")
        block = ctx.enter_context(nc.Block())

        @block.gpsimd
        def _(e):
            e.indirect_dma_start(row[:, :], None, p.sums[layer],
                                 bass.IndirectOffsetOnAxis(ap=p.fix_from[:, 0:1], axis=0)).then_inc(got, 16)
            e.wait_ge(ready, 1)
            e.indirect_dma_start(p.sums[layer], bass.IndirectOffsetOnAxis(ap=p.fix_to[:, 0:1], axis=0),
                                 row[:, :], None, bounds_check=p.n_edges - 1, oob_is_err=False)\
                .then_inc(done, 16)
            e.wait_ge(done, 16)

        @block.vector
        def _(e):
            if h:
                e.tensor_copy(wide[:, :, :], bcast(p.peak[:, 0, 0:h], 2, P)).then_inc(v2p, 1)
                e.wait_ge(got, 16)
                e.wait_ge(p2v, 1)
                e.tensor_tensor(wide[:, :, :], ps[:, :, :], bcast(p.chain_pen[:, :], 1, h), ALU.add)
                e.drain()
                e.tensor_reduce(top[:, :], wide[:, :, :], AX.X, ALU.max)
                e.drain()
                e.tensor_tensor(top[:, :], top[:, :], row[:, h * (d + 1):], ALU.max)
                e.drain()
                e.tensor_tensor(wide[:, :, :], wide[:, :, :], bcast(top[:, :], 2, P), ALU.subtract)
                e.tensor_tensor(scale[:, :], row[:, h * (d + 1):], top[:, :], ALU.subtract).then_inc(v2a, 1)
                e.wait_ge(p2v, 2)
                e.tensor_copy(turned[:, :, :], ps_t[:, :, :]).then_inc(v2p, 1)
                e.wait_ge(p2v, 3)
                own = row[:, 0:h * (d + 1)].rearrange("p (h d) -> p h d", h=h)
                e.tensor_tensor(own, own, bcast(scale[:, :], 2, d + 1), ALU.mult)
                e.drain()
                e.tensor_tensor(row[:, 0:h * (d + 1)], row[:, 0:h * (d + 1)], ps_s[:, 0:h * (d + 1)], ALU.add)\
                    .then_inc(ready, 1)
            else:
                e.wait_ge(got, 16)
                e.wait_ge(p2v, 1)
                e.tensor_tensor(row[:, :], row[:, :], ps_s[:, 0:d], ALU.add).then_inc(ready, 1)

        @block.scalar
        def _(e):
            if h:
                e.wait_ge(v2a, 1)
                e.activation(wide[:, :, :], wide[:, :, :], ACT.Exp)
                e.activation(scale[:, :], scale[:, :], ACT.Exp).then_inc(a2v, 1)

        @block.tensor
        def _(e):
            if h:
                e.wait_ge(v2p, 1)
                for k in range(h):
                    last = e.matmul(ps[:, k, :], wide[:, k, :], p.ident[:, :], start=True, stop=True)
                last.then_inc(p2v, 1)
                e.wait_ge(a2v, 1)
                for k in range(h):
                    last = e.transpose(ps_t[:, k, :], wide[:, k, :], p.ident[:, :])
                last.then_inc(p2v, 1)
                e.wait_ge(v2p, 2)
                for k in range(h):
                    s = slice(k * (d + 1), (k + 1) * (d + 1))
                    last = e.matmul(ps_s[:, s], turned[:, k, :], p.carry[:, s], start=True, stop=True)
                last.then_inc(p2v, 1)
            else:
                e.matmul(ps_s[:, 0:d], p.chain_t[:, :], p.carry[:, 0:d], start=True, stop=True)\
                    .then_inc(p2v, 1)


class NodePhase:

    def __init__(self, p, layer, ctx):
        nc = p.nc
        self.p, self.layer = p, layer
        tag = f"node{layer}"
        self.sb = lambda n, s, d=F32: ctx.enter_context(nc.sbuf_tensor(f"{tag}_{n}", s, d))
        self.sem = lambda n: ctx.enter_context(nc.semaphore(f"{tag}_{n}"))
        self.sbs = lambda n, s, d=F32: [self.sb(f"{n}{b}", s, d) for b in (0, 1)]
        self.sems = lambda n: [self.sem(f"{n}{b}") for b in (0, 1)]
        self.ps = lambda n, s: [ctx.enter_context(nc.psum_tensor(f"{tag}_{n}{b}", s, F32)) for b in (0, 1)]
        self.rounds = p.groups // 2
        self.index = self.sbs("ix", [P, G], U32)
        self.rows = self.sbs("rows", [P, G, p.width[layer]])
        self.index_in, self.gathered = self.sems("index_in"), self.sems("gathered")
        self.rows_free = self.sems("rows_free")
        self.state = self.sbs("state", [P, G, FD])
        self.state_ready, self.state_out = self.sems("state_ready"), self.sems("state_out")
        self.state_free = self.sems("state_free")
        self.state_kept = self.sems("state_kept")
        self.passed = self.sem("passed")
        self.square = self.sbs("square", [P, G, FD])
        self.mean, self.var = self.sbs("mean", [P, G]), self.sbs("var", [P, G])
        self.to_square, self.from_square = self.sems("to_square"), self.sems("from_square")
        self.to_root, self.from_root = self.sems("to_root"), self.sems("from_root")

    def staged(self, e, stages):
        with e.Fori(0, self.rounds) as i:
            for stage in stages:
                for b in (0, 1):
                    stage(i, b)

    def sync(self, e, table, extra=(), more_indices=None):
        p = self.p
        first = [slice(b * G, (b + 1) * G) for b in (0, 1)]
        for b in (0, 1):
            e.sem_inc(self.state_free[b], 1)
            e.dma_start(self.index[b][:, :], p.end_index[:, first[b]]).then_inc(self.index_in[b], 16)
            if more_indices:
                tiles, of, came, _, _, free = more_indices
                e.sem_inc(free[b], 1)
                e.dma_start(tiles[b][:, :], of[:, first[b]]).then_inc(came[b], 16)
        out = None if table is None else table.rearrange("(p t) f -> p t f", p=P)
        stores = 16 * (1 + len(extra))

        def store(b, now):
            e.dma_start(out[:, now, :], self.state[b][:, :, :]).then_inc(self.state_out[b], 16)
            for tiles, to in extra:
                e.dma_start(to[:, now, :], tiles[b]).then_inc(self.state_out[b], 16)

        with e.Fori(0, self.rounds - 1) as i:
            after = [bass.ds(i * (2 * G) + (2 + b) * G, G) for b in (0, 1)]
            for b in (0, 1):
                hold(e, self.rows_free[b], at(i, 1, 2), self.passed)
                e.dma_start(self.index[b][:, :], p.end_index[:, after[b]]).then_inc(self.index_in[b], 16)
            if out is not None:
                for b in (0, 1):
                    hold(e, self.state_ready[b], at(i, 1, 1), self.passed)
                    store(b, rows_of(i, b, G))
                for b in (0, 1):
                    e.wait_ge(self.state_out[b], at(i, stores, stores))
                    e.sem_inc(self.state_free[b], 1)
                    if more_indices:
                        tiles, of, came, read, step, free = more_indices
                        hold(e, read[b], at(i, step, step), self.passed)
                        e.sem_inc(free[b], 1)
                        e.dma_start(tiles[b][:, :], of[:, after[b]]).then_inc(came[b], 16)
        if out is not None:
            for b in (0, 1):
                e.wait_ge(self.state_ready[b], self.rounds)
                store(b, slice((2 * self.rounds - 2 + b) * G, (2 * self.rounds - 1 + b) * G))
            for b in (0, 1):
                e.wait_ge(self.state_out[b], stores * self.rounds)

    def gather(self, e, i, b):
        e.wait_ge(self.index_in[b], at(i, 16, 16))
        hold(e, self.rows_free[b], at(i, 1, 1), self.passed)
        for t in range(G):
            e.indirect_dma_start(self.rows[b][:, t, :], None, self.p.sums[self.layer],
                                 bass.IndirectOffsetOnAxis(ap=self.index[b][:, t:t + 1], axis=0))\
                .then_inc(self.gathered[b], 16)

    def gpsimd(self, e):
        for b in (0, 1):
            e.sem_inc(self.rows_free[b], 1)
        self.staged(e, [lambda i, b: self.gather(e, i, b)])

    def wait_gathered(self, e, i, b):
        e.wait_ge(self.gathered[b], at(i, 16 * G, 16 * G))

    def shares(self, e, i, b, share, heads, depth):
        den = self.rows[b][:, :, 0:heads * (depth + 1)].rearrange("p t (h d) -> p t h d", h=heads)[:, :, :, depth]
        e.reciprocal(share[:, :, :], den)
        e.drain()
        e.tensor_tensor(share[:, :, :], share[:, :, :],
                        bcast(self.p.live[:, rows_of(i, b, G)], 2, heads), ALU.mult)
        e.drain()

    def centre(self, e, b, a):
        centre(e, a, self.mean[b][:, :]).then_inc(self.to_square[b], 1)

    def sum_squares(self, e, i, b, per, n):
        e.wait_ge(self.from_square[b], at(i, per, n))
        e.tensor_reduce(self.var[b][:, :], self.square[b][:, :, :], AX.X, ALU.add).then_inc(self.to_root[b], 1)

    def scale(self, e, i, b, per, n, a):
        e.wait_ge(self.from_root[b], at(i, per, n))
        scale_rows(e, a, self.var[b][:, :])

    def act_square(self, e, i, b, per, n, a):
        e.wait_ge(self.to_square[b], at(i, per, n))
        e.activation(self.square[b][:, :, :], a, ACT.Square).then_inc(self.from_square[b], 1)

    def act_root(self, e, i, b, per, n, eps):
        e.wait_ge(self.to_root[b], at(i, per, n))
        e.activation(self.var[b][:, :], self.var[b][:, :], ACT.Sqrt, bias=eps, scale=1.0 / FD)\
            .then_inc(self.from_root[b], 1)

    def act_keep(self, e, i, b):
        e.wait_ge(self.state_kept[b], at(i, 2, 1))
        e.activation(self.p.x[:, rows_of(i, b, G), :], self.state[b][:, :, :], ACT.Copy)
        e.drain().then_inc(self.state_kept[b], 1)


def centre(e, a, mean):
    e.tensor_reduce(mean, a, AX.X, ALU.add)
    e.drain()
    e.tensor_scalar(mean, mean, 1.0 / FD, None, ALU.mult)
    e.drain()
    e.tensor_tensor(a, a, bcast(mean, 2, FD), ALU.subtract)
    return e.drain()


def scale_rows(e, a, root):
    e.reciprocal(root, root)
    e.drain()
    e.tensor_tensor(a, a, bcast(root, 2, FD), ALU.mult)
    e.drain()


class Product:

    def __init__(self, ph, name, per=1):
        self.ph, self.per = ph, per
        self.t_ps = ph.ps(f"{name}_t_ps", [P, 2, QUAD, P])
        self.h_ps = ph.ps(f"{name}_h_ps", [P, G, FD])
        self.tile_t = ph.sbs(f"{name}_t", [P, G, P])
        self.given, self.turned = ph.sems(f"{name}_given"), ph.sems(f"{name}_turned")
        self.moved, self.done = ph.sems(f"{name}_moved"), ph.sems(f"{name}_done")

    def pe(self, e, i, b, tile, w, n=1):
        wide, cols = w.shape[0], w.shape[1]
        hold(e, self.given[b], at(i, self.per, n), self.ph.passed)
        for t in range(G):
            last = e.transpose(self.t_ps[b][0:wide, t // QUAD, t % QUAD, :], tile[:, t, :], self.ph.p.ident[:, :])
        last.then_inc(self.turned[b], 1)
        e.wait_ge(self.moved[b], at(i, self.per, n))
        for t in range(G):
            last = e.matmul(self.h_ps[b][:, t, 0:cols], self.tile_t[b][0:wide, t, :], w[:, :],
                            start=True, stop=True)
        last.then_inc(self.done[b], 1)

    def act(self, e, i, b, wide, n=1):
        e.wait_ge(self.turned[b], at(i, self.per, n))
        e.activation(self.tile_t[b][0:wide, 0:QUAD, :], self.t_ps[b][0:wide, 0, :, :], ACT.Copy)
        e.activation(self.tile_t[b][0:wide, QUAD:G, :], self.t_ps[b][0:wide, 1, 0:G - QUAD, :], ACT.Copy)\
            .then_inc(self.moved[b], 1)

    def wait(self, e, i, b, n=1):
        e.wait_ge(self.done[b], at(i, self.per, n))


def node_phase_0(p):
    nc = p.nc
    with nc.reset_on_exit(), ExitStack() as ctx:
        ph = NodePhase(p, 0, ctx)
        share = ph.sbs("share", [P, G, 4])
        agg = ph.sbs("agg", [P, G, FD])
        diff = ph.sbs("diff", [P, G, FD])
        gate = ph.sbs("gate", [P, G])
        er = ph.sbs("er", [P, G, 2])
        start_ix = ph.sbs("start_ix", [P, G], U32)
        first_er = ph.sb("first_er", [P, 2])
        times_attn = Product(ph, "attn")
        to_exp, from_exp = ph.sems("to_exp"), ph.sems("from_exp")
        start_in, sent, er_ready = ph.sems("start_in"), ph.sems("sent"), ph.sems("er_ready")
        er_free = ph.sems("er_free")
        s_first, s_last = ph.sem("first"), ph.sem("last")
        tables_out = ph.sem("tables_out")
        block = ctx.enter_context(nc.Block())

        @block.sync
        def _(e):
            ph.sync(e, p.x_tables[0],
                    [([er[0][:, :, :], er[1][:, :, :]], p.er_table.rearrange("(p t) f -> p t f", p=P))],
                    (start_ix, p.start_index, start_in, sent, 16 * G, er_free))
            e.sem_inc(tables_out, 1)

        @block.gpsimd
        def _(e):
            for b in (0, 1):
                e.sem_inc(ph.rows_free[b], 1)
                ph.gather(e, 0, b)

            def scatter(i, b):
                e.wait_ge(start_in[b], at(i, 16, 16))
                hold(e, er_ready[b], at(i, 1, 1), ph.passed)
                for t in range(G):
                    e.indirect_dma_start(p.er_edges, bass.IndirectOffsetOnAxis(ap=start_ix[b][:, t:t + 1], axis=0),
                                         er[b][:, t, :], None, bounds_check=p.n_edges - 1,
                                         oob_is_err=False).then_inc(sent[b], 16)

            with e.Fori(0, ph.rounds - 1) as i:
                for b in (0, 1):
                    ph.gather(e, i + 1, b)
                for b in (0, 1):
                    scatter(i, b)
            for b in (0, 1):
                scatter(ph.rounds - 1, b)
            e.wait_ge(tables_out, 1)
            e.indirect_dma_start(first_er[:, :], None, p.er_table,
                                 bass.IndirectOffsetOnAxis(ap=p.first_index[:, 0:1], axis=0))\
                .then_inc(s_first, 16)
            for b in (0, 1):
                e.wait_ge(sent[b], 16 * G * ph.rounds)
            e.wait_ge(s_first, 16)
            e.dma_start(p.er_edges.rearrange("(p j) f -> p j f", p=P)[:, 0, :], first_er[:, :])\
                .then_inc(s_last, 16)
            e.wait_ge(s_last, 16)

        @block.tensor
        def _(e):
            ph.staged(e, [lambda i, b: times_attn.pe(e, i, b, ph.state[b], p.attn_r)])

        @block.scalar
        def _(e):
            def sigmoid(i, b):
                e.wait_ge(to_exp[b], at(i, 1, 1))
                e.activation(gate[b][:, :], gate[b][:, :], ACT.Exp, bias=p.gate_bias[:, 0:1], scale=-1.0)\
                    .then_inc(from_exp[b], 1)

            def take_er(i, b):
                times_attn.act(e, i, b, FD)
                ph.act_keep(e, i, b)
                times_attn.wait(e, i, b)
                e.wait_ge(er_free[b], at(i, 1, 1))
                e.activation(er[b][:, :, :], times_attn.h_ps[b][:, :, 0:2], ACT.Copy)
                e.drain().then_inc(er_ready[b], 1)
                e.drain().then_inc(ph.state_ready[b], 1)

            eps = p.eps[:, 0:1]
            ph.staged(e, [
                sigmoid,
                lambda i, b: ph.act_square(e, i, b, 2, 1, agg[b][:, :, :]),
                lambda i, b: ph.act_root(e, i, b, 2, 1, eps),
                lambda i, b: ph.act_square(e, i, b, 2, 2, ph.state[b][:, :, :]),
                lambda i, b: ph.act_root(e, i, b, 2, 2, eps),
                take_er,
            ])

        @block.vector
        def _(e):
            def aggregate(i, b):
                a, d = agg[b][:, :, :], diff[b][:, :, :]
                ph.wait_gathered(e, i, b)
                ph.shares(e, i, b, share[b], 4, 16)
                rows = ph.rows[b][:, :, 0:68].rearrange("p t (h d) -> p t h d", h=4)[:, :, :, 0:16]
                e.tensor_tensor(a.rearrange("p t (h d) -> p t h d", h=4), rows,
                                bcast(share[b][:, :, :], 3, 16), ALU.mult)
                e.drain().then_inc(ph.rows_free[b], 1)
                e.tensor_tensor(d, a, bcast(p.gate_b[:, :], 1, G), ALU.mult)
                e.drain()
                e.tensor_reduce(gate[b][:, :], d, AX.X, ALU.add)
                e.drain()
                now = rows_of(i, b, G)
                e.tensor_tensor(gate[b][:, :], gate[b][:, :], p.skip_gate[:, now], ALU.add).then_inc(to_exp[b], 1)
                e.tensor_tensor(d, p.aux[:, now, :], a, ALU.subtract)

            def mix(i, b):
                a, d = agg[b][:, :, :], diff[b][:, :, :]
                e.wait_ge(from_exp[b], at(i, 1, 1))
                e.tensor_scalar(gate[b][:, :], gate[b][:, :], 1.0, None, ALU.add)
                e.drain()
                e.reciprocal(gate[b][:, :], gate[b][:, :])
                e.drain()
                e.tensor_tensor(d, d, bcast(gate[b][:, :], 2, FD), ALU.mult)
                e.drain()
                e.tensor_tensor(a, a, d, ALU.add)
                e.drain()
                ph.centre(e, b, a)

            def activate(i, b):
                a, d, state = agg[b][:, :, :], diff[b][:, :, :], ph.state[b][:, :, :]
                ph.scale(e, i, b, 2, 1, a)
                e.tensor_tensor(a, a, bcast(p.param["L0_gnn_ln_g"][:, :], 1, G), ALU.mult)
                e.drain()
                e.tensor_tensor(a, a, bcast(p.param["L0_gnn_ln_b"][:, :], 1, G), ALU.add)
                e.drain()
                e.tensor_scalar(d, a, 0.0, p.slope[:, 0:1], ALU.min, ALU.mult)
                e.drain()
                e.scalar_tensor_tensor(a, a, 0.0, d, ALU.max, ALU.add)
                e.drain()
                e.wait_ge(ph.state_free[b], at(i, 1, 1))
                e.tensor_tensor(state, p.x[:, rows_of(i, b, G), :], a, ALU.add)
                e.drain()
                ph.centre(e, b, state)

            def finish(i, b):
                ph.scale(e, i, b, 2, 2, ph.state[b][:, :, :])
                e.drain().then_inc(times_attn.given[b], 1)
                e.sem_inc(ph.state_kept[b], 1)

            ph.staged(e, [
                aggregate, mix,
                lambda i, b: ph.sum_squares(e, i, b, 2, 1),
                activate,
                lambda i, b: ph.sum_squares(e, i, b, 2, 2),
                finish,
            ])


def node_phase_1(p):
    nc = p.nc
    T = p.nodes_pp
    with nc.reset_on_exit(), ExitStack() as ctx:
        ph = NodePhase(p, 1, ctx)
        share = ph.sbs("share", [P, G, 2])
        agg = ph.sbs("agg", [P, G, P])
        times_w = Product(ph, "w")
        squares = ph.sb("squares", [P, T, FD])
        mean = ph.sb("all_mean", [P, T])
        root = ph.sb("all_root", [P, T])
        part = ph.sb("part", [P, FD])
        bn_mean = ph.sb("bn_mean", [P, FD])
        bn_scale = ph.sb("bn_scale", [P, FD])
        mean_sq = ph.sb("mean_sq", [P, FD])
        sum_ps = ctx.enter_context(nc.psum_tensor("n1_sum_ps", [P, 512], F32))
        kept = ph.sems("kept")
        v2p, p2v, v2a, a2v, done, out = (ph.sem(n) for n in ("v2p", "p2v", "v2a", "a2v", "done", "out"))
        halves = [slice(0, T // 2), slice(T // 2, T)]
        block = ctx.enter_context(nc.Block())

        @block.sync
        def _(e):
            ph.sync(e, None)
            table = p.x_tables[1].rearrange("(p t) f -> p t f", p=P)
            for k, s in enumerate(halves):
                e.wait_ge(done, k + 1)
                e.dma_start(table[:, s, :], p.x[:, s, :]).then_inc(out, 16)
            e.wait_ge(out, 32)

        @block.gpsimd
        def _(e):
            ph.gpsimd(e)

        @block.tensor
        def _(e):
            ph.staged(e, [lambda i, b: times_w.pe(e, i, b, agg[b], p.w1_heads)])
            for k in range(2):
                e.wait_ge(v2p, k + 1)
                e.matmul(sum_ps[:, k * FD:(k + 1) * FD], p.ones[:, :], part[:, :], start=True, stop=True)\
                    .then_inc(p2v, 1)

        @block.scalar
        def _(e):
            def keep_h(i, b):
                times_w.wait(e, i, b)
                e.activation(p.aux[:, rows_of(i, b, G), :], times_w.h_ps[b][:, :, :], ACT.Copy)
                e.drain().then_inc(kept[b], 1)

            ph.staged(e, [lambda i, b: times_w.act(e, i, b, P), keep_h])
            for k, s in enumerate(halves):
                e.wait_ge(v2a, k + 1)
                e.activation(squares[:, s, :], p.aux[:, s, :], ACT.Square).then_inc(a2v, 1)
            e.wait_ge(v2a, 3)
            e.activation(bn_scale[:, :], bn_scale[:, :], ACT.Sqrt, bias=p.eps[:, 0:1], scale=1.0 / p.n_nodes)\
                .then_inc(a2v, 1)
            for k, s in enumerate(halves):
                e.wait_ge(v2a, k + 4)
                e.activation(squares[:, s, :], p.x[:, s, :], ACT.Square).then_inc(a2v, 1)
            for k, s in enumerate(halves):
                e.wait_ge(v2a, k + 6)
                e.activation(root[:, s], root[:, s], ACT.Sqrt, bias=p.eps[:, 0:1], scale=1.0 / FD)\
                    .then_inc(a2v, 1)

        @block.vector
        def _(e):
            def aggregate(i, b):
                ph.wait_gathered(e, i, b)
                ph.shares(e, i, b, share[b], 2, FD)
                rows = ph.rows[b][:, :, 0:130].rearrange("p t (h d) -> p t h d", h=2)[:, :, :, 0:FD]
                e.tensor_tensor(agg[b][:, :, :].rearrange("p t (h d) -> p t h d", h=2), rows,
                                bcast(share[b][:, :, :], 3, FD), ALU.mult)
                e.drain().then_inc(ph.rows_free[b], 1)
                e.sem_inc(times_w.given[b], 1)

            def taken(i, b):
                e.wait_ge(kept[b], at(i, 1, 1))

            ph.staged(e, [aggregate, taken])
            gamma, beta = p.param["L1_gnn_bn_gamma"], p.param["L1_gnn_bn_beta"]
            by_feature = lambda a: a.rearrange("p t f -> p f t")
            e.tensor_reduce(part[:, :], by_feature(p.aux[:, :, :]), AX.X, ALU.add)
            e.drain().then_inc(v2p, 1)
            e.wait_ge(p2v, 1)
            e.tensor_scalar(bn_mean[:, :], sum_ps[:, 0:FD], 1.0 / p.n_nodes, None, ALU.mult)
            e.drain()
            for s in halves:
                h = p.aux[:, s, :]
                e.tensor_tensor(h, h, bcast(bn_mean[:, :], 1, T // 2), ALU.subtract)
                e.drain().then_inc(v2a, 1)
            e.tensor_tensor(mean_sq[:, :], bn_mean[:, :], bn_mean[:, :], ALU.mult)
            e.wait_ge(a2v, 2)
            e.tensor_reduce(part[:, :], by_feature(squares[:, :, :]), AX.X, ALU.add)
            e.drain().then_inc(v2p, 1)
            e.wait_ge(p2v, 2)
            e.scalar_tensor_tensor(bn_scale[:, :], mean_sq[:, :], -float(p.n_rows - p.n_nodes),
                                   sum_ps[:, FD:2 * FD], ALU.mult, ALU.add)
            e.drain()
            e.tensor_scalar(bn_scale[:, :], bn_scale[:, :], 0.0, None, ALU.max)
            e.drain().then_inc(v2a, 1)
            e.wait_ge(a2v, 3)
            e.reciprocal(bn_scale[:, :], bn_scale[:, :])
            e.drain()
            e.tensor_tensor(bn_scale[:, :], bn_scale[:, :], gamma[:, :], ALU.mult)
            e.drain()
            for s in halves:
                h, x = p.aux[:, s, :], p.x[:, s, :]
                e.tensor_tensor(h, h, bcast(bn_scale[:, :], 1, T // 2), ALU.mult)
                e.drain()
                e.tensor_tensor(h, h, bcast(beta[:, :], 1, T // 2), ALU.add)
                e.drain()
                e.scalar_tensor_tensor(x, h, 0.0, x, ALU.max, ALU.add)
                e.drain()
                centre(e, x, mean[:, s]).then_inc(v2a, 1)
            for k, s in enumerate(halves):
                e.wait_ge(a2v, 4 + k)
                e.tensor_reduce(root[:, s], squares[:, s, :], AX.X, ALU.add)
                e.drain().then_inc(v2a, 1)
            for k, s in enumerate(halves):
                e.wait_ge(a2v, 6 + k)
                scale_rows(e, p.x[:, s, :], root[:, s])
                e.drain().then_inc(done, 1)


def node_phase_2(p):
    nc = p.nc
    with nc.reset_on_exit(), ExitStack() as ctx:
        ph = NodePhase(p, 2, ctx)
        share = ph.sbs("share", [P, G, 1])
        agg = ph.sbs("agg", [P, G, FD])
        other = ph.sbs("other", [P, G, FD])
        times_w = Product(ph, "w")
        taken = ph.sems("taken")
        block = ctx.enter_context(nc.Block())

        @block.sync
        def _(e):
            ph.sync(e, p.x_tables[2])

        @block.gpsimd
        def _(e):
            ph.gpsimd(e)

        @block.tensor
        def _(e):
            ph.staged(e, [lambda i, b: times_w.pe(e, i, b, agg[b], p.w2_out)])

        @block.scalar
        def _(e):
            def take(i, b):
                times_w.wait(e, i, b)
                e.activation(other[b][:, :, :], times_w.h_ps[b][:, :, :], ACT.Copy)
                e.drain().then_inc(taken[b], 1)

            def keep(i, b):
                ph.act_keep(e, i, b)

            ph.staged(e, [
                lambda i, b: times_w.act(e, i, b, FD),
                take,
                lambda i, b: ph.act_square(e, i, b, 2, 1, other[b][:, :, :]),
                lambda i, b: ph.act_root(e, i, b, 2, 1, p.eps[:, 1:2]),
                lambda i, b: ph.act_square(e, i, b, 2, 2, ph.state[b][:, :, :]),
                lambda i, b: ph.act_root(e, i, b, 2, 2, p.eps[:, 0:1]),
                keep,
            ])

        @block.vector
        def _(e):
            def aggregate(i, b):
                ph.wait_gathered(e, i, b)
                ph.shares(e, i, b, share[b], 1, FD)
                e.tensor_tensor(agg[b][:, :, :], ph.rows[b][:, :, 0:FD],
                                share[b][:, :, :].to_broadcast([P, G, FD]), ALU.mult)
                e.drain().then_inc(ph.rows_free[b], 1)
                e.sem_inc(times_w.given[b], 1)

            def add_x(i, b):
                o = other[b][:, :, :]
                e.wait_ge(taken[b], at(i, 1, 1))
                e.scalar_tensor_tensor(o, o, 0.01, o, ALU.mult, ALU.max)
                e.drain()
                e.tensor_tensor(o, o, p.x[:, rows_of(i, b, G), :], ALU.add)
                e.drain()
                ph.centre(e, b, o)

            def affine(i, b):
                o, state, now = other[b][:, :, :], ph.state[b][:, :, :], rows_of(i, b, G)
                ph.scale(e, i, b, 2, 1, o)
                e.tensor_tensor(o, o, bcast(p.param["L2_gnn_gamma"][:, :], 1, G), ALU.mult)
                e.drain()
                e.tensor_tensor(o, o, bcast(p.param["L2_gnn_beta"][:, :], 1, G), ALU.add)
                e.wait_ge(ph.state_free[b], at(i, 1, 1))
                e.tensor_tensor(state, p.x[:, now, :], bcast(p.x_share[:, now], 2, FD), ALU.mult)
                e.drain()
                e.tensor_tensor(o, o, bcast(p.live[:, now], 2, FD), ALU.mult)
                e.drain()
                e.tensor_tensor(state, state, o, ALU.add)
                e.drain()
                ph.centre(e, b, state)

            def finish(i, b):
                ph.scale(e, i, b, 2, 2, ph.state[b][:, :, :])
                e.drain().then_inc(ph.state_kept[b], 1)
                e.wait_ge(ph.state_kept[b], at(i, 2, 2))
                e.sem_inc(ph.state_ready[b], 1)

            ph.staged(e, [
                aggregate, add_x,
                lambda i, b: ph.sum_squares(e, i, b, 2, 1),
                affine,
                lambda i, b: ph.sum_squares(e, i, b, 2, 2),
                finish,
            ])


def node_phase_3(p):
    nc = p.nc
    with nc.reset_on_exit(), ExitStack() as ctx:
        ph = NodePhase(p, 3, ctx)
        agg = ph.sbs("agg", [P, G, P])
        hidden = ph.sbs("hidden", [P, G, FD])
        net = Product(ph, "net", 3)
        steps = [(agg, p.w3_msg), (agg, p.w3_upd1), (hidden, p.w3_upd2)]
        block = ctx.enter_context(nc.Block())

        @block.sync
        def _(e):
            ph.sync(e, p.out)

        @block.gpsimd
        def _(e):
            ph.gpsimd(e)

        @block.tensor
        def _(e):
            ph.staged(e, [lambda i, b, k=k, tile=tile, w=w: net.pe(e, i, b, tile[b], w, k + 1)
                          for k, (tile, w) in enumerate(steps)])

        @block.scalar
        def _(e):
            ph.staged(e, [lambda i, b, k=k, w=w: net.act(e, i, b, w.shape[0], k + 1)
                          for k, (_, w) in enumerate(steps)]
                      + [lambda i, b: ph.act_square(e, i, b, 1, 1, ph.state[b][:, :, :]),
                         lambda i, b: ph.act_root(e, i, b, 1, 1, p.eps[:, 0:1])])

        @block.vector
        def _(e):
            def mean_hidden(i, b):
                ph.wait_gathered(e, i, b)
                e.tensor_tensor(agg[b][:, :, :], ph.rows[b][:, :, :],
                                bcast(p.mean_share[:, rows_of(i, b, G)], 2, P), ALU.mult)
                e.drain().then_inc(net.given[b], 1)
                e.sem_inc(ph.rows_free[b], 1)
                e.tensor_tensor(hidden[b][:, :, :], bcast(p.bias_share[:, rows_of(i, b, G)], 2, FD),
                                bcast(p.msg_bias[:, :], 1, G), ALU.mult)

            def join(i, b):
                e.drain()
                net.wait(e, i, b, 1)
                e.tensor_tensor(agg[b][:, :, FD:], net.h_ps[b][:, :, :], hidden[b][:, :, :], ALU.add)
                e.tensor_copy(agg[b][:, :, 0:FD], p.x[:, rows_of(i, b, G), :])
                e.drain().then_inc(net.given[b], 1)

            def update(i, b):
                h = hidden[b][:, :, :]
                net.wait(e, i, b, 2)
                e.tensor_tensor(h, net.h_ps[b][:, :, :], bcast(p.param["L3_gnn_upd_b1"][:, :], 1, G), ALU.add)
                e.drain()
                e.tensor_scalar(h, h, 0.0, None, ALU.max)
                e.drain().then_inc(net.given[b], 1)
                e.wait_ge(ph.state_free[b], at(i, 1, 1))
                e.tensor_tensor(ph.state[b][:, :, :], p.x[:, rows_of(i, b, G), :],
                                bcast(p.param["L3_gnn_upd_b2"][:, :], 1, G), ALU.add)

            def residual(i, b):
                state = ph.state[b][:, :, :]
                e.drain()
                net.wait(e, i, b, 3)
                e.tensor_tensor(state, net.h_ps[b][:, :, :], state, ALU.add)
                e.drain()
                ph.centre(e, b, state)

            def finish(i, b):
                ph.scale(e, i, b, 1, 1, ph.state[b][:, :, :])
                e.drain().then_inc(ph.state_ready[b], 1)

            ph.staged(e, [mean_hidden, join, update, residual,
                          lambda i, b: ph.sum_squares(e, i, b, 1, 1), finish])


def gnn_program(nc, ins, out, n_nodes):
    with ExitStack() as top:
        p = Program(nc, ins, out, n_nodes, top)
        setup_phase(p)
        search_phase(p)
        spread_phase(p, p.k_table, p.k_edges, FD, "spread_k")
        edge_phase_0(p)
        fix_phase(p, 0)
        node_phase_0(p)
        edge_phase_1(p)
        fix_phase(p, 1)
        node_phase_1(p)
        edge_phase_2(p)
        fix_phase(p, 2)
        node_phase_2(p)
        edge_phase_3(p)
        fix_phase(p, 3)
        node_phase_3(p)


def laid_out(inputs, edges_pp, nodes_pp, find):
    n_nodes, n_edges = inputs["x"].shape[0], inputs["src"].shape[0]
    arrays = {}
    for name, a in inputs.items():
        a = np.ascontiguousarray(a)
        if name == "x":
            full = np.zeros((P * nodes_pp, a.shape[1]), a.dtype)
            full[:n_nodes] = a
        elif name in ("src", "dst") or name.startswith("edge_attr"):
            full = np.full((P * edges_pp, *a.shape[1:]), n_nodes if name == "dst" else 0, a.dtype)
            full[:n_edges] = a
            if name == "dst":
                arrays["dst_table"] = full.reshape(find)
            full = full.reshape(P, edges_pp, *a.shape[1:])
        else:
            full = a.reshape(1) if a.ndim == 0 else a
        arrays[name] = full
    arrays["src"] = arrays["src"].view(np.uint32)
    return arrays


def kernel(**inputs):
    import concourse.bacc as bacc
    from concourse.bass_utils import run_bass_kernel_spmd

    n_nodes, n_edges = inputs["x"].shape[0], inputs["src"].shape[0]
    edges_pp = -(-n_edges // (P * 2 * J)) * 2 * J
    nodes_pp = -(-(n_nodes + 1) // (P * 2 * G)) * 2 * G
    rows = next(r for r in range(int((P * edges_pp) ** 0.5), 0, -1) if P * edges_pp % r == 0)
    arrays = laid_out(inputs, edges_pp, nodes_pp, (rows, P * edges_pp // rows))
    nc = bacc.Bacc("TRN2", target_bir_lowering=False, num_devices=1)
    aps = {name: nc.dram_tensor("in_" + name, a.shape, mybir.dt.from_np(a.dtype), kind="ExternalInput").ap()
           for name, a in arrays.items()}
    out = nc.dram_tensor("out_x", (P * nodes_pp, FD), F32, kind="ExternalOutput").ap()
    gnn_program(nc, aps, out, n_nodes)
    r = run_bass_kernel_spmd(nc, [{"in_" + name: a for name, a in arrays.items()}], core_ids=[0])
    return r.results[0]["out_x"][:n_nodes]
```

```python
from contextlib import ExitStack

import numpy as np

import concourse.bass as bass
from concourse import mybir

F32 = mybir.dt.float32
I32 = mybir.dt.int32
U32 = mybir.dt.uint32
ALU = mybir.AluOpType
ACT = mybir.ActivationFunctionType
AX = mybir.AxisListType

P = 128
J = 28
G = 7
QUAD = 4
FD = 64
HEADS = 8
FAR = -1.0e30
SKIPPED = 1.0e9
BC = ["L0_gnn_Wg", "L0_gnn_ln_g", "L0_gnn_ln_b", "L1_gnn_bn_gamma", "L1_gnn_bn_beta", "L2_gnn_gamma",
      "L2_gnn_beta", "L3_gnn_msg_b2", "L3_gnn_upd_b1", "L3_gnn_upd_b2"]


def at(i, per, k):
    return i * per + k


def hold(e, sem, value, passed):
    e.wait_ge(sem, value)
    e.sem_inc(passed, 1)


def rows_of(i, b, size):
    return bass.ds(i * (2 * size) + b * size, size)


def bcast(ap, axis, n):
    a = ap.unsqueeze(axis)
    shape = list(a.shape)
    shape[axis] = n
    return a.to_broadcast(shape)


class Program:

    def __init__(self, nc, ins, out, n_nodes, ctx):
        self.nc, self.ins, self.out, self.ctx = nc, ins, out, ctx
        self.n_nodes = n_nodes
        self.edges_pp = ins["src"].shape[1]
        self.nodes_pp = ins["x"].shape[0] // P
        self.n_edges = P * self.edges_pp
        self.n_rows = P * self.nodes_pp
        self.chunks = self.edges_pp // J
        self.groups = self.nodes_pp // G
        assert self.chunks % 2 == 0 and self.groups % 2 == 0 and J % QUAD == 0
        self.find_rows, self.find_cols = ins["dst_table"].shape

        def dram(name, shape, dt=F32):
            return nc.dram_tensor(name, shape, dt).ap()

        n, e = self.n_rows, self.n_edges
        self.qv_table = dram("qv_table", [n, 2 * FD])
        self.k_table = dram("k_table", [n, FD])
        self.k_edges = dram("k_edges", [e, FD])
        self.clear_per_group = min(3, self.chunks // self.groups)
        self.clear_first = self.chunks - self.clear_per_group * self.groups
        self.er_table = dram("er_table", [n, 2])
        self.er_edges = dram("er_edges", [e, 2])
        self.end_table = dram("end_table", [n + 1, 1])
        self.x_tables = [dram(f"x_table{k}", [n, FD]) for k in (1, 2, 3)]
        self.find_index = dram("find_index", [P, self.nodes_pp], U32)
        self.start_index = dram("start_index", [P, self.nodes_pp], U32)
        self.shape = [(4, 16), (2, 64), (1, 64), (0, 128)]
        self.width = [h * (d + 2) if h else d for h, d in self.shape]
        self.sums = [dram(f"sums{k}", [e, w]) for k, w in enumerate(self.width)]

        def keep(name, shape, dt=F32):
            return ctx.enter_context(nc.sbuf_tensor(name, shape, dt))

        self.x = keep("x_now", [P, self.nodes_pp, FD])
        self.aux = keep("aux_now", [P, self.nodes_pp, FD])
        self.same = keep("same", [P, self.edges_pp])
        self.node = keep("node_number", [P, self.nodes_pp])
        self.end_index = keep("end_index", [P, self.nodes_pp + 2 * G], U32)
        self.live = keep("live", [P, self.nodes_pp])
        self.real = keep("real", [P, self.nodes_pp])
        self.degree = keep("degree", [P, self.nodes_pp])
        self.x_share = keep("x_share", [P, self.nodes_pp])
        self.mean_share = keep("mean_share", [P, self.nodes_pp])
        self.bias_share = keep("bias_share", [P, self.nodes_pp])
        self.skip_gate = keep("skip_gate", [P, self.nodes_pp])
        self.msg_bias = keep("msg_bias", [P, FD])
        self.eps = keep("eps", [P, 2])
        self.ident = keep("ident", [P, P])
        self.ones = keep("ones", [P, P])
        self.chain = keep("chain", [P, P])
        self.chain_t = keep("chain_t", [P, P])
        self.chain_pen = keep("chain_pen", [P, P])
        self.first = keep("first_dst", [P, 1])
        self.first_index = keep("first_index", [P, 1], U32)
        self.first_end_index = keep("first_end_index", [P, 1], U32)
        self.fix_from = keep("fix_from", [P, 1], U32)
        self.fix_to = keep("fix_to", [P, 1], U32)
        self.carry = keep("carry", [P, 2 * 65])
        self.peak = keep("peak", [P, J + 1, 4])
        self.param = {}
        for name in BC:
            self.param[name] = keep("bc_" + name, [P, int(np.prod(ins[name].shape))])
        self.gate_bias = keep("gate_bias", [P, 1])
        self.slope = keep("prelu_slope", [P, 1])
        self.w_nodes = keep("w_nodes", [FD + 1, 4 * FD])
        self.gate_a = keep("gate_a", [P, FD])
        self.gate_b = keep("gate_b", [P, FD])
        self.w1 = keep("w1", [FD, 2 * FD])
        self.w1_heads = keep("w1_heads", [2 * FD, FD])
        self.attn_l = keep("attn_l", [P, 2, FD])
        self.attn_r = keep("attn_r", [FD, 2])
        self.w2_mk = keep("w2_mk", [P, P])
        self.w2_qr = keep("w2_qr", [P, P])
        self.w2_qe = keep("w2_qe", [P, P])
        self.w2_out = keep("w2_out", [FD, FD])
        self.w3_hidden = keep("w3_hidden", [97, P])
        self.w3_msg = keep("w3_msg", [P, FD])
        self.w3_upd1 = keep("w3_upd1", [P, FD])
        self.w3_upd2 = keep("w3_upd2", [FD, FD])


def clear_chunk(p, e, i, k, per):
    size = J * FD
    flat = p.k_edges.rearrange("(p j) f -> p (j f)", p=P)
    e.dma_start(flat[:, bass.ds(i * (per * size) + k * size, size)], p.zeros[:, :]).then_inc(p.cleared, 16)


def setup_phase(p, sems):
    nc, ins = p.nc, p.ins
    with ExitStack() as ctx:
        dst_i = ctx.enter_context(nc.sbuf_tensor("dst_i", [P, p.edges_pp], I32))
        dst_f = ctx.enter_context(nc.sbuf_tensor("dst_f", [P, p.edges_pp + 1], F32))
        node_i = ctx.enter_context(nc.sbuf_tensor("node_i", [P, p.nodes_pp], I32))
        before = ctx.enter_context(nc.sbuf_tensor("before", [P, P], F32))
        att_cols = ctx.enter_context(nc.sbuf_tensor("att_cols", [FD, 4], F32))
        att_wide = ctx.enter_context(nc.sbuf_tensor("att_wide", [FD, 2, P], F32))
        w1_t = ctx.enter_context(nc.sbuf_tensor("w1_t", [FD, 2, FD], F32))
        tail_wide = ctx.enter_context(nc.sbuf_tensor("tail_wide", [P, P], F32))
        ps_a = ctx.enter_context(nc.psum_tensor("setup_ps_a", [P, 4, P], F32))
        ps_b = ctx.enter_context(nc.psum_tensor("setup_ps_b", [P, 4, P], F32))
        loaded = sems.enter_context(nc.semaphore("setup_loaded"))
        dst_in = sems.enter_context(nc.semaphore("dst_in"))
        cleared = sems.enter_context(nc.semaphore("w2_cleared"))
        zeroed = sems.enter_context(nc.semaphore("zeroed"))
        pool_done = sems.enter_context(nc.semaphore("setup_pool"))
        to_pe = sems.enter_context(nc.semaphore("setup_to_pe"))
        from_pe = sems.enter_context(nc.semaphore("setup_from_pe"))
        block = ctx.enter_context(nc.Block())
        loads = [0]

        def load(e, to, of):
            e.dma_start(to, of).then_inc(loaded, 16)
            loads[0] += 16

        @block.scalar
        def _(e):
            for name in BC:
                flat = ins[name]
                if len(flat.shape) == 2:
                    flat = flat.rearrange("a b -> (a b)")
                load(e, p.param[name][:, :], flat.partition_broadcast(P))
            load(e, p.w2_mk[:, 0:FD], ins["L2_gnn_W_msg"])
            load(e, p.w2_mk[:, FD:P], ins["L2_gnn_W_k"])
            load(e, p.w2_out[:, :], ins["L2_gnn_W_out"])
            load(e, p.w3_upd1[:, :], ins["L3_gnn_upd_w1"])
            load(e, p.w3_upd2[:, :], ins["L3_gnn_upd_w2"])
            e.wait_ge(cleared, 1)
            for half in range(2):
                s = slice(half * FD, (half + 1) * FD)
                load(e, p.w2_qr[s, s], ins["L2_gnn_W_q"][0:FD, :])
                load(e, p.w2_qe[s, s], ins["L2_gnn_W_q"][FD:P, :])
            load(e, p.x[:, :, :], ins["x"].rearrange("(p t) f -> p t f", p=P))
            e.wait_ge(zeroed, 1)
            if p.clear_first:
                with e.Fori(0, p.clear_first) as i:
                    clear_chunk(p, e, i, 0, 1)

        @block.sync
        def _(e):
            e.dma_start(dst_i[:, :], ins["dst"]).then_inc(dst_in, 16)
            with nc.allow_non_contiguous_dma(reason="one element of every table row"):
                load(e, p.heads_i[:, :], ins["dst_table"][:, 0:1].rearrange("(p q) a -> p (q a)", p=P))
            for k, name in enumerate("qvks"):
                load(e, p.w_nodes[0:FD, k * FD:(k + 1) * FD], ins[f"L0_gnn_W{name}"])
                load(e, p.w_nodes[FD:FD + 1, k * FD:(k + 1) * FD], ins[f"L0_gnn_b{name}"].unsqueeze(0))
            load(e, p.gate_bias[:, :], ins["L0_gnn_bg"].partition_broadcast(P))
            load(e, p.slope[:, :], ins["L0_gnn_prelu_a"].partition_broadcast(P))
            load(e, p.w1[:, :], ins["L1_gnn_W"])
            for h in range(2):
                load(e, p.w1_heads[h * FD:(h + 1) * FD, :], ins["L1_gnn_W"][:, h * FD:(h + 1) * FD])
            with nc.allow_non_contiguous_dma(reason="four short columns"):
                for k, name in enumerate("lr"):
                    load(e, att_cols[:, 2 * k:2 * k + 2], ins[f"L1_gnn_attn_{name}"].rearrange("h d -> d h"))
            for k in range(2):
                load(e, p.w3_hidden[0:96, k * FD:(k + 1) * FD], ins["L3_gnn_msg_w1"][k, :, :])
                load(e, p.w3_hidden[96:97, k * FD:(k + 1) * FD], ins["L3_gnn_msg_b1"][k:k + 1, :])
                load(e, p.w3_msg[k * FD:(k + 1) * FD, :], ins["L3_gnn_msg_w2"][k, :, :])

        @block.gpsimd
        def _(e):
            e.memset(p.ident[:, :], 0.0)
            e.memset(p.ones[:, :], 1.0)
            e.memset(before[:, :], 1.0).then_inc(pool_done, 1)
            e.wait_ge(pool_done, 1)
            e.affine_select(out=p.ident[:, :], in_=p.ident[:, :], compare_op=ALU.not_equal, fill=1.0,
                            base=0, pattern=[[-1, P]], channel_multiplier=1)
            e.affine_select(out=before[:, :], in_=before[:, :], compare_op=ALU.is_gt, fill=0.0,
                            base=0, pattern=[[-1, P]], channel_multiplier=1)
            e.iota(node_i[:, :], pattern=[[1, p.nodes_pp]], base=0, channel_multiplier=p.nodes_pp)\
                .then_inc(pool_done, 1)

        @block.vector
        def _(e):
            e.memset(p.zeros[:, :], 0.0)
            e.drain().then_inc(zeroed, 1)
            e.memset(p.w2_qr[:, :], 0.0)
            e.memset(p.w2_qe[:, :], 0.0).then_inc(cleared, 1)
            e.memset(dst_f[:, 0:1], -1.0)
            e.wait_ge(dst_in, 16)
            e.tensor_copy(dst_f[:, 1:], dst_i[:, :])
            e.drain()
            e.tensor_tensor(p.same[:, :], dst_f[:, 1:], dst_f[:, 0:p.edges_pp], ALU.is_equal)
            e.tensor_copy(p.first[:, :], dst_f[:, 1:2])
            e.tensor_copy(p.first_index[:, :], dst_i[:, 0:1])
            e.tensor_scalar(p.first_end_index[:, :], dst_f[:, 1:2], 1.0, None, ALU.add)
            e.wait_ge(pool_done, 2)
            e.tensor_copy(p.node[:, :], node_i[:, :])
            e.tensor_copy(tail_wide[:, :], dst_f[:, p.edges_pp:].to_broadcast([P, P]))
            e.wait_ge(loaded, loads[0])
            e.tensor_copy(att_wide[:, :, :], bcast(att_cols[:, 0:2], 2, P)).then_inc(to_pe, 1)
            wg = p.param["L0_gnn_Wg"]
            e.tensor_tensor(p.gate_a[:, :], wg[:, 0:FD], wg[:, 2 * FD:3 * FD], ALU.add)
            e.tensor_tensor(p.gate_b[:, :], wg[:, FD:2 * FD], wg[:, 2 * FD:3 * FD], ALU.subtract)
            e.tensor_scalar(p.gate_bias[:, :], p.gate_bias[:, :], -1.0, None, ALU.mult)
            e.tensor_scalar(p.w1_heads[:, :], p.w1_heads[:, :], 0.5, None, ALU.mult)
            e.wait_ge(from_pe, 1)
            e.tensor_scalar(p.chain[:, :], ps_a[:, 0, :], p.first[:, 0:1], None, ALU.is_equal)
            e.tensor_copy(w1_t[:, :, :], ps_a[0:FD, 1:3, 0:FD])
            e.drain()
            e.tensor_tensor(p.chain[:, :], p.chain[:, :], before[:, :], ALU.mult)
            e.drain().then_inc(to_pe, 1)
            e.tensor_scalar(p.chain_pen[:, :], p.chain[:, :], -1.0, -FAR, ALU.add, ALU.mult)
            e.wait_ge(from_pe, 2)
            e.tensor_copy(p.chain_t[:, :], ps_a[:, 3, :])
            e.tensor_copy(p.attn_l[:, :, :], ps_b[:, 0:2, 0:FD])
            e.tensor_copy(p.attn_r[:, :], ps_b[0:FD, 2, 0:2])
            e.memset(p.eps[:, 0:1], 1e-5)
            e.memset(p.eps[:, 1:2], 1e-6)
            b2 = p.param["L3_gnn_msg_b2"]
            e.tensor_tensor(p.msg_bias[:, :], b2[:, 0:FD], b2[:, FD:], ALU.add)

        @block.tensor
        def _(e):
            e.wait_ge(pool_done, 2)
            e.wait_ge(to_pe, 1)
            e.matmul(ps_a[:, 0, :], tail_wide[:, :], p.ident[:, :], start=True, stop=True)
            for h in range(2):
                ins_ = e.transpose(ps_a[0:FD, 1 + h, 0:FD], p.w1[:, h * FD:(h + 1) * FD],
                                   p.ident[0:FD, 0:FD])
            ins_.then_inc(from_pe, 1)
            e.wait_ge(to_pe, 2)
            e.transpose(ps_a[:, 3, :], p.chain[:, :], p.ident[:, :])
            for k in range(2):
                e.matmul(ps_b[:, k, 0:FD], att_wide[:, k, :], w1_t[:, k, :], start=True, stop=True)
            for k in range(2):
                ins_ = e.matmul(ps_b[0:FD, 2, k:k + 1], w1_t[:, k, :], att_cols[:, 2 + k:3 + k],
                                start=True, stop=True)
            ins_.then_inc(from_pe, 1)


def search_phase(p, sems):
    nc = p.nc
    Q, W, T = p.find_rows // P, p.find_cols, p.nodes_pp
    rounds = p.groups // 2
    with ExitStack() as ctx:
        sb = lambda n, s, d=F32: ctx.enter_context(nc.sbuf_tensor(n, s, d))
        sem = lambda n: sems.enter_context(nc.semaphore(n))
        heads = sb("heads", [P, Q])
        holder = sb("holder", [P, Q])
        offset = sb("offset", [P, Q])
        count_i = sb("count_i", [P, P], I32)
        number = sb("number", [P, P])
        floor = sb("floor", [P, P])
        reached = sb("reached", [P, Q, P])
        is_before = sb("is_before", [P, Q, P])
        is_holder = sb("is_holder", [P, Q, P])
        at_most = sb("at_most", [P, Q, T])
        compared = sb("compared", [P, G, W])
        row = sb("found_row", [P, T])
        row_u = sb("found_row_u", [P, T], U32)
        start_u = sb("start_u", [P, T], U32)
        count = sb("found_count", [P, T])
        ends = sb("ends", [P, T])
        starts = sb("starts", [P, T])
        start_f = sb("start_f", [P, T])
        picked = [sb(f"picked{b}", [P, G, W], I32) for b in (0, 1)]
        pick_ix = [sb(f"pick_ix{b}", [P, G], U32) for b in (0, 1)]
        end_zero = sb("end_zero", [1, 1])
        fix_f = sb("fix_f", [P, 1])
        fix_lim = sb("fix_lim", [P, 1])
        fix_ok = sb("fix_ok", [P, 1])
        lim_i = sb("lim_i", [P, 1], I32)
        chained = sb("chained", [P, 1])
        x_in = [sb(f"x_in{b}", [P, G, FD + 1]) for b in (0, 1)]
        x_t = [sb(f"x_t{b}", [FD + 1, G, P]) for b in (0, 1)]
        qv_out = [sb(f"qv_out{b}", [P, G, 2 * FD]) for b in (0, 1)]
        k_out = [sb(f"k_out{b}", [P, G, FD]) for b in (0, 1)]
        row_ps = ctx.enter_context(nc.psum_tensor("row_ps", [P, T], F32))
        xt_ps = ctx.enter_context(nc.psum_tensor("xt_ps", [P, 2, QUAD, P], F32))
        proj_ps = ctx.enter_context(nc.psum_tensor("proj_ps", [P, 4, 2, 4 * FD], F32))
        s_count = sem("s_count")
        s_cut = sem("s_cut")
        s_rps = sem("s_rps")
        s_row = sem("s_row")
        s_rowst = sem("s_rowst")
        s_ix = [sem(f"s_ix{b}") for b in (0, 1)]
        s_got = [sem(f"s_got{b}") for b in (0, 1)]
        s_free = [sem(f"s_free{b}") for b in (0, 1)]
        s_end = sem("s_end")
        s_endst = sem("s_endst")
        s_start = sem("s_start")
        s_zero = sem("s_zero")
        s_index = sem("s_index")
        s_indexst = sem("s_indexst")
        s_fix = sem("s_fix")
        s_lim = sem("s_lim")
        s_xin = sem("s_xin")
        s_xps = sem("s_xps")
        s_xt = sem("s_xt")
        s_proj = sem("s_proj")
        s_taken = sem("s_taken")
        s_out = sem("s_out")
        s_outst = [sem(f"s_outst{b}") for b in (0, 1)]
        s_passed = sem("s_passed")
        block = ctx.enter_context(nc.Block())

        @block.sync
        def _(e):
            e.wait_ge(s_row, 1)
            e.dma_start(p.find_index, row_u[:, :]).then_inc(s_rowst, 16)
            e.wait_ge(s_rowst, 16)
            with e.Fori(0, rounds) as i:
                for b in (0, 1):
                    hold(e, s_free[b], at(i, 1, 1), s_passed)
                    e.dma_start(pick_ix[b][:, :], p.find_index[:, rows_of(i, b, G)]).then_inc(s_ix[b], 16)
                    for k in range(p.clear_per_group):
                        clear_chunk(p, e, i, p.clear_first + b * p.clear_per_group + k, 2 * p.clear_per_group)
            with e.Fori(0, 2) as i:
                e.dma_start(p.er_edges.rearrange("(p j) f -> p (j f)", p=P)[:, bass.ds(i * p.edges_pp, p.edges_pp)],
                            p.zeros[:, 0:p.edges_pp]).then_inc(p.cleared, 16)
            e.wait_ge(s_zero, 1)
            e.wait_ge(s_end, 1)
            e.dma_start(p.end_table[0:1, :], end_zero[0:1, :]).then_inc(s_endst, 16)
            e.dma_start(p.end_table[1:, :].rearrange("(p t) a -> p (t a)", p=P), ends[:, :])\
                .then_inc(s_endst, 16)
            e.wait_ge(s_endst, 32)
            e.dma_start(starts[:, :], p.end_table[0:p.n_rows, :].rearrange("(p t) a -> p (t a)", p=P))\
                .then_inc(s_start, 16)
            e.wait_ge(s_index, 1)
            e.dma_start(p.start_index, start_u[:, :]).then_inc(s_indexst, 16)
            e.wait_ge(s_indexst, 16)
            e.wait_ge(p.cleared, 16 * p.chunks + 32)

        @block.gpsimd
        def _(e):
            e.iota(count_i[:, :], pattern=[[1, P]], base=0, channel_multiplier=0).then_inc(s_count, 1)
            e.iota(lim_i[:, :], pattern=[[0, 1]], base=p.edges_pp, channel_multiplier=p.edges_pp)\
                .then_inc(s_lim, 1)
            with e.Fori(0, rounds) as i:
                for b in (0, 1):
                    hold(e, s_ix[b], at(i, 16, 16), s_passed)
                    for t in range(G):
                        e.indirect_dma_start(picked[b][:, t, :], None, p.ins["dst_table"],
                                             bass.IndirectOffsetOnAxis(ap=pick_ix[b][:, t:t + 1], axis=0))\
                            .then_inc(s_got[b], 16)
            e.wait_ge(s_endst, 32)
            e.indirect_dma_start(fix_f[:, :], None, p.end_table,
                                 bass.IndirectOffsetOnAxis(ap=p.first_end_index[:, 0:1], axis=0))\
                .then_inc(s_fix, 16)

        @block.vector
        def _(e):
            e.wait_ge(s_count, 1)
            e.tensor_copy(number[:, :], count_i[:, :])
            for b in (0, 1):
                e.drain().then_inc(s_free[b], 1)
            e.tensor_scalar(floor[:, :], number[:, :], float(T), None, ALU.mult)
            e.tensor_copy(heads[:, :], p.heads_i[:, :])
            e.drain()
            for c in range(Q):
                e.tensor_scalar(reached[:, c, :], floor[:, :], heads[:, c:c + 1], None, ALU.is_le)
            e.drain()
            e.tensor_reduce(holder[:, :], reached[:, :, :], AX.X, ALU.add)
            e.drain()
            e.tensor_scalar(holder[:, :], holder[:, :], -1.0, None, ALU.add)
            e.drain()
            e.scalar_tensor_tensor(offset[:, :], holder[:, :], -float(T), heads[:, :], ALU.mult, ALU.add)
            e.drain()
            for c in range(Q):
                e.tensor_scalar(is_before[:, c, :], number[:, :], holder[:, c:c + 1], None, ALU.is_gt)
                e.tensor_scalar(is_holder[:, c, :], number[:, :], holder[:, c:c + 1], None, ALU.is_equal)
                e.tensor_scalar(at_most[:, c, :], number[:, 0:T], offset[:, c:c + 1], None, ALU.is_ge)
            e.drain().then_inc(s_cut, 1)
            e.memset(end_zero[:, :], 0.0).then_inc(s_zero, 1)
            e.wait_ge(s_rps, 1)
            e.tensor_copy(row[:, :], row_ps[:, :])
            e.drain()
            e.tensor_scalar(row[:, :], row[:, :], -1.0, 0.0, ALU.add, ALU.max)
            e.drain()
            e.tensor_copy(row_u[:, :], row[:, :]).then_inc(s_row, 1)
            with e.Fori(0, rounds) as i:
                for b in (0, 1):
                    now = rows_of(i, b, G)
                    e.wait_ge(s_got[b], at(i, 16 * G, 16 * G))
                    e.tensor_tensor(compared[:, :, 0:W], picked[b][:, :, :],
                                    bcast(p.node[:, now], 2, W), ALU.is_le)
                    e.drain().then_inc(s_free[b], 1)
                    e.tensor_reduce(count[:, now], compared[:, :, 0:W], AX.X, ALU.add)
                    e.drain()
            e.scalar_tensor_tensor(ends[:, :], row[:, :], float(W), count[:, :], ALU.mult, ALU.add)\
                .then_inc(s_end, 1)
            e.tensor_scalar(p.real[:, :], p.node[:, :], float(p.n_nodes), None, ALU.is_lt)
            e.wait_ge(s_start, 16)
            e.tensor_tensor(p.degree[:, :], ends[:, :], starts[:, :], ALU.subtract)
            e.drain()
            e.tensor_tensor(p.degree[:, :], p.degree[:, :], p.real[:, :], ALU.mult)
            e.tensor_scalar(count[:, :], ends[:, :], -1.0, 0.0, ALU.add, ALU.max)
            e.drain()
            e.tensor_scalar(p.live[:, :], p.degree[:, :], 0.0, None, ALU.is_gt)
            e.tensor_copy(p.end_index[:, 0:T], count[:, :])
            e.memset(p.end_index[:, T:], 0)
            e.drain()
            e.tensor_scalar(start_f[:, :], p.live[:, :], -1.0, -SKIPPED, ALU.add, ALU.mult)
            e.tensor_tensor(starts[:, :], starts[:, :], p.live[:, :], ALU.mult)
            e.drain()
            e.tensor_tensor(start_f[:, :], start_f[:, :], starts[:, :], ALU.add)
            e.drain()
            e.tensor_copy(start_u[:, :], start_f[:, :]).then_inc(s_index, 1)
            e.tensor_scalar(p.x_share[:, :], p.live[:, :], -1.0, 2.0, ALU.mult, ALU.add)
            e.tensor_scalar(p.mean_share[:, :], p.degree[:, :], 1e-8, None, ALU.add)
            e.drain()
            e.reciprocal(p.mean_share[:, :], p.mean_share[:, :])
            e.drain()
            e.tensor_tensor(p.bias_share[:, :], p.mean_share[:, :], p.degree[:, :], ALU.mult)
            e.drain()
            e.tensor_tensor(p.mean_share[:, :], p.mean_share[:, :], p.live[:, :], ALU.mult)
            e.wait_ge(s_lim, 1)
            e.tensor_copy(fix_lim[:, :], lim_i[:, :])
            e.tensor_reduce(chained[:, :], p.chain[:, :], AX.X, ALU.max)
            e.wait_ge(s_fix, 16)
            e.drain()
            e.tensor_tensor(fix_ok[:, :], fix_f[:, :], fix_lim[:, :], ALU.is_le)
            e.drain()
            e.tensor_scalar(fix_lim[:, :], fix_f[:, :], -1.0, 0.0, ALU.add, ALU.max)
            e.drain()
            e.tensor_tensor(fix_ok[:, :], fix_ok[:, :], chained[:, :], ALU.mult)
            e.tensor_copy(p.fix_from[:, :], fix_lim[:, :])
            e.drain()
            e.tensor_tensor(fix_lim[:, :], fix_lim[:, :], fix_ok[:, :], ALU.mult)
            e.tensor_scalar(fix_ok[:, :], fix_ok[:, :], -1.0, -SKIPPED, ALU.add, ALU.mult)
            e.drain()
            e.tensor_tensor(fix_f[:, :], fix_lim[:, :], fix_ok[:, :], ALU.add)
            e.drain()
            e.tensor_copy(p.fix_to[:, :], fix_f[:, :])

        @block.tensor
        def _(e):
            e.wait_ge(s_cut, 1)
            for c in range(Q):
                e.matmul(row_ps[:, :], is_before[:, c, :], p.ones[:, 0:T], start=c == 0, stop=False)
                last = e.matmul(row_ps[:, :], is_holder[:, c, :], at_most[:, c, :], start=False,
                                stop=c == Q - 1)
            last.then_inc(s_rps, 1)

            def turn(i, b, n):
                e.wait_ge(s_xin, at(i, 2, n + 1))
                e.wait_ge(s_xt, at(i, 2, n + 1))
                for t in range(G):
                    last = e.transpose(xt_ps[0:FD + 1, t // QUAD, t % QUAD, :], x_in[b][:, t, :],
                                       p.ident[:, :])
                last.then_inc(s_xps, 1)

            def project(i, b):
                e.wait_ge(s_xt, at(i, 2, b + 2))
                for half in (0, 1):
                    e.wait_ge(s_taken, at(i, 4, 2 * b + half + 1))
                    for t in range(half * QUAD, min(G, (half + 1) * QUAD)):
                        last = e.matmul(proj_ps[:, t // 2, t % 2, :], x_t[b][:, t, :], p.w_nodes[:, :],
                                        start=True, stop=True)
                    last.then_inc(s_proj, 1)

            turn(0, 0, 0)
            with e.Fori(0, rounds - 1) as i:
                for b in (0, 1):
                    turn(i, 1 - b, b + 1)
                    project(i, b)
            turn(rounds - 1, 1, 1)
            project(rounds - 1, 0)
            project(rounds - 1, 1)

        @block.scalar
        def _(e):
            def put(i, b, n):
                e.activation(x_in[b][:, :, 0:FD], p.x[:, bass.ds(i * (2 * G) + n * G, G), :], ACT.Copy)\
                    .then_inc(s_xin, 1)
                e.wait_ge(s_xps, at(i, 2, n + 1))
                e.activation(x_t[b][:, 0:QUAD, :], xt_ps[0:FD + 1, 0, :, :], ACT.Copy)
                e.activation(x_t[b][:, QUAD:G, :], xt_ps[0:FD + 1, 1, 0:G - QUAD, :], ACT.Copy)\
                    .then_inc(s_xt, 1)

            def take(i, b):
                for half in (0, 1):
                    e.wait_ge(s_proj, at(i, 4, 2 * b + half + 1))
                    for k in (2 * half, 2 * half + 1):
                        n = min(2, G - 2 * k)
                        ts = slice(2 * k, 2 * k + n)
                        e.activation(qv_out[b][:, ts, :], proj_ps[:, k, 0:n, 0:2 * FD], ACT.Copy)
                        e.activation(k_out[b][:, ts, :], proj_ps[:, k, 0:n, 2 * FD:3 * FD], ACT.Copy)
                        skip = p.aux[:, bass.ds(i * (2 * G) + b * G + 2 * k, n), :]
                        ins_ = e.activation(skip, proj_ps[:, k, 0:n, 3 * FD:], ACT.Copy)
                    ins_.then_inc(s_taken, 1)
                e.drain().then_inc(s_out, 1)
                e.wait_ge(s_out, at(i, 2, b + 1))
                for table, tile in ((p.qv_table, qv_out[b]), (p.k_table, k_out[b])):
                    e.dma_start(table.rearrange("(p t) f -> p t f", p=P)[:, rows_of(i, b, G), :],
                                tile[:, :, :]).then_inc(s_outst[b], 16)

            for b in (0, 1):
                e.activation(x_in[b][:, :, FD:FD + 1], p.ones[:, 0:G].unsqueeze(2), ACT.Copy)
            e.sem_inc(s_taken, 2)
            e.sem_inc(s_xt, 1)
            put(0, 0, 0)
            with e.Fori(0, rounds - 1) as i:
                for b in (0, 1):
                    put(i, 1 - b, b + 1)
                    take(i, b)
                for b in (0, 1):
                    e.wait_ge(s_outst[b], at(i, 32, 32))
            put(rounds - 1, 1, 1)
            take(rounds - 1, 0)
            take(rounds - 1, 1)
            for b in (0, 1):
                e.wait_ge(s_outst[b], 32 * rounds)


def spread_phase(p, table, edges, width, tag):
    nc = p.nc
    with nc.reset_on_exit(), ExitStack() as ctx:
        sb = lambda n, s, d=F32: ctx.enter_context(nc.sbuf_tensor(f"{tag}_{n}", s, d))
        sem = lambda n: ctx.enter_context(nc.semaphore(f"{tag}_{n}"))
        index = [sb(f"ix{b}", [P, G], U32) for b in (0, 1)]
        rows = [sb(f"rows{b}", [P, G, width]) for b in (0, 1)]
        firsts = sb("firsts", [P, width])
        s_in = [sem(f"in{b}") for b in (0, 1)]
        s_sent = [sem(f"sent{b}") for b in (0, 1)]
        s_first = sem("first")
        s_passed = sem("passed")
        s_done = sem("done")
        block = ctx.enter_context(nc.Block())
        nodes = table.rearrange("(p t) f -> p t f", p=P)

        @block.sync
        def _(e):
            def load(b, now):
                e.dma_start(index[b][:, :], p.start_index[:, now]).then_inc(s_in[b], 16)
                e.dma_start(rows[b][:, :, :], nodes[:, now, :]).then_inc(s_in[b], 16)

            for b in (0, 1):
                load(b, slice(b * G, (b + 1) * G))
            with e.Fori(0, p.groups // 2 - 1) as i:
                for b in (0, 1):
                    hold(e, s_sent[b], at(i, 16 * G, 16 * G), s_passed)
                    load(b, bass.ds(i * (2 * G) + (2 + b) * G, G))

        @block.gpsimd
        def _(e):
            e.indirect_dma_start(firsts[:, :], None, table,
                                 bass.IndirectOffsetOnAxis(ap=p.first_index[:, 0:1], axis=0))\
                .then_inc(s_first, 16)
            with e.Fori(0, p.groups // 2) as i:
                for b in (0, 1):
                    hold(e, s_in[b], at(i, 32, 32), s_passed)
                    for t in range(G):
                        e.indirect_dma_start(edges, bass.IndirectOffsetOnAxis(ap=index[b][:, t:t + 1], axis=0),
                                             rows[b][:, t, :], None, bounds_check=p.n_edges - 1,
                                             oob_is_err=False).then_inc(s_sent[b], 16)
            for b in (0, 1):
                e.wait_ge(s_sent[b], 16 * G * (p.groups // 2))
            e.wait_ge(s_first, 16)
            e.dma_start(edges.rearrange("(p j) f -> p j f", p=P)[:, 0, :], firsts[:, :]).then_inc(s_done, 16)
            e.wait_ge(s_done, 16)


class EdgePhase:

    def __init__(self, p, layer, ctx, gather_from, gather_into):
        nc = p.nc
        self.p, self.k = p, layer
        self.heads, self.depth = p.shape[layer]
        self.width = p.width[layer]
        self.rounds = p.chunks // 2
        self.gather_from, self.gather_into = gather_from, gather_into
        tag = f"edge{layer}"
        self.sb = lambda n, s, d=F32: ctx.enter_context(nc.sbuf_tensor(f"{tag}_{n}", s, d))
        self.sem = lambda n: ctx.enter_context(nc.semaphore(f"{tag}_{n}"))
        self.index = [self.sb(f"ix{b}", [P, J], U32) for b in (0, 1)]
        self.sums = [self.sb(f"sums{b}", [P, J + 1, self.width]) for b in (0, 1)]
        self.val = [t[:, 1:, :] for t in self.sums]
        self.index_in = [self.sem(f"index_in{b}") for b in (0, 1)]
        self.attr_in = [self.sem(f"attr_in{b}") for b in (0, 1)]
        self.gathered = [self.sem(f"gathered{b}") for b in (0, 1)]
        self.rows_free = [self.sem(f"rows_free{b}") for b in (0, 1)]
        self.attr_free = [self.sem(f"attr_free{b}") for b in (0, 1)]
        self.ready = [self.sem(f"ready{b}") for b in (0, 1)]
        self.stored = [self.sem(f"stored{b}") for b in (0, 1)]
        self.val_free = [self.sem(f"val_free{b}") for b in (0, 1)]
        self.passed = self.sem("passed")
        self.src_now = self.p.ins["src"]
        h = self.heads
        if h:
            self.pen = self.sb("pen", [P, J])
            self.weight_arg = self.sb("weight_arg", [P, J, h])
            self.decay_arg = self.sb("decay_arg", [P, J, h])
            self.decay = self.sb("decay", [P, J + 1, h])
            self.to_exp, self.from_exp = self.sem("to_exp"), self.sem("from_exp")
        self.same_now = self.sb("same_now", [P, J + 1])

    def sync(self, e, attrs):
        p = self.p
        out = p.sums[self.k].rearrange("(p j) f -> p j f", p=P)

        def load(b, now):
            e.dma_start(self.index[b][:, :], self.src_now[:, now]).then_inc(self.index_in[b], 16)
            for tiles, of in attrs:
                e.dma_start(tiles[b], of[:, now, :]).then_inc(self.attr_in[b], 16)

        def store(b, now):
            e.dma_start(out[:, now, :], self.val[b]).then_inc(self.stored[b], 16)

        for b in (0, 1):
            e.sem_inc(self.val_free[b], 1)
            load(b, slice(b * J, (b + 1) * J))
        with e.Fori(0, self.rounds - 1) as i:
            for b in (0, 1):
                hold(e, self.rows_free[b], at(i, 1, 2), self.passed)
                if attrs:
                    hold(e, self.attr_free[b], at(i, 1, 1), self.passed)
                load(b, bass.ds(i * (2 * J) + (2 + b) * J, J))
                hold(e, self.ready[b], at(i, 1, 1), self.passed)
                store(b, rows_of(i, b, J))
                e.wait_ge(self.stored[b], at(i, 16, 16))
                e.sem_inc(self.val_free[b], 1)
        for b in (0, 1):
            e.wait_ge(self.ready[b], self.rounds)
            store(b, slice((2 * self.rounds - 2 + b) * J, (2 * self.rounds - 1 + b) * J))
        for b in (0, 1):
            e.wait_ge(self.stored[b], 16 * self.rounds)

    def gpsimd(self, e):
        for b in (0, 1):
            e.sem_inc(self.rows_free[b], 1)
        with e.Fori(0, self.rounds) as i:
            for b in (0, 1):
                e.wait_ge(self.index_in[b], at(i, 16, 16))
                hold(e, self.rows_free[b], at(i, 1, 1), self.passed)
                for j in range(J):
                    e.indirect_dma_start(self.gather_into(b, j), None, self.gather_from,
                                         bass.IndirectOffsetOnAxis(ap=self.index[b][:, j:j + 1], axis=0))\
                        .then_inc(self.gathered[b], 16)

    def wait_gathered(self, e, i, b):
        e.wait_ge(self.gathered[b], at(i, 16 * J, 16 * J))

    def wait_attrs(self, e, i, b, n):
        e.wait_ge(self.attr_in[b], at(i, 16 * n, 16 * n))

    def wait_val_free(self, e, i, b):
        e.wait_ge(self.val_free[b], at(i, 1, 1))

    def clear_carries(self, e):
        e.memset(self.sums[0][:, 0, :], 0.0)
        e.memset(self.p.peak[:, 0, :], FAR)
        e.memset(self.same_now[:, 0:1], 1.0)
        if self.heads:
            e.memset(self.decay[:, 0, :], 1.0)
        e.drain()

    def segment_flags(self, e, i, b):
        now = rows_of(i, b, J)
        if self.heads:
            e.tensor_scalar(self.pen[:, :], self.p.same[:, now], -1.0, -FAR, ALU.add, ALU.mult)
        e.tensor_copy(self.same_now[:, 1:], self.p.same[:, now])
        e.drain()

    def running_softmax(self, e, i, b, score):
        h, peak = self.heads, self.p.peak
        for n in range(h):
            e.tensor_tensor_scan(out=peak[:, 1:, n], data0=self.pen[:, :], data1=score[:, :, n],
                                 initial=peak[:, 0, n:n + 1], op0=ALU.add, op1=ALU.max)
        e.drain()
        e.tensor_tensor(self.weight_arg[:, :, :], score[:, :, :], peak[:, 1:, 0:h], ALU.subtract)
        e.tensor_tensor(self.decay_arg[:, :, :], peak[:, 0:J, 0:h], bcast(self.pen[:, :], 2, h), ALU.add)
        e.drain()
        e.tensor_tensor(self.decay_arg[:, :, :], self.decay_arg[:, :, :], peak[:, 1:, 0:h], ALU.subtract)\
            .then_inc(self.to_exp, 1)
        at_row = h * (self.depth + 1)
        e.tensor_copy(self.val[b][:, :, at_row:at_row + h], peak[:, 1:, 0:h])

    def weights(self, b):
        h, d = self.heads, self.depth
        return self.val[b][:, :, 0:h * (d + 1)].rearrange("p j (h d) -> p j h d", h=h)[:, :, :, d]

    def values(self, b):
        h, d = self.heads, self.depth
        return self.val[b][:, :, 0:h * (d + 1)].rearrange("p j (h d) -> p j h d", h=h)[:, :, :, 0:d]

    def exponentials(self, e, i, b):
        e.wait_ge(self.to_exp, at(i, 2, 1 + b))
        e.activation(self.weights(b), self.weight_arg[:, :, :], ACT.Exp)
        e.activation(self.decay[:, 1:, :], self.decay_arg[:, :, :], ACT.Exp).then_inc(self.from_exp, 1)

    def wait_weights(self, e, i, b):
        e.wait_ge(self.from_exp, at(i, 2, 1 + b))

    def scan_sums(self, e, b):
        self.scan(e, b, range(self.heads * (self.depth + 1) if self.heads else self.depth))
        self.pass_on(e, b)

    def scan(self, e, b, features):
        h, d = self.heads, self.depth
        sums = self.sums[b]
        for f in features:
            keep = self.decay[:, :, f // (d + 1)] if h else self.same_now[:, :]
            e.tensor_tensor_scan(out=sums[:, :, f], data0=keep, data1=sums[:, :, f], initial=0.0,
                                 op0=ALU.mult, op1=ALU.add)

    def pass_on(self, e, b):
        h = self.heads
        n = h * (self.depth + 1) if h else self.depth
        e.drain()
        e.tensor_copy(self.sums[1 - b][:, 0, 0:n], self.sums[b][:, J, 0:n])
        if h:
            e.tensor_copy(self.p.peak[:, 0, 0:h], self.p.peak[:, J, 0:h])
        e.drain().then_inc(self.ready[b], 1)

    def keep_tails(self, e):
        e.tensor_copy(self.p.carry[:, 0:min(self.width, 130)], self.sums[0][:, 0, 0:min(self.width, 130)])


def edge_phase_0(p):
    nc = p.nc
    with nc.reset_on_exit(), ExitStack() as ctx:
        tiles = [ctx.enter_context(nc.sbuf_tensor(f"qv{b}", [P, J, 2 * FD], F32)) for b in (0, 1)]
        ph = EdgePhase(p, 0, ctx, p.qv_table, lambda b, j: tiles[b][:, j, :])
        k_all = [ph.sb(f"k{b}", [P, J + 1, FD]) for b in (0, 1)]
        k = [t[:, 1:, :] for t in k_all]
        score = ph.sb("score", [P, J, 4])
        gated = ph.sb("gated", [P, p.nodes_pp, FD])
        block = ctx.enter_context(nc.Block())
        k_edges = p.k_edges.rearrange("(p j) f -> p j f", p=P)

        @block.sync
        def _(e):
            ph.sync(e, [(k, k_edges)])

        @block.gpsimd
        def _(e):
            ph.gpsimd(e)

        @block.vector
        def _(e):
            e.memset(k_all[0][:, 0, :], 0.0)
            e.tensor_tensor(gated[:, :, :], p.aux[:, :, :], bcast(p.gate_a[:, :], 1, p.nodes_pp), ALU.mult)
            e.drain()
            e.tensor_reduce(p.skip_gate[:, :], gated[:, :, :], AX.X, ALU.add)
            ph.clear_carries(e)
            with e.Fori(0, ph.rounds) as i:
                for b in (0, 1):
                    ph.segment_flags(e, i, b)
                    ph.wait_attrs(e, i, b, 1)
                    for f in range(FD):
                        e.tensor_tensor_scan(out=k_all[b][:, :, f], data0=ph.same_now[:, :],
                                             data1=k_all[b][:, :, f], initial=0.0, op0=ALU.mult, op1=ALU.add)
                    e.drain()
                    e.tensor_copy(k_all[1 - b][:, 0, :], k_all[b][:, J, :])
                    e.drain()
                    ph.wait_gathered(e, i, b)
                    e.tensor_tensor(k[b], k[b], tiles[b][:, :, 0:FD], ALU.mult)
                    e.drain()
                    e.tensor_reduce(score[:, :, :], k[b].rearrange("p j (h d) -> p j h d", h=4),
                                    AX.X, ALU.add)
                    e.drain().then_inc(ph.attr_free[b], 1)
                    e.tensor_scalar(score[:, :, :], score[:, :, :], 0.25, None, ALU.mult)
                    e.drain()
                    ph.wait_val_free(e, i, b)
                    ph.running_softmax(e, i, b, score)
                    ph.wait_weights(e, i, b)
                    e.tensor_tensor(ph.values(b), tiles[b][:, :, FD:].rearrange("p j (h d) -> p j h d", h=4),
                                    bcast(ph.weights(b), 3, 16), ALU.mult)
                    e.drain().then_inc(ph.rows_free[b], 1)
                    ph.scan_sums(e, b)
            ph.keep_tails(e)

        @block.scalar
        def _(e):
            with e.Fori(0, ph.rounds) as i:
                for b in (0, 1):
                    ph.exponentials(e, i, b)


def edge_phase_1(p):
    nc = p.nc
    with nc.reset_on_exit(), ExitStack() as ctx:
        g = [ctx.enter_context(nc.sbuf_tensor(f"g{b}", [P, J, FD], F32)) for b in (0, 1)]
        ph = EdgePhase(p, 1, ctx, p.x_tables[0], lambda b, j: g[b][:, j, :])
        bond = [ph.sb(f"bond{b}", [P, J, FD]) for b in (0, 1)]
        product = ph.sb("product", [P, J, 2, FD])
        score = ph.sb("score", [P, J, 2])
        er = ph.sb("er", [P, p.edges_pp, 2])
        er_in = ph.sem("er_in")
        weighed = ph.sem("weighed")
        block = ctx.enter_context(nc.Block())

        @block.sync
        def _(e):
            e.dma_start(er[:, :, :], p.er_edges.rearrange("(p j) f -> p j f", p=P)).then_inc(er_in, 16)
            ph.sync(e, [([bond[0][:, :, :], bond[1][:, :, :]], p.ins["edge_attr_64"])])

        @block.gpsimd
        def _(e):
            ph.gpsimd(e)

        @block.vector
        def _(e):
            ph.clear_carries(e)
            e.wait_ge(er_in, 16)
            for n in range(2):
                e.tensor_tensor_scan(out=er[:, :, n], data0=p.same[:, :], data1=er[:, :, n], initial=0.0,
                                     op0=ALU.mult, op1=ALU.add)
            e.drain()
            with e.Fori(0, ph.rounds) as i:
                for b in (0, 1):
                    ph.segment_flags(e, i, b)
                    ph.wait_attrs(e, i, b, 1)
                    ph.wait_gathered(e, i, b)
                    e.tensor_tensor(g[b][:, :, :], g[b][:, :, :], bond[b][:, :, :], ALU.add)
                    e.drain().then_inc(ph.attr_free[b], 1)
                    e.tensor_tensor(product[:, :, :, :], bcast(g[b][:, :, :], 2, 2),
                                    bcast(p.attn_l[:, :, :], 1, J), ALU.mult)
                    e.drain()
                    e.tensor_reduce(score[:, :, :], product[:, :, :, :], AX.X, ALU.add)
                    e.drain()
                    e.tensor_tensor(score[:, :, :], score[:, :, :], er[:, rows_of(i, b, J), :], ALU.add)
                    e.drain()
                    e.scalar_tensor_tensor(score[:, :, :], score[:, :, :], 0.2, score[:, :, :],
                                           ALU.mult, ALU.max)
                    e.drain()
                    ph.wait_val_free(e, i, b)
                    ph.running_softmax(e, i, b, score)
                    ph.wait_weights(e, i, b)
                    e.tensor_tensor(ph.values(b)[:, :, 0, :], g[b][:, :, :],
                                    bcast(ph.weights(b)[:, :, 0], 2, FD), ALU.mult)
                    e.drain()
                    ph.scan(e, b, range(0, FD + 1))
                    e.wait_ge(weighed, at(i, 2, 1 + b))
                    e.sem_inc(ph.rows_free[b], 1)
                    ph.scan(e, b, range(FD + 1, 2 * FD + 2))
                    ph.pass_on(e, b)
            ph.keep_tails(e)

        @block.scalar
        def _(e):
            with e.Fori(0, ph.rounds) as i:
                for b in (0, 1):
                    ph.exponentials(e, i, b)
                    e.drain()
                    for j in range(J):
                        e.activation(ph.values(b)[:, j, 1, :], g[b][:, j, :], ACT.Copy,
                                     scale=ph.weights(b)[:, j, 1:2])
                    e.drain().then_inc(weighed, 1)


def edge_phase_2(p):
    nc = p.nc
    quads = J // QUAD
    per = 2 * quads
    with nc.reset_on_exit(), ExitStack() as ctx:
        se = [ctx.enter_context(nc.sbuf_tensor(f"se{b}", [P, J, P], F32)) for b in (0, 1)]
        ph = EdgePhase(p, 2, ctx, p.x_tables[1], lambda b, j: se[b][:, j, 0:FD])
        eh = [ph.sb(f"eh{b}", [P, J, FD]) for b in (0, 1)]
        qr = [ph.sb(f"qr{b}", [P, J, FD]) for b in (0, 1)]
        qe = [ph.sb(f"qe{b}", [P, J, FD]) for b in (0, 1)]
        se_t = [ph.sb(f"se_t{u}", [P, QUAD, P]) for u in (0, 1)]
        q_t = [ph.sb(f"q_t{u}", [P, QUAD, P]) for u in (0, 1)]
        q_now = [ph.sb(f"q_now{u}", [P, QUAD, FD]) for u in (0, 1)]
        product = ph.sb("product", [P, J, FD])
        score = ph.sb("score", [P, J, 1])
        ps = lambda n: ctx.enter_context(nc.psum_tensor(n, [P, QUAD, P], F32))
        se_ps = [ps(f"se_ps{u}") for u in (0, 1)]
        q_ps = [ps(f"q_ps{u}") for u in (0, 1)]
        mk_ps = [ps(f"mk_ps{u}") for u in (0, 1)]
        qo_ps = [ps(f"qo_ps{u}") for u in (0, 1)]
        joined = ph.sem("joined")
        turned = ph.sem("turned")
        moved = ph.sem("moved")
        multiplied = ph.sem("multiplied")
        taken = ph.sem("taken")
        scored = ph.sem("scored")
        msg_in = ph.sem("msg_in")
        block = ctx.enter_context(nc.Block())

        @block.sync
        def _(e):
            attr = lambda tiles, name: ([t[:, :, :] for t in tiles], p.ins[name])
            ph.sync(e, [attr(eh, "edge_attr_64"), attr(qr, "edge_attr_64_n2"), attr(qe, "edge_attr_64_n3")])

        @block.gpsimd
        def _(e):
            ph.gpsimd(e)

        @block.tensor
        def _(e):
            e.sem_inc(multiplied, 2)

            def turn(i, b, c):
                n = b * quads + c
                u = n % 2
                e.wait_ge(moved, at(i, per, n + 1))
                for j in range(QUAD):
                    e.transpose(se_ps[u][:, j, :], se[b][:, QUAD * c + j, :], p.ident[:, :])
                for s, tile in enumerate((qr, qe)):
                    for half in range(2):
                        j = QUAD * c + 2 * half
                        last = e.transpose(q_ps[u][:, 2 * s + half, :],
                                           tile[b][:, j:j + 2, :].rearrange("p a f -> p (a f)"), p.ident[:, :])
                last.then_inc(turned, 1)
                if c == quads - 1:
                    e.drain().then_inc(ph.rows_free[b], 1)
                    e.drain().then_inc(ph.attr_free[b], 1)

            def multiply(i, b, c):
                n = b * quads + c
                u = n % 2
                e.wait_ge(moved, at(i, per, n + 3))
                e.wait_ge(taken, at(i, per, n + 1))
                e.wait_ge(scored, at(i, per, n + 1))
                for j in range(QUAD):
                    e.matmul(mk_ps[u][:, j, :], se_t[u][:, j, :], p.w2_mk[:, :], start=True, stop=True)
                for half in range(2):
                    e.matmul(qo_ps[u][:, half, :], q_t[u][:, half, :], p.w2_qr[:, :], start=True, stop=False)
                    last = e.matmul(qo_ps[u][:, half, :], q_t[u][:, 2 + half, :], p.w2_qe[:, :],
                                    start=False, stop=True)
                last.then_inc(multiplied, 1)

            with e.Fori(0, ph.rounds) as i:
                for b in (0, 1):
                    ph.wait_gathered(e, i, b)
                    ph.wait_attrs(e, i, b, 3)
                    e.wait_ge(joined, at(i, 2, b + 1))
                    turn(i, b, 0)
                    for c in range(quads):
                        if c + 1 < quads:
                            turn(i, b, c + 1)
                        multiply(i, b, c)

        @block.scalar
        def _(e):
            e.sem_inc(moved, 2)
            e.sem_inc(taken, 2)

            def move(i, b, c):
                n = b * quads + c
                u = n % 2
                e.wait_ge(turned, at(i, per, n + 1))
                e.wait_ge(multiplied, at(i, per, n + 1))
                e.activation(se_t[u][:, :, :], se_ps[u][:, :, :], ACT.Copy)
                e.activation(q_t[u][:, :, :], q_ps[u][:, :, :], ACT.Copy).then_inc(moved, 1)

            def take(i, b, c):
                n = b * quads + c
                u = n % 2
                e.wait_ge(multiplied, at(i, per, n + 3))
                e.wait_ge(scored, at(i, per, n + 1))
                e.activation(q_now[u][:, :, :], qo_ps[u][:, 0:2, :].rearrange("p a (c f) -> p (a c) f", c=2),
                             ACT.Copy)
                e.activation(ph.val[b][:, QUAD * c:QUAD * (c + 1), 0:FD], mk_ps[u][:, :, 0:FD], ACT.Copy)\
                    .then_inc(taken, 1)

            with e.Fori(0, ph.rounds) as i:
                for b in (0, 1):
                    e.wait_ge(ph.rows_free[b], at(i, 1, 1))
                    ph.wait_attrs(e, i, b, 3)
                    e.activation(se[b][:, :, FD:], eh[b][:, :, :], ACT.Copy).then_inc(joined, 1)
                    ph.wait_val_free(e, i, b)
                    move(i, b, 0)
                    for c in range(quads):
                        if c + 1 < quads:
                            move(i, b, c + 1)
                        take(i, b, c)
                    e.drain().then_inc(msg_in, 1)
                    ph.exponentials(e, i, b)

        @block.vector
        def _(e):
            e.sem_inc(scored, 2)
            ph.clear_carries(e)
            with e.Fori(0, ph.rounds) as i:
                for b in (0, 1):
                    ph.segment_flags(e, i, b)
                    for c in range(quads):
                        n = b * quads + c
                        u = n % 2
                        e.wait_ge(taken, at(i, per, n + 3))
                        e.tensor_tensor(product[:, QUAD * c:QUAD * (c + 1), :], mk_ps[u][:, :, FD:],
                                        q_now[u][:, :, :], ALU.mult).then_inc(scored, 1)
                    e.drain()
                    e.tensor_reduce(score[:, :, :], product[:, :, :], AX.X, ALU.add)
                    e.drain()
                    e.tensor_scalar(score[:, :, :], score[:, :, :], 0.125, None, ALU.mult)
                    e.drain()
                    e.wait_ge(msg_in, at(i, 2, b + 1))
                    ph.running_softmax(e, i, b, score)
                    msg = ph.val[b][:, :, 0:FD]
                    e.scalar_tensor_tensor(msg, msg, 0.01, msg, ALU.mult, ALU.max)
                    e.drain()
                    ph.wait_weights(e, i, b)
                    e.tensor_tensor(msg, msg, ph.weights(b).to_broadcast([P, J, FD]), ALU.mult)
                    e.drain()
                    ph.scan_sums(e, b)
            ph.keep_tails(e)


def edge_phase_3(p):
    nc = p.nc
    quads = J // QUAD
    per = 2 * quads
    K = 97
    with nc.reset_on_exit(), ExitStack() as ctx:
        comb = [ctx.enter_context(nc.sbuf_tensor(f"comb{b}", [P, J, K], F32)) for b in (0, 1)]
        ph = EdgePhase(p, 3, ctx, p.x_tables[2], lambda b, j: comb[b][:, j, 0:FD])
        ea = [ph.sb(f"ea{b}", [P, J, 32]) for b in (0, 1)]
        comb_t = [ph.sb(f"comb_t{u}", [K, QUAD, P]) for u in (0, 1)]
        ps = lambda n: ctx.enter_context(nc.psum_tensor(n, [P, QUAD, P], F32))
        t_ps = [ps(f"t_ps{u}") for u in (0, 1)]
        h_ps = [ps(f"h_ps{u}") for u in (0, 1)]
        joined = ph.sem("joined")
        turned = ph.sem("turned")
        moved = ph.sem("moved")
        multiplied = ph.sem("multiplied")
        taken = ph.sem("taken")
        block = ctx.enter_context(nc.Block())

        @block.sync
        def _(e):
            ph.sync(e, [([t[:, :, :] for t in ea], p.ins["edge_attr_32"])])

        @block.gpsimd
        def _(e):
            ph.gpsimd(e)

        @block.tensor
        def _(e):
            e.sem_inc(multiplied, 2)

            def turn(i, b, c):
                n = b * quads + c
                e.wait_ge(moved, at(i, per, n + 1))
                for j in range(QUAD):
                    last = e.transpose(t_ps[n % 2][0:K, j, :], comb[b][:, QUAD * c + j, :], p.ident[:, :])
                last.then_inc(turned, 1)
                if c == quads - 1:
                    e.drain().then_inc(ph.rows_free[b], 1)

            def multiply(i, b, c):
                n = b * quads + c
                e.wait_ge(moved, at(i, per, n + 3))
                e.wait_ge(taken, at(i, per, n + 1))
                for j in range(QUAD):
                    last = e.matmul(h_ps[n % 2][:, j, :], comb_t[n % 2][:, j, :], p.w3_hidden[:, :],
                                    start=True, stop=True)
                last.then_inc(multiplied, 1)

            with e.Fori(0, ph.rounds) as i:
                for b in (0, 1):
                    ph.wait_gathered(e, i, b)
                    e.wait_ge(joined, at(i, 2, b + 1))
                    turn(i, b, 0)
                    for c in range(quads):
                        if c + 1 < quads:
                            turn(i, b, c + 1)
                        multiply(i, b, c)

        @block.scalar
        def _(e):
            e.sem_inc(moved, 2)
            e.sem_inc(taken, 2)
            for b in (0, 1):
                e.activation(comb[b][:, :, K - 1:], p.ones[:, 0:J].unsqueeze(2), ACT.Copy)

            def move(i, b, c):
                n = b * quads + c
                e.wait_ge(turned, at(i, per, n + 1))
                e.wait_ge(multiplied, at(i, per, n + 1))
                e.activation(comb_t[n % 2][:, :, :], t_ps[n % 2][0:K, :, :], ACT.Copy).then_inc(moved, 1)

            def take(i, b, c):
                n = b * quads + c
                e.wait_ge(multiplied, at(i, per, n + 3))
                e.activation(ph.val[b][:, QUAD * c:QUAD * (c + 1), :], h_ps[n % 2][:, :, :], ACT.Relu)\
                    .then_inc(taken, 1)

            with e.Fori(0, ph.rounds) as i:
                for b in (0, 1):
                    e.wait_ge(ph.rows_free[b], at(i, 1, 1))
                    ph.wait_attrs(e, i, b, 1)
                    e.activation(comb[b][:, :, FD:K - 1], ea[b][:, :, :], ACT.Copy).then_inc(joined, 1)
                    e.drain().then_inc(ph.attr_free[b], 1)
                    ph.wait_val_free(e, i, b)
                    move(i, b, 0)
                    for c in range(quads):
                        if c + 1 < quads:
                            move(i, b, c + 1)
                        take(i, b, c)

        @block.vector
        def _(e):
            ph.clear_carries(e)
            with e.Fori(0, ph.rounds) as i:
                for b in (0, 1):
                    ph.segment_flags(e, i, b)
                    e.wait_ge(taken, at(i, per, (b + 1) * quads + 2))
                    ph.scan_sums(e, b)
            ph.keep_tails(e)


def fix_phase(p, layer):
    nc = p.nc
    h, d = p.shape[layer]
    w = p.width[layer]
    with nc.reset_on_exit(), ExitStack() as ctx:
        sb = lambda n, s, dt=F32: ctx.enter_context(nc.sbuf_tensor(f"fix{layer}_{n}", s, dt))
        sem = lambda n: ctx.enter_context(nc.semaphore(f"fix{layer}_{n}"))
        row = sb("row", [P, w])
        n = max(h, 1)
        wide = sb("wide", [P, n, P])
        turned = sb("turned", [P, n, P])
        top = sb("top", [P, n])
        scale = sb("scale", [P, n])
        ps = ctx.enter_context(nc.psum_tensor(f"fix{layer}_ps", [P, n, P], F32))
        ps_t = ctx.enter_context(nc.psum_tensor(f"fix{layer}_ps_t", [P, n, P], F32))
        ps_s = ctx.enter_context(nc.psum_tensor(f"fix{layer}_ps_s", [P, 130], F32))
        got, ready, done, v2a, a2v = sem("got"), sem("ready"), sem("done"), sem("v2a"), sem("a2v")
        v2p, p2v = sem("v2p"), sem("p2v")
        block = ctx.enter_context(nc.Block())

        @block.gpsimd
        def _(e):
            e.indirect_dma_start(row[:, :], None, p.sums[layer],
                                 bass.IndirectOffsetOnAxis(ap=p.fix_from[:, 0:1], axis=0)).then_inc(got, 16)
            e.wait_ge(ready, 1)
            e.indirect_dma_start(p.sums[layer], bass.IndirectOffsetOnAxis(ap=p.fix_to[:, 0:1], axis=0),
                                 row[:, :], None, bounds_check=p.n_edges - 1, oob_is_err=False)\
                .then_inc(done, 16)
            e.wait_ge(done, 16)

        @block.vector
        def _(e):
            if h:
                e.tensor_copy(wide[:, :, :], bcast(p.peak[:, 0, 0:h], 2, P)).then_inc(v2p, 1)
                e.wait_ge(got, 16)
                e.wait_ge(p2v, 1)
                e.tensor_tensor(wide[:, :, :], ps[:, :, :], bcast(p.chain_pen[:, :], 1, h), ALU.add)
                e.drain()
                e.tensor_reduce(top[:, :], wide[:, :, :], AX.X, ALU.max)
                e.drain()
                e.tensor_tensor(top[:, :], top[:, :], row[:, h * (d + 1):], ALU.max)
                e.drain()
                e.tensor_tensor(wide[:, :, :], wide[:, :, :], bcast(top[:, :], 2, P), ALU.subtract)
                e.tensor_tensor(scale[:, :], row[:, h * (d + 1):], top[:, :], ALU.subtract).then_inc(v2a, 1)
                e.wait_ge(p2v, 2)
                e.tensor_copy(turned[:, :, :], ps_t[:, :, :]).then_inc(v2p, 1)
                e.wait_ge(p2v, 3)
                own = row[:, 0:h * (d + 1)].rearrange("p (h d) -> p h d", h=h)
                e.tensor_tensor(own, own, bcast(scale[:, :], 2, d + 1), ALU.mult)
                e.drain()
                e.tensor_tensor(row[:, 0:h * (d + 1)], row[:, 0:h * (d + 1)], ps_s[:, 0:h * (d + 1)], ALU.add)\
                    .then_inc(ready, 1)
            else:
                e.wait_ge(got, 16)
                e.wait_ge(p2v, 1)
                e.tensor_tensor(row[:, :], row[:, :], ps_s[:, 0:d], ALU.add).then_inc(ready, 1)

        @block.scalar
        def _(e):
            if h:
                e.wait_ge(v2a, 1)
                e.activation(wide[:, :, :], wide[:, :, :], ACT.Exp)
                e.activation(scale[:, :], scale[:, :], ACT.Exp).then_inc(a2v, 1)

        @block.tensor
        def _(e):
            if h:
                e.wait_ge(v2p, 1)
                for k in range(h):
                    last = e.matmul(ps[:, k, :], wide[:, k, :], p.ident[:, :], start=True, stop=True)
                last.then_inc(p2v, 1)
                e.wait_ge(a2v, 1)
                for k in range(h):
                    last = e.transpose(ps_t[:, k, :], wide[:, k, :], p.ident[:, :])
                last.then_inc(p2v, 1)
                e.wait_ge(v2p, 2)
                for k in range(h):
                    s = slice(k * (d + 1), (k + 1) * (d + 1))
                    last = e.matmul(ps_s[:, s], turned[:, k, :], p.carry[:, s], start=True, stop=True)
                last.then_inc(p2v, 1)
            else:
                e.matmul(ps_s[:, 0:d], p.chain_t[:, :], p.carry[:, 0:d], start=True, stop=True)\
                    .then_inc(p2v, 1)


class NodePhase:

    def __init__(self, p, layer, ctx):
        nc = p.nc
        self.p, self.layer = p, layer
        tag = f"node{layer}"
        self.sb = lambda n, s, d=F32: ctx.enter_context(nc.sbuf_tensor(f"{tag}_{n}", s, d))
        self.sem = lambda n: ctx.enter_context(nc.semaphore(f"{tag}_{n}"))
        self.sbs = lambda n, s, d=F32: [self.sb(f"{n}{b}", s, d) for b in (0, 1)]
        self.sems = lambda n: [self.sem(f"{n}{b}") for b in (0, 1)]
        self.ps = lambda n, s: [ctx.enter_context(nc.psum_tensor(f"{tag}_{n}{b}", s, F32)) for b in (0, 1)]
        self.rounds = p.groups // 2
        self.index = self.sbs("ix", [P, G], U32)
        self.rows = self.sbs("rows", [P, G, p.width[layer]])
        self.gathered = self.sems("gathered")
        self.rows_free = self.sems("rows_free")
        self.state = self.sbs("state", [P, G, FD])
        self.state_ready, self.state_out = self.sems("state_ready"), self.sems("state_out")
        self.state_free = self.sems("state_free")
        self.state_kept = self.sems("state_kept")
        self.passed = self.sem("passed")
        self.square = self.sbs("square", [P, G, FD])
        self.mean, self.var = self.sbs("mean", [P, G]), self.sbs("var", [P, G])
        self.to_square, self.from_square = self.sems("to_square"), self.sems("from_square")
        self.to_root, self.from_root = self.sems("to_root"), self.sems("from_root")

    def staged(self, e, stages, ahead=(), place=0):
        def run(i, some):
            for stage in some:
                for b in (0, 1):
                    stage(i, b)

        if not ahead:
            with e.Fori(0, self.rounds) as i:
                run(i, stages)
            return
        run(0, ahead)
        with e.Fori(0, self.rounds - 1) as i:
            run(i, stages[:place])
            run(i + 1, ahead)
            run(i, stages[place:])
        run(self.rounds - 1, stages)

    def sync(self, e, table, extra=(), more_indices=None):
        p = self.p
        first = [slice(b * G, (b + 1) * G) for b in (0, 1)]
        for b in (0, 1):
            e.sem_inc(self.state_free[b], 1)
            if more_indices:
                tiles, of, came, _, _, free = more_indices
                e.sem_inc(free[b], 1)
                e.dma_start(tiles[b][:, :], of[:, first[b]]).then_inc(came[b], 16)
        out = None if table is None else table.rearrange("(p t) f -> p t f", p=P)
        stores = 16 * (1 + len(extra))

        def store(b, now):
            e.dma_start(out[:, now, :], self.state[b][:, :, :]).then_inc(self.state_out[b], 16)
            for tiles, to in extra:
                e.dma_start(to[:, now, :], tiles[b]).then_inc(self.state_out[b], 16)

        if out is None:
            return
        with e.Fori(0, self.rounds - 1) as i:
            after = [bass.ds(i * (2 * G) + (2 + b) * G, G) for b in (0, 1)]
            for b in (0, 1):
                hold(e, self.state_ready[b], at(i, 1, 1), self.passed)
                store(b, rows_of(i, b, G))
            for b in (0, 1):
                e.wait_ge(self.state_out[b], at(i, stores, stores))
                e.sem_inc(self.state_free[b], 1)
            if more_indices:
                tiles, of, came, read, step, free = more_indices
                for b in (0, 1):
                    hold(e, read[b], at(i, step, step), self.passed)
                    e.sem_inc(free[b], 1)
                    e.dma_start(tiles[b][:, :], of[:, after[b]]).then_inc(came[b], 16)
        for b in (0, 1):
            e.wait_ge(self.state_ready[b], self.rounds)
            store(b, slice((2 * self.rounds - 2 + b) * G, (2 * self.rounds - 1 + b) * G))
        for b in (0, 1):
            e.wait_ge(self.state_out[b], stores * self.rounds)

    def gather(self, e, i, b):
        hold(e, self.rows_free[b], at(i, 1, 1), self.passed)
        for t in range(G):
            e.indirect_dma_start(self.rows[b][:, t, :], None, self.p.sums[self.layer],
                                 bass.IndirectOffsetOnAxis(ap=self.index[b][:, t:t + 1], axis=0))\
                .then_inc(self.gathered[b], 16)

    def gpsimd(self, e):
        self.staged(e, [lambda i, b: self.gather(e, i, b)])

    def first_indices(self, e):
        for b in (0, 1):
            e.tensor_copy(self.index[b][:, :], self.p.end_index[:, b * G:(b + 1) * G])
            e.drain().then_inc(self.rows_free[b], 1)

    def wait_gathered(self, e, i, b):
        e.wait_ge(self.gathered[b], at(i, 16 * G, 16 * G))
        e.tensor_copy(self.index[b][:, :], self.p.end_index[:, bass.ds(i * (2 * G) + (2 + b) * G, G)])

    def shares(self, e, i, b, share, heads, depth):
        den = self.rows[b][:, :, 0:heads * (depth + 1)].rearrange("p t (h d) -> p t h d", h=heads)[:, :, :, depth]
        e.reciprocal(share[:, :, :], den)
        e.drain()
        e.tensor_tensor(share[:, :, :], share[:, :, :],
                        bcast(self.p.live[:, rows_of(i, b, G)], 2, heads), ALU.mult)
        e.drain()

    def centre(self, e, b, a):
        centre(e, a, self.mean[b][:, :]).then_inc(self.to_square[b], 1)

    def sum_squares(self, e, i, b, per, n):
        e.wait_ge(self.from_square[b], at(i, per, n))
        e.tensor_reduce(self.var[b][:, :], self.square[b][:, :, :], AX.X, ALU.add).then_inc(self.to_root[b], 1)

    def scale(self, e, i, b, per, n, a):
        e.wait_ge(self.from_root[b], at(i, per, n))
        scale_rows(e, a, self.var[b][:, :])

    def act_square(self, e, i, b, per, n, a):
        e.wait_ge(self.to_square[b], at(i, per, n))
        e.activation(self.square[b][:, :, :], a, ACT.Square).then_inc(self.from_square[b], 1)

    def act_root(self, e, i, b, per, n, eps):
        e.wait_ge(self.to_root[b], at(i, per, n))
        e.activation(self.var[b][:, :], self.var[b][:, :], ACT.Sqrt, bias=eps, scale=1.0 / FD)\
            .then_inc(self.from_root[b], 1)

    def act_keep(self, e, i, b):
        e.wait_ge(self.state_kept[b], at(i, 2, 1))
        e.activation(self.p.x[:, rows_of(i, b, G), :], self.state[b][:, :, :], ACT.Copy)
        e.drain().then_inc(self.state_kept[b], 1)


def centre(e, a, mean):
    e.tensor_reduce(mean, a, AX.X, ALU.add)
    e.drain()
    e.tensor_scalar(mean, mean, 1.0 / FD, None, ALU.mult)
    e.drain()
    e.tensor_tensor(a, a, bcast(mean, 2, FD), ALU.subtract)
    return e.drain()


def scale_rows(e, a, root):
    e.reciprocal(root, root)
    e.drain()
    e.tensor_tensor(a, a, bcast(root, 2, FD), ALU.mult)
    e.drain()


class Product:

    def __init__(self, ph, name, per=1):
        self.ph, self.per = ph, per
        self.t_ps = ph.ps(f"{name}_t_ps", [P, 2, QUAD, P])
        self.h_ps = ph.ps(f"{name}_h_ps", [P, G, FD])
        self.tile_t = ph.sbs(f"{name}_t", [P, G, P])
        self.given, self.turned = ph.sems(f"{name}_given"), ph.sems(f"{name}_turned")
        self.moved, self.done = ph.sems(f"{name}_moved"), ph.sems(f"{name}_done")

    def pe(self, tiles, w, n=1):
        wide, cols = w.shape[0], w.shape[1]

        def turn(e, i, b):
            hold(e, self.given[b], at(i, self.per, n), self.ph.passed)
            for t in range(G):
                last = e.transpose(self.t_ps[b][0:wide, t // QUAD, t % QUAD, :], tiles[b][:, t, :],
                                   self.ph.p.ident[:, :])
            last.then_inc(self.turned[b], 1)

        def multiply(e, i, b):
            e.wait_ge(self.moved[b], at(i, self.per, n))
            for t in range(G):
                last = e.matmul(self.h_ps[b][:, t, 0:cols], self.tile_t[b][0:wide, t, :], w[:, :],
                                start=True, stop=True)
            last.then_inc(self.done[b], 1)

        return [turn, multiply]

    def act(self, e, i, b, wide, n=1):
        e.wait_ge(self.turned[b], at(i, self.per, n))
        e.activation(self.tile_t[b][0:wide, 0:QUAD, :], self.t_ps[b][0:wide, 0, :, :], ACT.Copy)
        e.activation(self.tile_t[b][0:wide, QUAD:G, :], self.t_ps[b][0:wide, 1, 0:G - QUAD, :], ACT.Copy)\
            .then_inc(self.moved[b], 1)

    def wait(self, e, i, b, n=1):
        e.wait_ge(self.done[b], at(i, self.per, n))


def node_phase_0(p):
    nc = p.nc
    with nc.reset_on_exit(), ExitStack() as ctx:
        ph = NodePhase(p, 0, ctx)
        share = ph.sbs("share", [P, G, 4])
        agg = ph.sbs("agg", [P, G, FD])
        diff = ph.sbs("diff", [P, G, FD])
        gate = ph.sbs("gate", [P, G])
        er = ph.sbs("er", [P, G, 2])
        start_ix = ph.sbs("start_ix", [P, G], U32)
        first_er = ph.sb("first_er", [P, 2])
        times_attn = Product(ph, "attn")
        to_exp, from_exp = ph.sems("to_exp"), ph.sems("from_exp")
        start_in, sent, er_ready = ph.sems("start_in"), ph.sems("sent"), ph.sems("er_ready")
        er_free = ph.sems("er_free")
        s_first, s_last = ph.sem("first"), ph.sem("last")
        tables_out = ph.sem("tables_out")
        block = ctx.enter_context(nc.Block())

        @block.sync
        def _(e):
            ph.sync(e, p.x_tables[0],
                    [([er[0][:, :, :], er[1][:, :, :]], p.er_table.rearrange("(p t) f -> p t f", p=P))],
                    (start_ix, p.start_index, start_in, sent, 16 * G, er_free))
            e.sem_inc(tables_out, 1)

        @block.gpsimd
        def _(e):
            for b in (0, 1):
                ph.gather(e, 0, b)
            for b in (0, 1):
                ph.gather(e, 1, b)

            def scatter(i, b):
                e.wait_ge(start_in[b], at(i, 16, 16))
                hold(e, er_ready[b], at(i, 1, 1), ph.passed)
                for t in range(G):
                    e.indirect_dma_start(p.er_edges, bass.IndirectOffsetOnAxis(ap=start_ix[b][:, t:t + 1], axis=0),
                                         er[b][:, t, :], None, bounds_check=p.n_edges - 1,
                                         oob_is_err=False).then_inc(sent[b], 16)

            if ph.rounds > 2:
                with e.Fori(0, ph.rounds - 2) as i:
                    for b in (0, 1):
                        ph.gather(e, i + 2, b)
                    for b in (0, 1):
                        scatter(i, b)
            for k in (2, 1):
                for b in (0, 1):
                    scatter(ph.rounds - k, b)
            e.wait_ge(tables_out, 1)
            e.indirect_dma_start(first_er[:, :], None, p.er_table,
                                 bass.IndirectOffsetOnAxis(ap=p.first_index[:, 0:1], axis=0))\
                .then_inc(s_first, 16)
            for b in (0, 1):
                e.wait_ge(sent[b], 16 * G * ph.rounds)
            e.wait_ge(s_first, 16)
            e.dma_start(p.er_edges.rearrange("(p j) f -> p j f", p=P)[:, 0, :], first_er[:, :])\
                .then_inc(s_last, 16)
            e.wait_ge(s_last, 16)

        @block.tensor
        def _(e):
            ph.staged(e, [lambda i, b, of=of: of(e, i, b) for of in times_attn.pe(ph.state, p.attn_r)])

        @block.scalar
        def _(e):
            def sigmoid(i, b):
                e.wait_ge(to_exp[b], at(i, 1, 1))
                e.activation(gate[b][:, :], gate[b][:, :], ACT.Exp, bias=p.gate_bias[:, 0:1], scale=-1.0)\
                    .then_inc(from_exp[b], 1)

            def take_er(i, b):
                times_attn.act(e, i, b, FD)
                ph.act_keep(e, i, b)
                times_attn.wait(e, i, b)
                e.wait_ge(er_free[b], at(i, 1, 1))
                e.activation(er[b][:, :, :], times_attn.h_ps[b][:, :, 0:2], ACT.Copy)
                e.drain().then_inc(er_ready[b], 1)
                e.drain().then_inc(ph.state_ready[b], 1)

            eps = p.eps[:, 0:1]
            ph.staged(e, [
                sigmoid,
                lambda i, b: ph.act_square(e, i, b, 2, 1, agg[b][:, :, :]),
                lambda i, b: ph.act_root(e, i, b, 2, 1, eps),
                lambda i, b: ph.act_square(e, i, b, 2, 2, ph.state[b][:, :, :]),
                lambda i, b: ph.act_root(e, i, b, 2, 2, eps),
                take_er,
            ])

        @block.vector
        def _(e):
            ph.first_indices(e)
            def aggregate(i, b):
                a, d = agg[b][:, :, :], diff[b][:, :, :]
                ph.wait_gathered(e, i, b)
                ph.shares(e, i, b, share[b], 4, 16)
                rows = ph.rows[b][:, :, 0:68].rearrange("p t (h d) -> p t h d", h=4)[:, :, :, 0:16]
                e.tensor_tensor(a.rearrange("p t (h d) -> p t h d", h=4), rows,
                                bcast(share[b][:, :, :], 3, 16), ALU.mult)
                e.drain().then_inc(ph.rows_free[b], 1)
                e.tensor_tensor(d, a, bcast(p.gate_b[:, :], 1, G), ALU.mult)
                e.drain()
                e.tensor_reduce(gate[b][:, :], d, AX.X, ALU.add)
                e.drain()
                now = rows_of(i, b, G)
                e.tensor_tensor(gate[b][:, :], gate[b][:, :], p.skip_gate[:, now], ALU.add).then_inc(to_exp[b], 1)
                e.tensor_tensor(d, p.aux[:, now, :], a, ALU.subtract)

            def mix(i, b):
                a, d = agg[b][:, :, :], diff[b][:, :, :]
                e.wait_ge(from_exp[b], at(i, 1, 1))
                e.tensor_scalar(gate[b][:, :], gate[b][:, :], 1.0, None, ALU.add)
                e.drain()
                e.reciprocal(gate[b][:, :], gate[b][:, :])
                e.drain()
                e.tensor_tensor(d, d, bcast(gate[b][:, :], 2, FD), ALU.mult)
                e.drain()
                e.tensor_tensor(a, a, d, ALU.add)
                e.drain()
                ph.centre(e, b, a)

            def activate(i, b):
                a, d, state = agg[b][:, :, :], diff[b][:, :, :], ph.state[b][:, :, :]
                ph.scale(e, i, b, 2, 1, a)
                e.tensor_tensor(a, a, bcast(p.param["L0_gnn_ln_g"][:, :], 1, G), ALU.mult)
                e.drain()
                e.tensor_tensor(a, a, bcast(p.param["L0_gnn_ln_b"][:, :], 1, G), ALU.add)
                e.drain()
                e.tensor_scalar(d, a, 0.0, p.slope[:, 0:1], ALU.min, ALU.mult)
                e.drain()
                e.scalar_tensor_tensor(a, a, 0.0, d, ALU.max, ALU.add)
                e.drain()
                e.wait_ge(ph.state_free[b], at(i, 1, 1))
                e.tensor_tensor(state, p.x[:, rows_of(i, b, G), :], a, ALU.add)
                e.drain()
                ph.centre(e, b, state)

            def finish(i, b):
                ph.scale(e, i, b, 2, 2, ph.state[b][:, :, :])
                e.drain().then_inc(times_attn.given[b], 1)
                e.sem_inc(ph.state_kept[b], 1)

            ph.staged(e, [
                aggregate, mix,
                lambda i, b: ph.sum_squares(e, i, b, 2, 1),
                activate,
                lambda i, b: ph.sum_squares(e, i, b, 2, 2),
                finish,
            ])


def node_phase_1(p):
    nc = p.nc
    T = p.nodes_pp
    with nc.reset_on_exit(), ExitStack() as ctx:
        ph = NodePhase(p, 1, ctx)
        share = ph.sbs("share", [P, G, 2])
        agg = ph.sbs("agg", [P, G, P])
        times_w = Product(ph, "w")
        squares = ph.sb("squares", [P, T, FD])
        mean = ph.sb("all_mean", [P, T])
        root = ph.sb("all_root", [P, T])
        part = ph.sb("part", [P, FD])
        bn_mean = ph.sb("bn_mean", [P, FD])
        bn_scale = ph.sb("bn_scale", [P, FD])
        mean_sq = ph.sb("mean_sq", [P, FD])
        sum_ps = ctx.enter_context(nc.psum_tensor("n1_sum_ps", [P, 512], F32))
        kept = ph.sems("kept")
        v2p, p2v, v2a, a2v, done, out = (ph.sem(n) for n in ("v2p", "p2v", "v2a", "a2v", "done", "out"))
        halves = [slice(0, T // 2), slice(T // 2, T)]
        block = ctx.enter_context(nc.Block())

        @block.sync
        def _(e):
            ph.sync(e, None)
            table = p.x_tables[1].rearrange("(p t) f -> p t f", p=P)
            for k, s in enumerate(halves):
                e.wait_ge(done, k + 1)
                e.dma_start(table[:, s, :], p.x[:, s, :]).then_inc(out, 16)
            e.wait_ge(out, 32)

        @block.gpsimd
        def _(e):
            ph.gpsimd(e)

        @block.tensor
        def _(e):
            ph.staged(e, [lambda i, b, of=of: of(e, i, b) for of in times_w.pe(agg, p.w1_heads)])
            for k in range(2):
                e.wait_ge(v2p, k + 1)
                e.matmul(sum_ps[:, k * FD:(k + 1) * FD], p.ones[:, :], part[:, :], start=True, stop=True)\
                    .then_inc(p2v, 1)

        @block.scalar
        def _(e):
            def keep_h(i, b):
                times_w.wait(e, i, b)
                e.activation(p.aux[:, rows_of(i, b, G), :], times_w.h_ps[b][:, :, :], ACT.Copy)
                e.drain().then_inc(kept[b], 1)

            ph.staged(e, [lambda i, b: times_w.act(e, i, b, P), keep_h])
            for k, s in enumerate(halves):
                e.wait_ge(v2a, k + 1)
                e.activation(squares[:, s, :], p.aux[:, s, :], ACT.Square).then_inc(a2v, 1)
            e.wait_ge(v2a, 3)
            e.activation(bn_scale[:, :], bn_scale[:, :], ACT.Sqrt, bias=p.eps[:, 0:1], scale=1.0 / p.n_nodes)\
                .then_inc(a2v, 1)
            for k, s in enumerate(halves):
                e.wait_ge(v2a, k + 4)
                e.activation(squares[:, s, :], p.x[:, s, :], ACT.Square).then_inc(a2v, 1)
            for k, s in enumerate(halves):
                e.wait_ge(v2a, k + 6)
                e.activation(root[:, s], root[:, s], ACT.Sqrt, bias=p.eps[:, 0:1], scale=1.0 / FD)\
                    .then_inc(a2v, 1)

        @block.vector
        def _(e):
            ph.first_indices(e)
            def aggregate(i, b):
                ph.wait_gathered(e, i, b)
                ph.shares(e, i, b, share[b], 2, FD)
                rows = ph.rows[b][:, :, 0:130].rearrange("p t (h d) -> p t h d", h=2)[:, :, :, 0:FD]
                e.tensor_tensor(agg[b][:, :, :].rearrange("p t (h d) -> p t h d", h=2), rows,
                                bcast(share[b][:, :, :], 3, FD), ALU.mult)
                e.drain().then_inc(ph.rows_free[b], 1)
                e.sem_inc(times_w.given[b], 1)

            def taken(i, b):
                e.wait_ge(kept[b], at(i, 1, 1))

            ph.staged(e, [aggregate, taken])
            gamma, beta = p.param["L1_gnn_bn_gamma"], p.param["L1_gnn_bn_beta"]
            by_feature = lambda a: a.rearrange("p t f -> p f t")
            e.tensor_reduce(part[:, :], by_feature(p.aux[:, :, :]), AX.X, ALU.add)
            e.drain().then_inc(v2p, 1)
            e.wait_ge(p2v, 1)
            e.tensor_scalar(bn_mean[:, :], sum_ps[:, 0:FD], 1.0 / p.n_nodes, None, ALU.mult)
            e.drain()
            for s in halves:
                h = p.aux[:, s, :]
                e.tensor_tensor(h, h, bcast(bn_mean[:, :], 1, T // 2), ALU.subtract)
                e.drain().then_inc(v2a, 1)
            e.tensor_tensor(mean_sq[:, :], bn_mean[:, :], bn_mean[:, :], ALU.mult)
            e.wait_ge(a2v, 2)
            e.tensor_reduce(part[:, :], by_feature(squares[:, :, :]), AX.X, ALU.add)
            e.drain().then_inc(v2p, 1)
            e.wait_ge(p2v, 2)
            e.scalar_tensor_tensor(bn_scale[:, :], mean_sq[:, :], -float(p.n_rows - p.n_nodes),
                                   sum_ps[:, FD:2 * FD], ALU.mult, ALU.add)
            e.drain()
            e.tensor_scalar(bn_scale[:, :], bn_scale[:, :], 0.0, None, ALU.max)
            e.drain().then_inc(v2a, 1)
            e.wait_ge(a2v, 3)
            e.reciprocal(bn_scale[:, :], bn_scale[:, :])
            e.drain()
            e.tensor_tensor(bn_scale[:, :], bn_scale[:, :], gamma[:, :], ALU.mult)
            e.drain()
            for s in halves:
                h, x = p.aux[:, s, :], p.x[:, s, :]
                e.tensor_tensor(h, h, bcast(bn_scale[:, :], 1, T // 2), ALU.mult)
                e.drain()
                e.tensor_tensor(h, h, bcast(beta[:, :], 1, T // 2), ALU.add)
                e.drain()
                e.scalar_tensor_tensor(x, h, 0.0, x, ALU.max, ALU.add)
                e.drain()
                centre(e, x, mean[:, s]).then_inc(v2a, 1)
            for k, s in enumerate(halves):
                e.wait_ge(a2v, 4 + k)
                e.tensor_reduce(root[:, s], squares[:, s, :], AX.X, ALU.add)
                e.drain().then_inc(v2a, 1)
            for k, s in enumerate(halves):
                e.wait_ge(a2v, 6 + k)
                scale_rows(e, p.x[:, s, :], root[:, s])
                e.drain().then_inc(done, 1)


def node_phase_2(p):
    nc = p.nc
    with nc.reset_on_exit(), ExitStack() as ctx:
        ph = NodePhase(p, 2, ctx)
        share = ph.sbs("share", [P, G, 1])
        agg = ph.sbs("agg", [P, G, FD])
        other = ph.sbs("other", [P, G, FD])
        times_w = Product(ph, "w")
        taken = ph.sems("taken")
        block = ctx.enter_context(nc.Block())

        @block.sync
        def _(e):
            ph.sync(e, p.x_tables[2])

        @block.gpsimd
        def _(e):
            ph.gpsimd(e)

        @block.tensor
        def _(e):
            ph.staged(e, [lambda i, b, of=of: of(e, i, b) for of in times_w.pe(agg, p.w2_out)])

        @block.scalar
        def _(e):
            def take(i, b):
                times_w.wait(e, i, b)
                e.activation(other[b][:, :, :], times_w.h_ps[b][:, :, :], ACT.Copy)
                e.drain().then_inc(taken[b], 1)

            def keep(i, b):
                ph.act_keep(e, i, b)

            ph.staged(e, [
                take,
                lambda i, b: ph.act_square(e, i, b, 2, 1, other[b][:, :, :]),
                lambda i, b: ph.act_root(e, i, b, 2, 1, p.eps[:, 1:2]),
                lambda i, b: ph.act_square(e, i, b, 2, 2, ph.state[b][:, :, :]),
                lambda i, b: ph.act_root(e, i, b, 2, 2, p.eps[:, 0:1]),
                keep,
            ], ahead=[lambda i, b: times_w.act(e, i, b, FD)], place=3)

        @block.vector
        def _(e):
            ph.first_indices(e)
            def aggregate(i, b):
                ph.wait_gathered(e, i, b)
                ph.shares(e, i, b, share[b], 1, FD)
                e.tensor_tensor(agg[b][:, :, :], ph.rows[b][:, :, 0:FD],
                                share[b][:, :, :].to_broadcast([P, G, FD]), ALU.mult)
                e.drain().then_inc(ph.rows_free[b], 1)
                e.sem_inc(times_w.given[b], 1)

            def add_x(i, b):
                o = other[b][:, :, :]
                e.wait_ge(taken[b], at(i, 1, 1))
                e.scalar_tensor_tensor(o, o, 0.01, o, ALU.mult, ALU.max)
                e.drain()
                e.tensor_tensor(o, o, p.x[:, rows_of(i, b, G), :], ALU.add)
                e.drain()
                ph.centre(e, b, o)

            def affine(i, b):
                o, state, now = other[b][:, :, :], ph.state[b][:, :, :], rows_of(i, b, G)
                ph.scale(e, i, b, 2, 1, o)
                e.tensor_tensor(o, o, bcast(p.param["L2_gnn_gamma"][:, :], 1, G), ALU.mult)
                e.drain()
                e.tensor_tensor(o, o, bcast(p.param["L2_gnn_beta"][:, :], 1, G), ALU.add)
                e.wait_ge(ph.state_free[b], at(i, 1, 1))
                e.tensor_tensor(state, p.x[:, now, :], bcast(p.x_share[:, now], 2, FD), ALU.mult)
                e.drain()
                e.tensor_tensor(o, o, bcast(p.live[:, now], 2, FD), ALU.mult)
                e.drain()
                e.tensor_tensor(state, state, o, ALU.add)
                e.drain()
                ph.centre(e, b, state)

            def finish(i, b):
                ph.scale(e, i, b, 2, 2, ph.state[b][:, :, :])
                e.drain().then_inc(ph.state_kept[b], 1)
                e.wait_ge(ph.state_kept[b], at(i, 2, 2))
                e.sem_inc(ph.state_ready[b], 1)

            ph.staged(e, [
                add_x,
                lambda i, b: ph.sum_squares(e, i, b, 2, 1),
                affine,
                lambda i, b: ph.sum_squares(e, i, b, 2, 2),
                finish,
            ], ahead=[aggregate], place=2)


def node_phase_3(p):
    nc = p.nc
    with nc.reset_on_exit(), ExitStack() as ctx:
        ph = NodePhase(p, 3, ctx)
        agg = ph.sbs("agg", [P, G, P])
        hidden = ph.sbs("hidden", [P, G, FD])
        net = Product(ph, "net", 3)
        steps = [(agg, p.w3_msg), (agg, p.w3_upd1), (hidden, p.w3_upd2)]
        block = ctx.enter_context(nc.Block())

        @block.sync
        def _(e):
            ph.sync(e, p.out)

        @block.gpsimd
        def _(e):
            ph.gpsimd(e)

        @block.tensor
        def _(e):
            ph.staged(e, [lambda i, b, of=of: of(e, i, b)
                          for k, (tile, w) in enumerate(steps) for of in net.pe(tile, w, k + 1)])

        @block.scalar
        def _(e):
            moves = [lambda i, b, k=k, w=w: net.act(e, i, b, w.shape[0], k + 1)
                     for k, (_, w) in enumerate(steps)]
            ph.staged(e, moves[1:] + [lambda i, b: ph.act_square(e, i, b, 1, 1, ph.state[b][:, :, :]),
                                      lambda i, b: ph.act_root(e, i, b, 1, 1, p.eps[:, 0:1])],
                      ahead=moves[:1], place=3)

        @block.vector
        def _(e):
            ph.first_indices(e)
            def mean_hidden(i, b):
                ph.wait_gathered(e, i, b)
                e.tensor_tensor(agg[b][:, :, :], ph.rows[b][:, :, :],
                                bcast(p.mean_share[:, rows_of(i, b, G)], 2, P), ALU.mult)
                e.drain().then_inc(net.given[b], 1)
                e.sem_inc(ph.rows_free[b], 1)
                e.tensor_tensor(hidden[b][:, :, :], bcast(p.bias_share[:, rows_of(i, b, G)], 2, FD),
                                bcast(p.msg_bias[:, :], 1, G), ALU.mult)

            def join(i, b):
                e.drain()
                net.wait(e, i, b, 1)
                e.tensor_tensor(agg[b][:, :, FD:], net.h_ps[b][:, :, :], hidden[b][:, :, :], ALU.add)
                e.tensor_copy(agg[b][:, :, 0:FD], p.x[:, rows_of(i, b, G), :])
                e.drain().then_inc(net.given[b], 1)

            def update(i, b):
                h = hidden[b][:, :, :]
                net.wait(e, i, b, 2)
                e.tensor_tensor(h, net.h_ps[b][:, :, :], bcast(p.param["L3_gnn_upd_b1"][:, :], 1, G), ALU.add)
                e.drain()
                e.tensor_scalar(h, h, 0.0, None, ALU.max)
                e.drain().then_inc(net.given[b], 1)
                e.wait_ge(ph.state_free[b], at(i, 1, 1))
                e.tensor_tensor(ph.state[b][:, :, :], p.x[:, rows_of(i, b, G), :],
                                bcast(p.param["L3_gnn_upd_b2"][:, :], 1, G), ALU.add)

            def residual(i, b):
                state = ph.state[b][:, :, :]
                e.drain()
                net.wait(e, i, b, 3)
                e.tensor_tensor(state, net.h_ps[b][:, :, :], state, ALU.add)
                e.drain()
                ph.centre(e, b, state)

            def finish(i, b):
                ph.scale(e, i, b, 1, 1, ph.state[b][:, :, :])
                e.drain().then_inc(ph.state_ready[b], 1)

            ph.staged(e, [join, update, residual, lambda i, b: ph.sum_squares(e, i, b, 1, 1), finish],
                      ahead=[mean_hidden], place=3)


def gnn_program(nc, ins, out, n_nodes):
    with ExitStack() as top:
        p = Program(nc, ins, out, n_nodes, top)
        with nc.reset_on_exit(), ExitStack() as early:
            p.zeros = early.enter_context(nc.sbuf_tensor("zeros", [P, J * FD], F32))
            p.heads_i = early.enter_context(nc.sbuf_tensor("heads_i", [P, HEADS], I32))
            p.cleared = early.enter_context(nc.semaphore("k_edges_cleared"))
            setup_phase(p, early)
            search_phase(p, early)
        spread_phase(p, p.k_table, p.k_edges, FD, "spread_k")
        edge_phase_0(p)
        fix_phase(p, 0)
        node_phase_0(p)
        edge_phase_1(p)
        fix_phase(p, 1)
        node_phase_1(p)
        edge_phase_2(p)
        fix_phase(p, 2)
        node_phase_2(p)
        edge_phase_3(p)
        fix_phase(p, 3)
        node_phase_3(p)


def laid_out(inputs, edges_pp, nodes_pp, find):
    n_nodes, n_edges = inputs["x"].shape[0], inputs["src"].shape[0]
    arrays = {}
    for name, a in inputs.items():
        a = np.ascontiguousarray(a)
        if name == "x":
            full = np.zeros((P * nodes_pp, a.shape[1]), a.dtype)
            full[:n_nodes] = a
        elif name in ("src", "dst") or name.startswith("edge_attr"):
            full = np.full((P * edges_pp, *a.shape[1:]), n_nodes if name == "dst" else 0, a.dtype)
            full[:n_edges] = a
            if name == "dst":
                arrays["dst_table"] = full.reshape(find)
            full = full.reshape(P, edges_pp, *a.shape[1:])
        else:
            full = a.reshape(1) if a.ndim == 0 else a
        arrays[name] = full
    arrays["src"] = arrays["src"].view(np.uint32)
    return arrays


def kernel(**inputs):
    import concourse.bacc as bacc
    from concourse.bass_utils import run_bass_kernel_spmd

    n_nodes, n_edges = inputs["x"].shape[0], inputs["src"].shape[0]
    edges_pp = -(-n_edges // (P * 2 * J)) * 2 * J
    nodes_pp = -(-(n_nodes + 1) // (P * 2 * G)) * 2 * G
    arrays = laid_out(inputs, edges_pp, nodes_pp, (P * HEADS, edges_pp // HEADS))
    nc = bacc.Bacc("TRN2", target_bir_lowering=False, num_devices=1)
    aps = {name: nc.dram_tensor("in_" + name, a.shape, mybir.dt.from_np(a.dtype), kind="ExternalInput").ap()
           for name, a in arrays.items()}
    out = nc.dram_tensor("out_x", (P * nodes_pp, FD), F32, kind="ExternalOutput").ap()
    gnn_program(nc, aps, out, n_nodes)
    r = run_bass_kernel_spmd(nc, [{"in_" + name: a for name, a in arrays.items()}], core_ids=[0])
    return r.results[0]["out_x"][:n_nodes]
```
